# Optimizing a Trainium2 kernel written in Bass

```python
import numpy as np
import jax
import jax.numpy as jnp

def _softmax(x, axis=-1):
    return jax.nn.softmax(x, axis=axis)

def _gelu(x):
    return jax.nn.gelu(x, approximate=True)

def _silu(x):
    return jax.nn.silu(x)

def _sigmoid(x):
    return jax.nn.sigmoid(x)

def _layernorm(x, axis=-1, eps=1e-05):
    m = jnp.mean(x, axis=axis, keepdims=True)
    v = jnp.var(x, axis=axis, keepdims=True)
    return (x - m) / jnp.sqrt(v + eps)

def _scatter_add(tgt, idx, src, axis=0):
    return tgt.at[idx].add(src)

def _segment_sum(src, seg, n):
    return jax.ops.segment_sum(src, seg, n)
kernel_name = 'mk_decoder_postln_d2_seqx_r8_3daf47'

def setup_inputs(seed: int=0):
    np.random.seed(seed)
    _w = jnp.asarray

    def _rec_inputs():
        import jax
        import jax.numpy as jnp
        _rk = jax.random.key(seed)
        x = 2.818e-05 + 1 * jax.random.normal(jax.random.fold_in(_rk, 1), (8, 128, 128), jnp.float32)
        _lenS = 128 - jax.random.randint(jax.random.fold_in(_rk, 7), (8,), 0, max(1, 128 // 4) + 1, jnp.int32)
        _lenS2 = 128 - jax.random.randint(jax.random.fold_in(_rk, 8), (8,), 0, max(1, 128 // 4) + 1, jnp.int32)
        _ctx_2048P = jax.random.normal(jax.random.fold_in(_rk, 11), (8, 16, 256), jnp.float32)
        _ctx_2048c = jax.random.dirichlet(jax.random.fold_in(_rk, 511), 0.3 * jnp.ones((16,), jnp.float32), (8, 128))
        _ctx_2048t = jnp.einsum('bsk,bkd->bsd', _ctx_2048c, _ctx_2048P)
        _ctx_2048t = _ctx_2048t * jax.lax.rsqrt(jnp.mean(jnp.square(_ctx_2048t)) + 1e-12) * 0.953939
        ctx_2048 = -0.000125008 + 0.999885 * (_ctx_2048t + 0.3 * jax.random.normal(jax.random.fold_in(_rk, 611), (8, 128, 256), jnp.float32))
        _validS = jnp.arange(128)[None, :] < _lenS[:, None]
        _validS2 = jnp.arange(128)[None, :] < _lenS2[:, None]
        _causal = jnp.tril(jnp.ones((128, 128), dtype=bool))
        mask_BxS2_fk1 = jnp.where(jnp.broadcast_to(_validS2[:, :], (8, 128)), 1.0, 0.0).astype(jnp.float32)
        mask_BxS2_ik0 = jnp.where(jnp.broadcast_to(_validS2[:, :], (8, 128)), 0, 1).astype(jnp.int32)
        return (x, ctx_2048, mask_BxS2_fk1, mask_BxS2_ik0)
    x, ctx_2048, mask_BxS2_fk1, mask_BxS2_ik0 = _rec_inputs()

    def _L0_attn_setup():
        import jax, jax.numpy as jnp
        import numpy as np
        import math
        EMBED_DIM = 128
        NUM_HEADS = 16
        HEAD_DIM = EMBED_DIM // NUM_HEADS
        MAX_LEN = 625
        LN_EPS = 1e-05

        def _positional_encoding(max_len, embed_dim):
            pos = np.arange(max_len, dtype=np.float32)[:, None]
            div = np.exp(np.arange(0, embed_dim, 2, dtype=np.float32) * (-math.log(10000.0) / embed_dim))
            pe = np.zeros((max_len, embed_dim), dtype=np.float32)
            pe[:, 0::2] = np.sin(pos * div)
            pe[:, 1::2] = np.cos(pos * div)
            return jnp.asarray(pe)[None]
        key = jax.random.key(seed)
        ks = jax.random.split(key, 12)
        s = 1.0 / math.sqrt(EMBED_DIM)
        D = EMBED_DIM
        return {'x': jax.random.normal(ks[0], (4, 256, D), dtype=jnp.float32), 'wq': jax.random.uniform(ks[1], (D, D), jnp.float32, -s, s), 'bq': jax.random.uniform(ks[2], (D,), jnp.float32, -s, s), 'wk': jax.random.uniform(ks[3], (D, D), jnp.float32, -s, s), 'bk': jax.random.uniform(ks[4], (D,), jnp.float32, -s, s), 'wv': jax.random.uniform(ks[5], (D, D), jnp.float32, -s, s), 'bv': jax.random.uniform(ks[6], (D,), jnp.float32, -s, s), 'wo': jax.random.uniform(ks[7], (D, D), jnp.float32, -s, s), 'bo': jax.random.uniform(ks[8], (D,), jnp.float32, -s, s), 'gamma': jnp.ones((D,), jnp.float32), 'beta': jnp.zeros((D,), jnp.float32), 'pe': _positional_encoding(MAX_LEN, D)}
    _L0_attn_all = _L0_attn_setup()
    _L0_attn_in = {k: v for k, v in _L0_attn_all.items() if k in ('wq', 'bq', 'wk', 'bk', 'wv', 'bv', 'wo', 'bo', 'gamma', 'beta', 'pe')}
    del _L0_attn_all

    def _L0_xattn_setup():
        import jax, jax.numpy as jnp
        import numpy as np
        B, S, T = (32, 64, 64)
        SRC_SIZE, TGT_SIZE, OUT_SIZE, NUM_HEAD = (256, 128, 128, 8)
        HEAD_DIM = OUT_SIZE // NUM_HEAD
        key = jax.random.key(seed)
        ks = jax.random.split(key, 12)
        src = jax.random.normal(ks[0], (B, S, SRC_SIZE), dtype=jnp.float32)
        tgt = jax.random.normal(ks[1], (B, T, TGT_SIZE), dtype=jnp.float32)
        src_mask = (jax.random.uniform(ks[2], (B, S)) > 0.3).astype(jnp.float32)
        src_mask = src_mask.at[:, 0].set(1.0)
        tgt_mask = (jax.random.uniform(ks[3], (B, T)) > 0.3).astype(jnp.float32)
        tgt_mask = tgt_mask.at[:, 0].set(1.0)

        def lin(k, out_f, in_f):
            return jax.random.normal(k, (out_f, in_f), dtype=jnp.float32) / np.sqrt(in_f)
        W_src = lin(ks[4], 2 * OUT_SIZE, SRC_SIZE)
        b_src = jnp.zeros((2 * OUT_SIZE,), jnp.float32)
        W_tgt = lin(ks[5], OUT_SIZE, TGT_SIZE)
        b_tgt = jnp.zeros((OUT_SIZE,), jnp.float32)
        W_out = lin(ks[6], OUT_SIZE, OUT_SIZE + TGT_SIZE)
        b_out = jnp.zeros((OUT_SIZE,), jnp.float32)
        return {'src': src, 'tgt': tgt, 'src_mask': src_mask, 'tgt_mask': tgt_mask, 'W_src': W_src, 'b_src': b_src, 'W_tgt': W_tgt, 'b_tgt': b_tgt, 'W_out': W_out, 'b_out': b_out}
    _L0_xattn_all = _L0_xattn_setup()
    _L0_xattn_in = {k: v for k, v in _L0_xattn_all.items() if k in ('W_src', 'b_src', 'W_tgt', 'b_tgt', 'W_out', 'b_out')}
    del _L0_xattn_all

    def _L0_ffn_setup():
        import jax, jax.numpy as jnp
        import numpy as np
        HIDDEN = 128
        N_ROUTED = 16
        N_SHARED = 2
        TOP_K = 2
        MID_R = HIDDEN // 4
        MID_S = HIDDEN // 2
        key = jax.random.key(seed)
        ks = jax.random.split(key, 8)
        s = 0.02
        return {'x': jax.random.normal(ks[0], (2, 128, HIDDEN), dtype=jnp.float32), 'router_w': jax.random.normal(ks[1], (HIDDEN, N_ROUTED), dtype=jnp.float32) * s, 'wg_r': jax.random.normal(ks[2], (N_ROUTED, HIDDEN, MID_R), dtype=jnp.float32) * s, 'wu_r': jax.random.normal(ks[3], (N_ROUTED, HIDDEN, MID_R), dtype=jnp.float32) * s, 'wd_r': jax.random.normal(ks[4], (N_ROUTED, MID_R, HIDDEN), dtype=jnp.float32) * s, 'wg_s': jax.random.normal(ks[5], (N_SHARED, HIDDEN, MID_S), dtype=jnp.float32) * s, 'wu_s': jax.random.normal(ks[6], (N_SHARED, HIDDEN, MID_S), dtype=jnp.float32) * s, 'wd_s': jax.random.normal(ks[7], (N_SHARED, MID_S, HIDDEN), dtype=jnp.float32) * s}
    _L0_ffn_all = _L0_ffn_setup()
    _L0_ffn_in = {k: v for k, v in _L0_ffn_all.items() if k in ('router_w', 'wg_r', 'wu_r', 'wd_r', 'wg_s', 'wu_s', 'wd_s')}
    del _L0_ffn_all

    def _L1_attn_setup():
        import jax, jax.numpy as jnp
        import numpy as np
        import math
        D_MODEL = 128
        D_STATE = 16
        D_CONV = 4
        EXPAND = 2
        D_INNER = EXPAND * D_MODEL
        D_HALF = D_INNER // 2
        DT_RANK = math.ceil(D_MODEL / 16)
        BATCH = 4
        SEQLEN = 128

        def _dwconv_same(x, K, b):
            k = K.shape[-1]
            y = jax.lax.conv_general_dilated(x, K, window_strides=(1,), padding=[((k - 1) // 2, k // 2)], dimension_numbers=('NCH', 'OIH', 'NCH'), feature_group_count=x.shape[1])
            return y + b[None, :, None]

        def _selective_scan(u, delta, A, Bm, Cm, Dp):
            dA = jnp.exp(jnp.einsum('bdl,dn->lbdn', delta, A))
            dBu = jnp.einsum('bdl,bnl,bdl->lbdn', delta, Bm, u)
            Ct = jnp.transpose(Cm, (2, 0, 1))
            h0 = jnp.zeros(dA.shape[1:], dA.dtype)

            def step(h, inp):
                dA_t, dBu_t, C_t = inp
                h = dA_t * h + dBu_t
                return (h, jnp.einsum('bdn,bn->bd', h, C_t))
            _, ys = jax.lax.scan(step, h0, (dA, dBu, Ct))
            y = jnp.transpose(ys, (1, 2, 0))
            return y + u * Dp[None, :, None]
        key = jax.random.key(seed)
        ks = jax.random.split(key, 10)

        def s(k, shape, scale):
            return jax.random.normal(k, shape, jnp.float32) * scale
        hidden_states = jax.random.normal(ks[0], (BATCH, SEQLEN, D_MODEL), jnp.float32)
        W_in = s(ks[1], (D_MODEL, D_INNER), D_MODEL ** (-0.5))
        W_xproj = s(ks[2], (D_HALF, DT_RANK + 2 * D_STATE), D_HALF ** (-0.5))
        dt_init_std = DT_RANK ** (-0.5)
        W_dt = jax.random.uniform(ks[3], (DT_RANK, D_HALF), jnp.float32, -dt_init_std, dt_init_std)
        dt = jnp.exp(jax.random.uniform(ks[4], (D_HALF,), jnp.float32, math.log(0.001), math.log(0.1)))
        dt = jnp.clip(dt, 0.0001, None)
        b_dt = dt + jnp.log(-jnp.expm1(-dt))
        A_log = jnp.log(jnp.tile(jnp.arange(1, D_STATE + 1, dtype=jnp.float32)[None, :], (D_HALF, 1)))
        D = jnp.ones((D_HALF,), jnp.float32)
        W_out = s(ks[5], (D_INNER, D_MODEL), D_INNER ** (-0.5))
        K_x = s(ks[6], (D_HALF, 1, D_CONV), 0.3)
        b_x = jnp.zeros((D_HALF,), jnp.float32)
        K_z = s(ks[7], (D_HALF, 1, D_CONV), 0.3)
        b_z = jnp.zeros((D_HALF,), jnp.float32)
        return dict(hidden_states=hidden_states, W_in=W_in, W_xproj=W_xproj, W_dt=W_dt, b_dt=b_dt, A_log=A_log, D=D, W_out=W_out, K_x=K_x, b_x=b_x, K_z=K_z, b_z=b_z)
    _L1_attn_all = _L1_attn_setup()
    _L1_attn_in = {k: v for k, v in _L1_attn_all.items() if k in ('W_in', 'W_xproj', 'W_dt', 'b_dt', 'A_log', 'D', 'W_out', 'K_x', 'b_x', 'K_z', 'b_z')}
    del _L1_attn_all

    def _L1_xattn_setup():
        import jax, jax.numpy as jnp
        import numpy as np
        UNITS = 128
        NUM_HEADS = 8

        def _split_heads(x, n):
            B, S, D = x.shape
            return x.reshape(B, S, n, D // n).transpose(0, 2, 1, 3)
        key = jax.random.key(seed)
        k1, k2, k3 = jax.random.split(key, 3)
        B, S = (8, 128)
        memory = jax.random.normal(k1, (B, S, 2 * UNITS), dtype=jnp.float32)
        query = jax.random.normal(k2, (B, S, UNITS), dtype=jnp.float32)
        seq_mask = jax.random.randint(k3, (B, S), 0, 2, dtype=jnp.int32)
        b = jnp.zeros((1,), dtype=jnp.float32)
        return {'memory': memory, 'query': query, 'seq_mask': seq_mask, 'b': b}
    _L1_xattn_all = _L1_xattn_setup()
    _L1_xattn_in = {k: v for k, v in _L1_xattn_all.items() if k in ('b',)}
    del _L1_xattn_all

    def _L1_ffn_setup():
        import jax, jax.numpy as jnp
        import numpy as np
        TOP_K = 2
        key = jax.random.key(seed)
        k0, k1, k2, k3, k4 = jax.random.split(key, 5)
        B, S, H, I, E = (1, 512, 128, 256, 8)
        hidden_states = jax.random.normal(k0, (B, S, H), dtype=jnp.float32)
        wg = jax.random.normal(k1, (E, H), dtype=jnp.float32) * 0.02
        w1 = jax.random.normal(k2, (E, I, H), dtype=jnp.float32) * 0.02
        w3 = jax.random.normal(k3, (E, I, H), dtype=jnp.float32) * 0.02
        w2 = jax.random.normal(k4, (E, H, I), dtype=jnp.float32) * 0.02
        return {'hidden_states': hidden_states, 'wg': wg, 'w1': w1, 'w3': w3, 'w2': w2}
    _L1_ffn_all = _L1_ffn_setup()
    _L1_ffn_in = {k: v for k, v in _L1_ffn_all.items() if k in ('wg', 'w1', 'w3', 'w2')}
    del _L1_ffn_all
    return {'x': x, 'ctx_2048': ctx_2048, 'mask_BxS2_fk1': mask_BxS2_fk1, 'mask_BxS2_ik0': mask_BxS2_ik0, 'L0_attn_wq': _L0_attn_in['wq'], 'L0_attn_bq': _L0_attn_in['bq'], 'L0_attn_wk': _L0_attn_in['wk'], 'L0_attn_bk': _L0_attn_in['bk'], 'L0_attn_wv': _L0_attn_in['wv'], 'L0_attn_bv': _L0_attn_in['bv'], 'L0_attn_wo': _L0_attn_in['wo'], 'L0_attn_bo': _L0_attn_in['bo'], 'L0_attn_gamma': _L0_attn_in['gamma'], 'L0_attn_beta': _L0_attn_in['beta'], 'L0_attn_pe': _L0_attn_in['pe'], 'L0_xattn_W_src': _L0_xattn_in['W_src'], 'L0_xattn_b_src': _L0_xattn_in['b_src'], 'L0_xattn_W_tgt': _L0_xattn_in['W_tgt'], 'L0_xattn_b_tgt': _L0_xattn_in['b_tgt'], 'L0_xattn_W_out': _L0_xattn_in['W_out'], 'L0_xattn_b_out': _L0_xattn_in['b_out'], 'L0_ffn_router_w': _L0_ffn_in['router_w'], 'L0_ffn_wg_r': _L0_ffn_in['wg_r'], 'L0_ffn_wu_r': _L0_ffn_in['wu_r'], 'L0_ffn_wd_r': _L0_ffn_in['wd_r'], 'L0_ffn_wg_s': _L0_ffn_in['wg_s'], 'L0_ffn_wu_s': _L0_ffn_in['wu_s'], 'L0_ffn_wd_s': _L0_ffn_in['wd_s'], 'L1_attn_W_in': _L1_attn_in['W_in'], 'L1_attn_W_xproj': _L1_attn_in['W_xproj'], 'L1_attn_W_dt': _L1_attn_in['W_dt'], 'L1_attn_b_dt': _L1_attn_in['b_dt'], 'L1_attn_A_log': _L1_attn_in['A_log'], 'L1_attn_D': _L1_attn_in['D'], 'L1_attn_W_out': _L1_attn_in['W_out'], 'L1_attn_K_x': _L1_attn_in['K_x'], 'L1_attn_b_x': _L1_attn_in['b_x'], 'L1_attn_K_z': _L1_attn_in['K_z'], 'L1_attn_b_z': _L1_attn_in['b_z'], 'L1_xattn_b': _L1_xattn_in['b'], 'L1_ffn_wg': _L1_ffn_in['wg'], 'L1_ffn_w1': _L1_ffn_in['w1'], 'L1_ffn_w3': _L1_ffn_in['w3'], 'L1_ffn_w2': _L1_ffn_in['w2']}

def reference(x, ctx_2048, mask_BxS2_fk1, mask_BxS2_ik0, L0_attn_wq, L0_attn_bq, L0_attn_wk, L0_attn_bk, L0_attn_wv, L0_attn_bv, L0_attn_wo, L0_attn_bo, L0_attn_gamma, L0_attn_beta, L0_attn_pe, L0_xattn_W_src, L0_xattn_b_src, L0_xattn_W_tgt, L0_xattn_b_tgt, L0_xattn_W_out, L0_xattn_b_out, L0_ffn_router_w, L0_ffn_wg_r, L0_ffn_wu_r, L0_ffn_wd_r, L0_ffn_wg_s, L0_ffn_wu_s, L0_ffn_wd_s, L1_attn_W_in, L1_attn_W_xproj, L1_attn_W_dt, L1_attn_b_dt, L1_attn_A_log, L1_attn_D, L1_attn_W_out, L1_attn_K_x, L1_attn_b_x, L1_attn_K_z, L1_attn_b_z, L1_xattn_b, L1_ffn_wg, L1_ffn_w1, L1_ffn_w3, L1_ffn_w2):
    import jax
    import jax.numpy as jnp

    def _L0_attn_ref(x, wq, bq, wk, bk, wv, bv, wo, bo, gamma, beta, pe):
        import jax, jax.numpy as jnp
        import numpy as np
        import math
        EMBED_DIM = 128
        NUM_HEADS = 16
        HEAD_DIM = EMBED_DIM // NUM_HEADS
        MAX_LEN = 625
        LN_EPS = 1e-05

        def _positional_encoding(max_len, embed_dim):
            pos = np.arange(max_len, dtype=np.float32)[:, None]
            div = np.exp(np.arange(0, embed_dim, 2, dtype=np.float32) * (-math.log(10000.0) / embed_dim))
            pe = np.zeros((max_len, embed_dim), dtype=np.float32)
            pe[:, 0::2] = np.sin(pos * div)
            pe[:, 1::2] = np.cos(pos * div)
            return jnp.asarray(pe)[None]
        B, S, D = x.shape
        H, Hd = (NUM_HEADS, HEAD_DIM)
        x = x + pe[:, :S, :]
        q = (x @ wq + bq).reshape(B, S, H, Hd).transpose(0, 2, 1, 3)
        k = (x @ wk + bk).reshape(B, S, H, Hd).transpose(0, 2, 1, 3)
        v = (x @ wv + bv).reshape(B, S, H, Hd).transpose(0, 2, 1, 3)
        scores = jnp.einsum('bhqd,bhkd->bhqk', q, k) / math.sqrt(Hd)
        attn = jax.nn.softmax(scores, axis=-1)
        out = jnp.einsum('bhqk,bhkd->bhqd', attn, v)
        out = out.transpose(0, 2, 1, 3).reshape(B, S, D)
        out = out @ wo + bo
        h = out + x
        mu = jnp.mean(h, axis=-1, keepdims=True)
        var = jnp.var(h, axis=-1, keepdims=True)
        return (h - mu) * jax.lax.rsqrt(var + LN_EPS) * gamma + beta

    def _L0_xattn_ref(src, tgt, src_mask, tgt_mask, W_src, b_src, W_tgt, b_tgt, W_out, b_out):
        import jax, jax.numpy as jnp
        import numpy as np
        B, S, T = (32, 64, 64)
        SRC_SIZE, TGT_SIZE, OUT_SIZE, NUM_HEAD = (256, 128, 128, 8)
        HEAD_DIM = OUT_SIZE // NUM_HEAD
        b, s, _ = src.shape
        t = tgt.shape[1]
        src_trans = jnp.einsum('bsf,of->bso', src, W_src) + b_src
        tgt_trans = jnp.einsum('btf,of->bto', tgt, W_tgt) + b_tgt
        src_trans = src_trans * src_mask[:, :, None]
        tgt_trans = tgt_trans * tgt_mask[:, :, None]
        src_key, src_val = jnp.split(src_trans, 2, axis=2)
        k = src_key.reshape(b, s, NUM_HEAD, HEAD_DIM)
        v = src_val.reshape(b, s, NUM_HEAD, HEAD_DIM)
        q = tgt_trans.reshape(b, t, NUM_HEAD, HEAD_DIM)
        scores = jnp.einsum('bthd,bshd->bhts', q, k) / np.sqrt(HEAD_DIM)
        scores = jnp.where(src_mask[:, None, None, :] == 0, -jnp.inf, scores)
        attn = jax.nn.softmax(scores, axis=-1)
        tgt_update = jnp.einsum('bhts,bshd->bthd', attn, v).reshape(b, t, OUT_SIZE)
        cat_tgt = jnp.concatenate([tgt, tgt_update], axis=2)
        return jnp.einsum('btf,of->bto', cat_tgt, W_out) + b_out

    def _L0_ffn_ref(x, router_w, wg_r, wu_r, wd_r, wg_s, wu_s, wd_s):
        import jax, jax.numpy as jnp
        import numpy as np
        HIDDEN = 128
        N_ROUTED = 16
        N_SHARED = 2
        TOP_K = 2
        MID_R = HIDDEN // 4
        MID_S = HIDDEN // 2
        orig_shape = x.shape
        flat = x.reshape(-1, orig_shape[-1])
        gs = jnp.einsum('td,ndm->tnm', flat, wg_s)
        us = jnp.einsum('td,ndm->tnm', flat, wu_s)
        out = jnp.einsum('tnm,nmd->td', jax.nn.silu(gs) * us, wd_s)
        logits = (flat @ router_w).astype(jnp.float32)
        probs = jax.nn.softmax(logits, axis=-1)
        weights, indices = jax.lax.top_k(probs, TOP_K)
        weights = weights / (weights.sum(axis=-1, keepdims=True) + 1e-09)
        weights = weights.astype(x.dtype)
        comb = jnp.sum(jax.nn.one_hot(indices, N_ROUTED, dtype=x.dtype) * weights[..., None], axis=1)
        g = jnp.einsum('td,edm->tem', flat, wg_r)
        u = jnp.einsum('td,edm->tem', flat, wu_r)
        h = jax.nn.silu(g) * u
        h = h * comb[:, :, None]
        out = out + jnp.einsum('tem,emd->td', h, wd_r)
        return out.reshape(orig_shape)

    def _L1_attn_ref(hidden_states, W_in, W_xproj, W_dt, b_dt, A_log, D, W_out, K_x, b_x, K_z, b_z):
        import jax, jax.numpy as jnp
        import numpy as np
        import math
        D_MODEL = 128
        D_STATE = 16
        D_CONV = 4
        EXPAND = 2
        D_INNER = EXPAND * D_MODEL
        D_HALF = D_INNER // 2
        DT_RANK = math.ceil(D_MODEL / 16)
        BATCH = 4
        SEQLEN = 128

        def _dwconv_same(x, K, b):
            k = K.shape[-1]
            y = jax.lax.conv_general_dilated(x, K, window_strides=(1,), padding=[((k - 1) // 2, k // 2)], dimension_numbers=('NCH', 'OIH', 'NCH'), feature_group_count=x.shape[1])
            return y + b[None, :, None]

        def _selective_scan(u, delta, A, Bm, Cm, Dp):
            dA = jnp.exp(jnp.einsum('bdl,dn->lbdn', delta, A))
            dBu = jnp.einsum('bdl,bnl,bdl->lbdn', delta, Bm, u)
            Ct = jnp.transpose(Cm, (2, 0, 1))
            h0 = jnp.zeros(dA.shape[1:], dA.dtype)

            def step(h, inp):
                dA_t, dBu_t, C_t = inp
                h = dA_t * h + dBu_t
                return (h, jnp.einsum('bdn,bn->bd', h, C_t))
            _, ys = jax.lax.scan(step, h0, (dA, dBu, Ct))
            y = jnp.transpose(ys, (1, 2, 0))
            return y + u * Dp[None, :, None]
        xz = jnp.transpose(hidden_states @ W_in, (0, 2, 1))
        x, z = jnp.split(xz, 2, axis=1)
        A = -jnp.exp(A_log)
        x = jax.nn.gelu(_dwconv_same(x, K_x, b_x), approximate=False)
        z = jax.nn.gelu(_dwconv_same(z, K_z, b_z), approximate=False)
        x_dbl = jnp.einsum('bdl,de->ble', x, W_xproj)
        dt, Bm, Cm = jnp.split(x_dbl, [DT_RANK, DT_RANK + D_STATE], axis=-1)
        dt = jnp.transpose(dt @ W_dt, (0, 2, 1))
        Bm = jnp.transpose(Bm, (0, 2, 1))
        Cm = jnp.transpose(Cm, (0, 2, 1))
        delta = jax.nn.softplus(dt + b_dt[None, :, None])
        y = _selective_scan(x, delta, A, Bm, Cm, D)
        y = jnp.transpose(jnp.concatenate([y, z], axis=1), (0, 2, 1))
        return y @ W_out

    def _L1_xattn_ref(memory, query, seq_mask, b):
        import jax, jax.numpy as jnp
        import numpy as np
        UNITS = 128
        NUM_HEADS = 8

        def _split_heads(x, n):
            B, S, D = x.shape
            return x.reshape(B, S, n, D // n).transpose(0, 2, 1, 3)
        H = NUM_HEADS
        depth = UNITS // H
        Q = _split_heads(query, H) * depth ** (-0.5)
        k_mem, v_mem = jnp.split(memory, 2, axis=2)
        K = _split_heads(k_mem, H)
        V = _split_heads(v_mem, H)
        logits = jnp.einsum('bhqd,bhkd->bhqk', Q, K) + b[0]
        mask = seq_mask.astype(jnp.float32)[:, None, None, :]
        logits = logits + -1e+30 * (1.0 - mask)
        weights = jax.nn.softmax(logits, axis=-1)
        out = jnp.einsum('bhqk,bhkd->bhqd', weights, V)
        B, _, S, _ = out.shape
        return out.transpose(0, 2, 1, 3).reshape(B, S, UNITS)

    def _L1_ffn_ref(hidden_states, wg, w1, w3, w2):
        import jax, jax.numpy as jnp
        import numpy as np
        TOP_K = 2
        orig_shape = hidden_states.shape
        H = orig_shape[-1]
        E = wg.shape[0]
        x = hidden_states.reshape(-1, H)
        router_logits = x @ wg.T
        probs = jax.nn.softmax(router_logits, axis=-1)
        topk_w, topk_idx = jax.lax.top_k(probs, TOP_K)
        topk_w = topk_w / jnp.sum(topk_w, axis=-1, keepdims=True)
        expert_w = jnp.sum(jax.nn.one_hot(topk_idx, E, dtype=x.dtype) * topk_w[..., None], axis=1)
        h1 = jnp.einsum('th,eih->tei', x, w1)
        h3 = jnp.einsum('th,eih->tei', x, w3)
        y = jnp.einsum('tei,ehi->teh', jax.nn.silu(h1) * h3, w2)
        out = jnp.einsum('te,teh->th', expert_w, y)
        return out.reshape(orig_shape)
    x = _layernorm(x + _L0_attn_ref(x, L0_attn_wq, L0_attn_bq, L0_attn_wk, L0_attn_bk, L0_attn_wv, L0_attn_bv, L0_attn_wo, L0_attn_bo, L0_attn_gamma, L0_attn_beta, L0_attn_pe), axis=-1)
    x = _layernorm(x + _L0_xattn_ref(ctx_2048, x, mask_BxS2_fk1, mask_BxS2_fk1, L0_xattn_W_src, L0_xattn_b_src, L0_xattn_W_tgt, L0_xattn_b_tgt, L0_xattn_W_out, L0_xattn_b_out), axis=-1)
    x = _layernorm(x + _L0_ffn_ref(x, L0_ffn_router_w, L0_ffn_wg_r, L0_ffn_wu_r, L0_ffn_wd_r, L0_ffn_wg_s, L0_ffn_wu_s, L0_ffn_wd_s), axis=-1)
    x = _layernorm(x + _L1_attn_ref(x, L1_attn_W_in, L1_attn_W_xproj, L1_attn_W_dt, L1_attn_b_dt, L1_attn_A_log, L1_attn_D, L1_attn_W_out, L1_attn_K_x, L1_attn_b_x, L1_attn_K_z, L1_attn_b_z), axis=-1)
    x = _layernorm(x + _L1_xattn_ref(ctx_2048, x, mask_BxS2_ik0, L1_xattn_b), axis=-1)
    x = _layernorm(x + _L1_ffn_ref(x, L1_ffn_wg, L1_ffn_w1, L1_ffn_w3, L1_ffn_w2), axis=-1)
    return x

_drawn_inputs = setup_inputs


def setup_inputs(seed=0):
    import zlib

    import numpy as np

    out = dict(_drawn_inputs(seed))
    spreads = {'L0_attn_gamma': (1.0, 0.2),
     'L0_attn_beta': (0.0, 0.1),
     'L0_xattn_b_src': (0.0, 0.1),
     'L0_xattn_b_tgt': (0.0, 0.743),
     'L0_xattn_b_out': (0.0, 0.1),
     'L1_attn_D': (1.0, 0.2),
     'L1_attn_b_x': (0.0, 0.1),
     'L1_attn_b_z': (0.0, 0.268)}
    factors = {'L0_attn_wq': 6.289,
     'L0_attn_bq': 8.0,
     'L0_attn_wk': 6.152,
     'L0_attn_bk': 8.0,
     'L0_attn_bv': 4.364,
     'L0_attn_bo': 2.739,
     'L0_ffn_router_w': 8.0,
     'L0_ffn_wg_r': 8.0,
     'L0_ffn_wu_r': 8.0,
     'L0_ffn_wd_r': 8.0,
     'L0_ffn_wg_s': 8.0,
     'L0_ffn_wu_s': 8.0,
     'L0_ffn_wd_s': 8.0,
     'L1_attn_W_xproj': 3.204,
     'L1_attn_W_dt': 8.0,
     'L1_attn_b_dt': 6.874,
     'L1_attn_A_log': 7.352,
     'L1_ffn_wg': 8.0,
     'L1_ffn_w1': 8.0,
     'L1_ffn_w3': 8.0,
     'L1_ffn_w2': 8.0}
    for name, (base, spread) in spreads.items():
        noise = np.random.default_rng([zlib.crc32(name.encode()), seed]).standard_normal(out[name].shape)
        drawn = base * np.exp(spread * noise) if base else spread * noise
        out[name] = jnp.asarray(drawn.astype(out[name].dtype))
    for name, factor in factors.items():
        out[name] = (out[name] * factor).astype(out[name].dtype)
    return out
```

```python
from contextlib import ExitStack

import numpy as np

import concourse.bass as bass
from concourse import mybir

STAGE = 6

B, S, D = 8, 128, 128
NG = 2
G = B // NG
T = G * S
NQ = 4
A_HEADS, X_HEADS = 16, 8
A_E, F_E = 16, 8
F_I = 256
A_BLOCKS = 5
NSTATE, RANK = 16, 8
LN_EPS = 1e-5
MASKED = 2.0 ** 100

PACKS = {
    "first": [("ident", 128), ("head4", 4), ("head2", 4), ("quad_row", 4), ("iota", 16), ("sel32", 32),
              ("pe", 128), ("wq", 128), ("wk", 128), ("bq", 1), ("bk", 1), ("wv", 128), ("wo", 128)],
    "cross": [("w_src", 512), ("w_tgt", 128), ("w_out", 256), ("b_srck", 1), ("b_tgt", 1), ("b1", 1)],
    "moe0": [("router0", A_E), ("wg0", 128 * A_BLOCKS), ("wu0", 128 * A_BLOCKS), ("wd0", 128 * A_BLOCKS)],
    "mamba": [("w_in", 256), ("w_dtlow", RANK), ("w_bc", 96), ("w_dt", 128), ("w_mo", 256), ("b_dt", 1),
              ("b_x", 1), ("b_z", 1), ("d_skip", 1), ("k_x", 4), ("k_z", 4), ("a_log", NSTATE)],
    "moe1": [("router1", F_E), ("w1", F_E * F_I), ("w3", F_E * F_I), ("w2", F_E * F_I)],
    "masks": [("fk_tok", B)],
}
ROWS = [("bv", D), ("bo", D), ("gamma", D), ("beta", D), ("b_srcv", D), ("b_out", D), ("fk", B * S)]


def columns(pack):
    at, out = 0, {}
    for name, width in pack:
        out[name] = (at, width)
        at += width
    return out, at


def decoder(nc, packed, rows, ik_tok, ik_row, x, ctx_t, v_ctx, out):
    fp32, bf16, u32, i32 = mybir.dt.float32, mybir.dt.bfloat16, mybir.dt.uint32, mybir.dt.int32
    ALU = mybir.AluOpType
    ACT = mybir.ActivationFunctionType
    AX = mybir.AxisListType.X
    groups = range(NG)

    with ExitStack() as stack:
        def sb(name, shape, dt=fp32):
            return stack.enter_context(nc.sbuf_tensor(name, shape, dt))

        def sem(name):
            return stack.enter_context(nc.semaphore(name))

        pack_sb, W = {}, {}
        for pname, pack in PACKS.items():
            where, width = columns(pack)
            pack_sb[pname] = sb("pack_" + pname, [128, width])
            for name, (at, w) in where.items():
                W[name] = pack_sb[pname][:, at:at + w]
        where, rows_width = columns(ROWS)
        rows_sb = sb("rows_sb", [128, rows_width])
        R = {name: rows_sb[:, at:at + w] for name, (at, w) in where.items()}
        ident = W["ident"]
        ik_tok_sb = sb("ik_tok_sb", [128, B], i32)
        ones = sb("ones", [128, 128])
        ones_row_b = sb("ones_row_b", [128, 128], bf16)
        sel32_b = sb("sel32_b", [128, 32, 128], bf16)
        spread_b = sb("spread_b", [128, A_E, 32], bf16)
        half = sb("half", [128, G])
        neg_a = sb("neg_a", [128, NSTATE])
        fk_row_bias = sb("fk_row_bias", [128, B * S], bf16)
        ik_row_bias = sb("ik_row_bias", [128, B * S], bf16)
        fk_bias = sb("fk_bias", [128, B])
        ik_bias = sb("ik_bias", [128, B])
        ik_bias_b1 = sb("ik_bias_b1", [128, B])
        neg_b1 = sb("neg_b1", [128, 1])
        a_exp = sb("a_exp", [128, NSTATE])

        def per_group(name, shape, dt=fp32):
            return [sb(f"{name}{g}", shape, dt) for g in groups]

        x_tok = per_group("x_tok", [128, G, D])
        x_pe = per_group("x_pe", [128, G, D])
        x_res = per_group("x_res", [128, G, D])
        h_tok = per_group("h_tok", [128, G, D])
        x_t = per_group("x_t", [128, T])
        ctx_sb = per_group("ctx_sb", [128, 2, T])
        v_ctx_sb = per_group("v_ctx_sb", [128, G, D])
        q_t = per_group("q_t", [128, T])
        k_t = per_group("k_t", [128, T])
        q_heads = per_group("q_heads", [128, NQ, T])
        k_heads = per_group("k_heads", [128, NQ, T])
        v_heads_a = per_group("v_heads_a", [128, G, A_HEADS * (D // A_HEADS + 1)])
        v_heads_x = per_group("v_heads_x", [128, G, X_HEADS * (D // X_HEADS + 1)])
        neg_max = per_group("neg_max", [128, G, 128])
        max_t = per_group("max_t", [128, 2, NQ, 128])
        probs = [sb(f"probs{i}", [128, 2, 512]) for i in range(2)]
        rec = sb("rec", [128, A_HEADS])
        att = per_group("att", [128, G, D])
        att_t = per_group("att_t", [128, T])
        stats = sb("stats", [128, G, 6])
        mean_var = per_group("mean_var", [128, G, 2])
        var_eps = sb("var_eps", [128, G])
        rstd = per_group("rstd", [128, G])

        logits = sb("logits", [128, G, A_E])
        top8 = sb("top8", [128, G, 8])
        top_i = sb("top_i", [128, G, 8], u32)
        top_f = sb("top_f", [128, G, 2])
        picked = sb("picked", [128, 2, G, A_E])
        gate_exp = sb("gate_exp", [128, G, A_E])
        gate_sum = sb("gate_sum", [128, 4, G])
        gates = per_group("gates", [128, G, 96])
        residue = sb("residue", [96, T])
        middle = sb("middle", [96, T], bf16)
        gate_parts = per_group("gate_parts", [96, T], bf16)
        silu = [sb(f"silu{i}", [128, T]) for i in range(2)]
        hidden = [sb(f"hidden{i}", [128, T]) for i in range(3)]

        NS = 2
        CHUNKS = NSTATE // NS

        def flat(ap):
            return ap.rearrange("p a b -> p (a b)")

        product = [flat(x_res[g][:, :, :]) for g in groups]
        x_gated = [(flat(att[g][:, :, :]), att_t[g][:, :]) for g in groups]
        moe_t = [flat(x_pe[g][:, :, :]) for g in groups]
        u_t, y_t = [k_t[g][:, :] for g in groups], [q_t[g][:, :] for g in groups]
        delta, z_t = [att_t[g][:, :] for g in groups], [flat(att[g][:, :, :]) for g in groups]
        delta_u = [flat(x_pe[g][:, :, :]) for g in groups]
        y_sum = [flat(x_res[g][:, :, :]) for g in groups]
        y_pair = [flat(h_tok[g][:, :, :]) for g in groups]
        (dt_abs, dt_exp, dt_relu, dt_ln), (dt_one, dt_back, dt_zero, dt_div) = (
            [[t[g][:, i, :] for g in groups] for i in range(4)] for t in (k_heads, q_heads))
        drive, state = [k_heads[g][:, 0:2, :] for g in groups], [k_heads[g][:, 2:4, :] for g in groups]
        read = [[q_heads[g][:, 2 * i:2 * i + 2, :] for i in range(2)] for g in groups]
        conv_x, conv_z_tap = ([max_t[g][:, i, :, :].rearrange("p a b -> p (a b)") for g in groups] for i in range(2))
        conv_z = [flat(v_heads_a[g][:, :, :])[:, 0:T] for g in groups]
        padded = [sb(f"padded_{n}", [128, G, S + 3]) for n in "xz"]
        dt_low = sb("dt_low", [RANK, T])
        bc_parts = per_group("bc_parts", [96, T], bf16)
        decay = [sb(f"decay{i}", [128, NS, T]) for i in range(2)]
        ik_row_sb = flat(decay[0][:, :, :]).bitcast(i32)

        psum = stack.enter_context(nc.psum_tensor("psum", [128, 8, 512], fp32))
        slot = [psum[:, i, :] for i in range(4)] + [psum[:, 4:6, :], psum[:, 6:8, :]]
        full = [sem(f"psum_full{i}") for i in range(6)]
        filled = [0] * 6
        released = [None] * 6
        nth = {}

        loaded = {p: sem("loaded_" + p) for p in [*PACKS, "rows", "ik"]}
        x_loaded = [sem(f"x_loaded{g}") for g in groups]
        ctx_loaded = [sem(f"ctx_loaded{g}") for g in groups]
        pool_consts, vector_consts, scalar_consts = sem("pool_consts"), sem("vector_consts"), sem("scalar_consts")
        x_pe_ready, res_ready = sem("x_pe_ready"), sem("res_ready")
        x_t_ready, x_tok_ready = sem("x_t_ready"), sem("x_tok_ready")
        heads_ready, v_ready = sem("heads_ready"), sem("v_ready")
        max_ready, max_t_ready = sem("max_ready"), sem("max_t_ready")
        exp_ready, weighed = sem("exp_ready"), sem("weighed")
        att_ready, att_t_ready = sem("att_ready"), sem("att_t_ready")
        sum_ready, var_ready, rstd_ready = sem("sum_ready"), sem("var_ready"), sem("rstd_ready")
        logits_ready, gate_shift_ready, gate_exp_ready = sem("logits_ready"), sem("gate_shift_ready"), sem("gate_exp_ready")
        gates_ready, gate_parts_ready = sem("gates_ready"), sem("gate_parts_ready")
        x_gated_ready, silu_ready, hidden_ready = sem("x_gated_ready"), sem("silu_ready"), sem("hidden_ready")
        hidden_used, moe_t_ready = sem("hidden_used"), sem("moe_t_ready")
        padded_ready, conv_x_ready, conv_z_ready = sem("padded_ready"), sem("conv_x_ready"), sem("conv_z_ready")
        u_ready, z_ready, dt_low_ready = sem("u_ready"), sem("z_ready"), sem("dt_low_ready")
        bc_parts_ready, dt_exp_ready, dt_one_ready = sem("bc_parts_ready"), sem("dt_exp_ready"), sem("dt_one_ready")
        dt_ln_ready, delta_ready = sem("dt_ln_ready"), sem("delta_ready")
        neg_a_ready = sem("neg_a_ready")
        decay_exp_ready, decay_ready, scanned = sem("decay_exp_ready"), sem("decay_ready"), sem("scanned")
        bc_used, y_sum_ready, y_ready = sem("bc_used"), sem("y_sum_ready"), sem("y_ready")
        vector_step, scalar_step, pool_step = sem("vector_step"), sem("scalar_step"), sem("pool_step")
        stored = sem("stored")

        VECTOR_CONSTS, POOL_CONSTS = 7, 2 + 5 * NG

        block = stack.enter_context(nc.Block())

        ORDER = [(layer, g) for layer in range(1, STAGE + 1) for g in groups]
        FORM = {1: (4, 8, 1), 2: (2, 16, 2), 5: (2, 16, 2)}
        MOE = {3: (A_E, A_BLOCKS), 6: (F_E, F_E * F_I // 128)}

        def before(layer, g, per):
            return sum(per(*o) for o in ORDER[:ORDER.index((layer, g))])

        def rank(layer, g):
            return before(layer, g, lambda l, _: 1)

        def att_rank(layer, g):
            return before(layer, g, lambda l, _: l in FORM)

        def proj_rank(layer, g):
            return before(layer, g, lambda l, _: l in (1, 2))

        def moe_rank(layer, g):
            return before(layer, g, lambda l, _: l in MOE)

        def max_rank(layer, g):
            return before(layer, g, lambda l, _: NQ * G // FORM[l][2] if l in FORM else 0)

        def block_rank(layer, g):
            return before(layer, g, lambda l, _: MOE[l][1] if l in MOE else 0)

        def norm_rank(layer, g, second=False):
            return before(layer, g, lambda l, _: 2 if l == 1 else 1) + second

        def v_heads(layer, g):
            return v_heads_a[g] if layer == 1 else v_heads_x[g]

        def heads_of(ap, heads):
            return ap.rearrange("p (j k) -> p j k", j=heads)

        @block.tensor
        def _(pe):
            mm = nc.tensor.matmul

            def claim(s, label, sem_, value):
                if released[s]:
                    pe.wait_ge(*released[s])
                released[s] = (sem_, value)
                if label:
                    filled[s] += 1
                    nth[label] = filled[s]
                return slot[s]

            def to_t(src, dst):
                for b in range(G):
                    last = nc.tensor.transpose(dst[0:src.shape[2], b * S:(b + 1) * S], src[:, b, :], ident)
                return last

            def by_token(dst, *pairs):
                for b in range(G):
                    for n, (left_t, right) in enumerate(pairs):
                        last = mm(dst[:, b * S:(b + 1) * S], left_t[:, b * S:(b + 1) * S], right,
                                  start=n == 0, stop=n == len(pairs) - 1)
                return last

            def x_to_t(layer, g):
                r = rank(layer, g)
                pe.wait_ge(x_tok_ready, rank(layer - 1, g) + 1)
                dst = claim(2, ("x_t", layer, g), x_t_ready, r + 1)
                to_t(x_tok[g], dst).then_inc(full[2], 1)

            def scores(layer, g, c):
                heads, _, seqs = FORM[layer]
                queries = x_t[g] if layer == 5 else q_t[g]
                for quad in range(NQ):
                    s = quad % 2
                    dst = claim(s, ("scores", layer, g, c, quad), max_ready,
                                max_rank(layer, g) + NQ * c + quad + 1)
                    rows = slice(32 * quad, 32 * quad + 32)
                    for i in range(seqs):
                        b = c * seqs + i
                        part = heads_of(dst[:, i * 256:i * 256 + heads * 128], heads)
                        last = mm(part, queries[rows, b * S:(b + 1) * S],
                                  k_heads[g][rows, 0:heads, b * S:(b + 1) * S], start=True, stop=layer == 1)
                        if layer > 1:
                            bias = fk_row_bias if layer == 2 else ik_row_bias
                            at = (g * G + b) * S
                            last = mm(part, ones_row_b[rows, :],
                                      bias[rows, at:at + S].unsqueeze(1).broadcast_to([32, heads, S]),
                                      start=False, stop=True)
                    last.then_inc(full[s], 1)

            def weigh(layer, g, u):
                heads, hd, _ = FORM[layer]
                a, b = att_rank(layer, g), u // 2
                if u % 2 == 0:
                    claim(3, None, att_ready, a * G + b + 1)
                pe.wait_ge(exp_ready, a * 2 * G + u + 1)
                for i in range(2):
                    for j in range(heads):
                        h = (2 * (u % 2) + i) * heads + j
                        cols = slice(h * (hd + 1), (h + 1) * (hd + 1))
                        last = mm(slot[3][:, cols], probs[u % 2][:, i, j * 128:(j + 1) * 128],
                                  v_heads(layer, g)[:, b, cols], start=True, stop=True)
                last.then_inc(weighed, 1)

            def attention(layer, g):
                heads, _, seqs = FORM[layer]
                a, chunks = att_rank(layer, g), G // seqs
                keys = ctx_sb[g][:, 0, :] if layer == 5 else k_t[g]
                pe.wait_ge(heads_ready, a + 1)
                for c in range(2):
                    scores(layer, g, c)
                for b in range(G):
                    pe.wait_ge(max_ready, max_rank(layer, g) + NQ * (b // seqs + 1))
                    dst = claim(2, ("max_t", layer, g, b), max_t_ready, a * G + b + 1)
                    nc.tensor.transpose(dst[:, 0:S], neg_max[g][:, b, :], ident).then_inc(full[2], 1)
                    for part_ in range(2):
                        u = 2 * b + part_
                        s = 4 + u % 2
                        dst = claim(s, ("scores_t", layer, g, u), exp_ready, a * 2 * G + u + 1)
                        quads = (2 * part_, 2 * part_ + 1)
                        for i, quad in enumerate(quads):
                            rows = slice(32 * quad, 32 * quad + 32)
                            mm(heads_of(dst[:, i, 0:heads * 128], heads), keys[rows, b * S:(b + 1) * S],
                               q_heads[g][rows, 0:heads, b * S:(b + 1) * S], start=True, stop=False)
                        if part_ == 0:
                            pe.wait_ge(max_t_ready, a * G + b + 1)
                        for i, quad in enumerate(quads):
                            rows = slice(32 * quad, 32 * quad + 32)
                            last = mm(heads_of(dst[:, i, 0:heads * 128], heads), ones[rows, :],
                                      max_t[g][rows, b % 2, 0:heads, :], start=False, stop=True)
                        last.then_inc(full[s], 1)
                        if u == 0:
                            pe.wait_ge(v_ready, a + 1)
                        else:
                            weigh(layer, g, u - 1)
                    if b + 2 < chunks:
                        scores(layer, g, b + 2)
                weigh(layer, g, 2 * G - 1)

            def att_to_t(layer, g):
                p = proj_rank(layer, g)
                pe.wait_ge(att_ready, (att_rank(layer, g) + 1) * G)
                to_t(att[g], claim(0, ("att_t", layer, g), att_t_ready, p + 1)).then_inc(full[0], 1)
                pe.wait_ge(att_t_ready, p + 1)

            def layer1(g):
                pe.wait_ge(x_pe_ready, g + 1)
                to_t(x_pe[g], claim(2, ("x_t", 1, g), x_t_ready, rank(1, g) + 1)).then_inc(full[2], 1)
                pe.wait_ge(x_t_ready, rank(1, g) + 1)
                a = att_rank(1, g)
                mm(claim(1, ("wk", 1, g), heads_ready, a + 1), W["wk"], x_t[g][:, :],
                   start=True, stop=True).then_inc(full[1], 1)
                mm(claim(0, ("wq", 1, g), heads_ready, a + 1), W["wq"], x_t[g][:, :],
                   start=True, stop=True).then_inc(full[0], 1)
                by_token(claim(2, ("wv", 1, g), v_ready, a + 1), (x_t[g], W["wv"])).then_inc(full[2], 1)
                attention(1, g)
                att_to_t(1, g)
                by_token(claim(1, ("sum", 1, g), sum_ready, rank(1, g) + 1),
                         (att_t[g], W["wo"])).then_inc(full[1], 1)

            def layer2(g):
                a = att_rank(2, g)
                if g == 0:
                    pe.wait_ge(loaded["cross"], 16)
                pe.wait_ge(ctx_loaded[g], 32)
                dst = claim(0, ("wk", 2, g), heads_ready, a + 1)
                for c in range(2):
                    last = mm(dst, W["w_src"][:, c * 256:c * 256 + 128], ctx_sb[g][:, c, :],
                              start=c == 0, stop=c == 1)
                last.then_inc(full[0], 1)
                by_token(claim(1, ("wv", 2, g), v_ready, a + 1),
                         *((ctx_sb[g][:, c, :], W["w_src"][:, c * 256 + 128:c * 256 + 256]) for c in range(2))
                         ).then_inc(full[1], 1)
                x_to_t(2, g)
                pe.wait_ge(x_t_ready, rank(2, g) + 1)
                mm(claim(3, ("wq", 2, g), heads_ready, a + 1), W["w_tgt"], x_t[g][:, :],
                   start=True, stop=True).then_inc(full[3], 1)
                attention(2, g)
                att_to_t(2, g)
                by_token(claim(1, ("sum", 2, g), sum_ready, rank(2, g) + 1),
                         (x_t[g], W["w_out"][:, 0:128]), (att_t[g], W["w_out"][:, 128:256])).then_inc(full[1], 1)

            def gates_to_t(layer, g):
                m = moe_rank(layer, g)
                pe.wait_ge(gates_ready, m + 1)
                to_t(gates[g], claim(1, ("gates_t", layer, g), gate_parts_ready, m + 1)
                     ).then_inc(full[1], 1)
                pe.wait_ge(gate_parts_ready, m + 1)

            def router(layer, g, name):
                experts = MOE[layer][0]
                x_to_t(layer, g)
                pe.wait_ge(x_t_ready, rank(layer, g) + 1)
                dst = claim(0, ("logits", layer, g), logits_ready, moe_rank(layer, g) + 1)
                for b in range(G):
                    last = mm(dst[:, b * experts:(b + 1) * experts], x_t[g][:, b * S:(b + 1) * S], W[name],
                              start=True, stop=True)
                last.then_inc(full[0], 1)

            def down(layer, g, k, w):
                blocks = MOE[layer][1]
                pe.wait_ge(hidden_ready, block_rank(layer, g) + k + 1)
                mm(slot[3], w[:, k * 128:(k + 1) * 128], hidden[k % 3][:, :],
                   start=k == 0, stop=k == blocks - 1).then_inc(hidden_used, 1)

            def moe_to_tok(layer, g):
                pe.wait_ge(moe_t_ready, moe_rank(layer, g) + 1)
                dst = claim(0, ("sum", layer, g), sum_ready, rank(layer, g) + 1)
                for b in range(G):
                    last = nc.tensor.transpose(dst[:, b * S:(b + 1) * S], moe_t[g][:, b * S:(b + 1) * S], ident)
                last.then_inc(full[0], 1)

            def layer3(g):
                if g == 0:
                    pe.wait_ge(loaded["moe0"], 16)
                router(3, g, "router0")
                claim(3, None, moe_t_ready, moe_rank(3, g) + 1)
                first = block_rank(3, g)
                for k in range(A_BLOCKS):
                    s = 4 + k % 2
                    dst = claim(s, ("up", 3, g, k), hidden_ready, first + k + 1)
                    for i, name in enumerate(("wg0", "wu0")):
                        last = mm(dst[:, i, :], W[name][:, k * 128:(k + 1) * 128], x_t[g][:, :],
                                  start=True, stop=True)
                    last.then_inc(full[s], 1)
                    if k == 1:
                        gates_to_t(3, g)
                    if k >= 1:
                        mm(claim(2, ("gate", 3, g, k), hidden_ready, first + k + 1),
                           spread_b[0:96, 4 * (k - 1):4 * k, :].rearrange("p e m -> p (e m)"), gate_parts[g][:, :],
                           start=True, stop=True).then_inc(full[2], 1)
                        down(3, g, k - 1, W["wd0"])
                down(3, g, A_BLOCKS - 1, W["wd0"])
                moe_to_tok(3, g)

            def layer6(g):
                if g == 0:
                    pe.wait_ge(loaded["moe1"], 16)
                router(6, g, "router1")
                claim(3, None, moe_t_ready, moe_rank(6, g) + 1)
                first, blocks = block_rank(6, g), MOE[6][1]
                per = F_I // 128

                def gate(e):
                    s = 1 + e % 2
                    mm(claim(s, ("gate", 6, g, e), x_gated_ready, g * F_E + e + 1), sel32_b[0:96, e, :],
                       gate_parts[g][:, :], start=True, stop=True).then_inc(full[s], 1)

                for k in range(blocks):
                    e, s = k // per, 4 + k % 2
                    dst = claim(s, ("up", 6, g, k), hidden_ready, first + k + 1)
                    mm(dst[:, 0, :], W["w1"][:, k * 128:(k + 1) * 128], x_t[g][:, :], start=True, stop=True)
                    if k == 0:
                        gates_to_t(6, g)
                        gate(0)
                    if k % per == 0:
                        if e + 1 < F_E:
                            gate(e + 1)
                        pe.wait_ge(x_gated_ready, g * F_E + e + 1)
                    mm(dst[:, 1, :], W["w3"][:, k * 128:(k + 1) * 128], x_gated[g][e % 2],
                       start=True, stop=True).then_inc(full[s], 1)
                    if k:
                        down(6, g, k - 1, W["w2"])
                down(6, g, blocks - 1, W["w2"])
                moe_to_tok(6, g)

            def layer4(g):
                if g == 0:
                    pe.wait_ge(loaded["mamba"], 16)
                x_to_t(4, g)
                pe.wait_ge(x_t_ready, rank(4, g) + 1)
                for s in range(2):
                    mm(claim(s, ("in", g, s), padded_ready, 2 * g + s + 1), W["w_in"][:, s * 128:(s + 1) * 128],
                       x_t[g][:, :], start=True, stop=True).then_inc(full[s], 1)
                pe.wait_ge(u_ready, g + 1)
                mm(claim(2, ("dt_low", g), dt_low_ready, g + 1)[0:RANK, :], W["w_dtlow"], u_t[g],
                   start=True, stop=True).then_inc(full[2], 1)
                mm(claim(1, ("bc", g), bc_parts_ready, g + 1)[0:96, :], W["w_bc"], u_t[g],
                   start=True, stop=True).then_inc(full[1], 1)
                pe.wait_ge(dt_low_ready, g + 1)
                mm(claim(0, ("dt", g), dt_exp_ready, g + 1), W["w_dt"][0:RANK, :], dt_low[:, :],
                   start=True, stop=True).then_inc(full[0], 1)
                pe.wait_ge(bc_parts_ready, g + 1)
                for c in range(CHUNKS):
                    for kind in range(2):
                        for i in range(NS // 2):
                            unit = (2 * c + kind) * (NS // 2) + i
                            s = 4 + unit % 2
                            dst = claim(s, ("bc", g, unit), bc_used, g * 2 * NSTATE // 2 + unit + 1)
                            for half_ in range(2):
                                n = c * NS + 2 * i + half_
                                last = mm(dst[:, half_, :], sel32_b[0:96, kind * NSTATE + n, :],
                                          bc_parts[g][:, :], start=True, stop=True)
                            last.then_inc(full[s], 1)
                pe.wait_ge(y_ready, g + 1)
                pe.wait_ge(z_ready, g + 1)
                by_token(claim(0, ("sum", 4, g), sum_ready, rank(4, g) + 1),
                         (y_t[g], W["w_mo"][:, 0:128]), (z_t[g], W["w_mo"][:, 128:256])).then_inc(full[0], 1)

            def layer5(g):
                x_to_t(5, g)
                attention(5, g)

            pe.wait_ge(loaded["first"], 16)
            pe.wait_ge(pool_consts, POOL_CONSTS)
            pe.wait_ge(vector_consts, VECTOR_CONSTS)
            for layer, g in ORDER:
                (layer1, layer2, layer3, layer4, layer5, layer6)[layer - 1](g)

        @block.vector
        def _(dve):
            v = nc.vector
            steps = [0]

            def then(instruction):
                steps[0] += 1
                instruction.then_inc(vector_step, 1)
                dve.wait_ge(vector_step, steps[0])

            def constants():
                dve.wait_ge(loaded["first"], 16)
                v.tensor_copy(ones_row_b[:, :], W["quad_row"][:, 0:1].broadcast_to([128, 128])
                              ).then_inc(vector_consts, 1)
                v.tensor_copy(sel32_b[:, :, :], W["sel32"].unsqueeze(2).broadcast_to([128, 32, 128])
                              ).then_inc(vector_consts, 1)
                v.tensor_copy(spread_b[:, :, :], W["sel32"][:, 0:A_E].unsqueeze(2).broadcast_to([128, A_E, 32])
                              ).then_inc(vector_consts, 1)
                dve.wait_ge(loaded["rows"], 16)
                dve.wait_ge(loaded["masks"], 16)
                dve.wait_ge(loaded["ik"], 32)
                for dst, src in ((fk_row_bias, R["fk"]), (fk_bias, W["fk_tok"])):
                    v.tensor_scalar(dst[:, :], src, 0.0, -MASKED, ALU.is_equal, ALU.mult).then_inc(vector_consts, 1)
                for dst, src in ((ik_row_bias, ik_row_sb), (ik_bias, ik_tok_sb[:, :])):
                    v.tensor_scalar(dst[:, :], src, -1.0, MASKED, ALU.add, ALU.mult).then_inc(vector_consts, 1)

            def cross_constants():
                dve.wait_ge(vector_consts, VECTOR_CONSTS)
                dve.wait_ge(loaded["cross"], 16)
                v.tensor_scalar(ik_bias_b1[:, :], ik_bias[:, :], W["b1"], None, ALU.add)
                then(v.tensor_scalar(neg_b1[:, :], W["b1"], -1.0, None, ALU.mult))

            def spread_heads(dst, src, masks, heads):
                for j in range(heads):
                    last = v.tensor_scalar(dst[:, j, :], src, masks[:, j:j + 1], float(D // NQ // heads) ** -0.5,
                                           ALU.mult, ALU.mult)
                return last

            def prepare1(g):
                a = att_rank(1, g)
                dve.wait_ge(full[1], nth["wk", 1, g])
                then(v.tensor_scalar(k_t[g][:, :], slot[1], W["bk"], None, ALU.add))
                spread_heads(k_heads[g], k_t[g][:, :], W["head4"], 4)
                dve.wait_ge(full[0], nth["wq", 1, g])
                then(v.tensor_scalar(q_t[g][:, :], slot[0], W["bq"], None, ALU.add))
                spread_heads(q_heads[g], q_t[g][:, :], W["head4"], 4).then_inc(heads_ready, 1)
                dve.wait_ge(full[2], nth["wv", 1, g])
                hd = D // A_HEADS
                v.tensor_tensor(v_heads_a[g][:, :, :].rearrange("p b (h e) -> p b h e", e=hd + 1)[:, :, :, 0:hd],
                                slot[2].rearrange("p (b h e) -> p b h e", b=G, e=hd),
                                R["bv"].rearrange("p (h e) -> p h e", e=hd).unsqueeze(1)
                                .broadcast_to([128, G, A_HEADS, hd]), ALU.add).then_inc(v_ready, 1)

            def values_x(g):
                hd = D // X_HEADS
                return (v_heads_x[g][:, :, :].rearrange("p b (h e) -> p b h e", e=hd + 1)[:, :, :, 0:hd], hd)

            def prepare2(g):
                if g == 0:
                    cross_constants()
                at = slice(g * T, (g + 1) * T)
                dve.wait_ge(full[0], nth["wk", 2, g])
                then(v.scalar_tensor_tensor(k_t[g][:, :], slot[0], W["b_srck"], R["fk"][:, at], ALU.add, ALU.mult))
                spread_heads(k_heads[g], k_t[g][:, :], W["head2"], 2)
                dve.wait_ge(full[1], nth["wv", 2, g])
                then(v.tensor_tensor(att[g][:, :, :], slot[1].rearrange("p (b e) -> p b e", b=G),
                                     R["b_srcv"].unsqueeze(1).broadcast_to([128, G, D]), ALU.add))
                dst, hd = values_x(g)
                v.tensor_tensor(dst, att[g][:, :, :].rearrange("p b (h e) -> p b h e", e=hd),
                                W["fk_tok"][:, g * G:(g + 1) * G].unsqueeze(2).unsqueeze(3)
                                .broadcast_to([128, G, X_HEADS, hd]), ALU.mult).then_inc(v_ready, 1)
                dve.wait_ge(full[3], nth["wq", 2, g])
                then(v.scalar_tensor_tensor(q_t[g][:, :], slot[3], W["b_tgt"], R["fk"][:, at],
                                            ALU.add, ALU.mult))
                spread_heads(q_heads[g], q_t[g][:, :], W["head2"], 2).then_inc(heads_ready, 1)

            def prepare5(g):
                dve.wait_ge(ctx_loaded[g], 32)
                spread_heads(k_heads[g], ctx_sb[g][:, 0, :], W["head2"], 2)
                dst, hd = values_x(g)
                v.tensor_copy(dst, v_ctx_sb[g][:, :, :].rearrange("p b (h e) -> p b h e", e=hd)).then_inc(v_ready, 1)
                dve.wait_ge(x_t_ready, rank(5, g) + 1)
                spread_heads(q_heads[g], x_t[g][:, :], W["head2"], 2).then_inc(heads_ready, 1)

            def maxima(layer, g, c):
                heads, _, seqs = FORM[layer]
                for quad in range(NQ):
                    dve.wait_ge(full[quad % 2], nth["scores", layer, g, c, quad])
                    dst = neg_max[g][:, c * seqs:(c + 1) * seqs, 32 * quad:32 * quad + heads]
                    v.tensor_reduce(dst, slot[quad % 2].rearrange("p (i j k) -> p i j k", i=seqs, j=heads), AX,
                                    ALU.max, negate=True).then_inc(max_ready, 1)

            def attention(layer, g):
                heads, hd, seqs = FORM[layer]
                a, chunks = att_rank(layer, g), G // seqs

                def normalize(b):
                    dve.wait_ge(weighed, a * 2 * G + 2 * b + 2)
                    sums = slot[3][:, 0:NQ * heads * (hd + 1)].rearrange("p (h e) -> p h e", e=hd + 1)
                    then(v.reciprocal(rec[:, 0:NQ * heads].unsqueeze(2), sums[:, :, hd:hd + 1]))
                    v.tensor_tensor(att[g][:, b, :].rearrange("p (h e) -> p h e", e=hd), sums[:, :, 0:hd],
                                    rec[:, 0:NQ * heads].unsqueeze(2).broadcast_to([128, NQ * heads, hd]),
                                    ALU.mult).then_inc(att_ready, 1)

                for c in range(2):
                    maxima(layer, g, c)
                for b in range(G):
                    dve.wait_ge(full[2], nth["max_t", layer, g, b])
                    if b >= 2:
                        dve.wait_ge(full[5], nth["scores_t", layer, g, 2 * (b - 2) + 1])
                    v.scalar_tensor_tensor(max_t[g][:, b % 2, 0:heads, :],
                                           slot[2][:, 0:S].unsqueeze(1).broadcast_to([128, heads, S]),
                                           neg_b1[:, :] if layer == 5 else 0.0,
                                           W["quad_row"][:, 0:heads].unsqueeze(2).broadcast_to([128, heads, S]),
                                           ALU.add, ALU.mult).then_inc(max_t_ready, 1)
                    if b:
                        normalize(b - 1)
                    if b + 2 < chunks:
                        maxima(layer, g, b + 2)
                normalize(G - 1)

            def norm(layer, g, src, dst, second=False):
                for b in range(G):
                    last = v.bn_stats(stats[:, b, :], src[:, b, :])
                then(last)
                for b in range(G):
                    last = v.bn_aggr(mean_var[g][:, b, :], stats[:, b, :])
                last.then_inc(var_ready, 1)
                dve.wait_ge(rstd_ready, norm_rank(layer, g, second) + 1)
                for b in range(G):
                    last = v.tensor_scalar(dst[:, b, :], src[:, b, :], mean_var[g][:, b, 0:1],
                                           rstd[g][:, b:b + 1], ALU.subtract, ALU.mult)
                return last

            def add_residual(layer, g, s, residual):
                n = rank(layer, g) + 1
                dve.wait_ge(full[s], nth["sum", layer, g])
                v.tensor_tensor(h_tok[g][:, :, :], slot[s].rearrange("p (b e) -> p b e", b=G), residual[:, :, :],
                                ALU.add).then_inc(sum_ready, 1)
                dve.wait_ge(sum_ready, n)

            def layer1(g):
                dve.wait_ge(x_loaded[g], 16)
                v.tensor_tensor(x_pe[g][:, :, :], x_tok[g][:, :, :],
                                W["pe"].unsqueeze(1).broadcast_to([128, G, D]), ALU.add).then_inc(x_pe_ready, 1)
                prepare1(g)
                attention(1, g)
                dve.wait_ge(res_ready, proj_rank(1, g) + 1)
                add_residual(1, g, 1, x_res[g])
                then(norm(1, g, h_tok[g], h_tok[g]))
                wide = [128, G, D]
                then(v.tensor_tensor(h_tok[g][:, :, :], h_tok[g][:, :, :],
                                     R["gamma"].unsqueeze(1).broadcast_to(wide), ALU.mult))
                then(v.tensor_tensor(h_tok[g][:, :, :], h_tok[g][:, :, :],
                                     R["beta"].unsqueeze(1).broadcast_to(wide), ALU.add))
                then(v.tensor_tensor(h_tok[g][:, :, :], h_tok[g][:, :, :], x_tok[g][:, :, :], ALU.add))
                norm(1, g, h_tok[g], x_tok[g], second=True).then_inc(x_tok_ready, 1)

            def layer2(g):
                prepare2(g)
                attention(2, g)
                dve.wait_ge(res_ready, proj_rank(2, g) + 1)
                add_residual(2, g, 1, x_res[g])
                norm(2, g, h_tok[g], x_tok[g]).then_inc(x_tok_ready, 1)

            def layer5(g):
                prepare5(g)
                attention(5, g)
                dve.wait_ge(att_ready, (att_rank(5, g) + 1) * G)
                v.tensor_tensor(h_tok[g][:, :, :], att[g][:, :, :], x_tok[g][:, :, :], ALU.add).then_inc(sum_ready, 1)
                dve.wait_ge(sum_ready, rank(5, g) + 1)
                norm(5, g, h_tok[g], x_tok[g]).then_inc(x_tok_ready, 1)

            def split(s, label, dst, done):
                dve.wait_ge(full[s], nth[label])
                x96 = slot[s][0:96, :]
                then(v.tensor_copy(dst[0:96, :], x96))
                then(v.tensor_tensor(residue[0:96, :], x96, dst[0:96, :], ALU.subtract))
                v.tensor_copy(dst[32:64, :], residue[32:64, :])
                then(v.tensor_copy(middle[64:96, :], residue[64:96, :]))
                v.tensor_tensor(dst[64:96, :], residue[64:96, :], middle[64:96, :], ALU.subtract).then_inc(done, 1)

            def route(layer, g):
                experts = MOE[layer][0]
                m = moe_rank(layer, g)
                lg = logits[:, :, 0:experts]
                full_shape = [128, G, experts]
                dve.wait_ge(full[0], nth["logits", layer, g])
                v.tensor_copy(lg, slot[0][:, 0:G * experts].rearrange("p (b e) -> p b e", b=G)
                              ).then_inc(logits_ready, 1)
                dve.wait_ge(logits_ready, m + 1)
                for b in range(G):
                    last = v.max(top8[:, b, :], logits[:, b, 0:experts])
                then(last)
                v.tensor_tensor(gate_exp[:, :, 0:experts], lg, top8[:, :, 0:1].broadcast_to(full_shape),
                                ALU.subtract).then_inc(gate_shift_ready, 1)
                for b in range(G):
                    last = v.max_index(top_i[:, b, :], top8[:, b, :], logits[:, b, 0:experts])
                then(last)
                then(v.tensor_copy(top_f[:, :, :], top_i[:, :, 0:2]))
                for i in range(2):
                    last = v.tensor_tensor(picked[:, i, :, 0:experts],
                                           W["iota"][:, 0:experts].unsqueeze(1).broadcast_to(full_shape),
                                           top_f[:, :, i:i + 1].broadcast_to(full_shape), ALU.is_equal)
                then(last)
                then(v.tensor_tensor(picked[:, 0, :, 0:experts], picked[:, 0, :, 0:experts],
                                     picked[:, 1, :, 0:experts], ALU.add))
                dve.wait_ge(gate_exp_ready, m + 1)
                ge = gate_exp[:, :, 0:experts]
                then(v.tensor_reduce(gate_sum[:, 0, :], ge, AX, ALU.add))
                then(v.reciprocal(gate_sum[:, 1, :], gate_sum[:, 0, :]))
                then(v.tensor_tensor(lg, ge, gate_sum[:, 1, :].unsqueeze(2).broadcast_to(full_shape), ALU.mult))
                then(v.tensor_tensor(lg, lg, picked[:, 0, :, 0:experts], ALU.mult))
                then(v.tensor_reduce(gate_sum[:, 2, :], lg, AX, ALU.add))
                if layer == 3:
                    then(v.tensor_scalar(gate_sum[:, 2, :], gate_sum[:, 2, :], 1e-9, None, ALU.add))
                then(v.reciprocal(gate_sum[:, 3, :], gate_sum[:, 2, :]))
                v.tensor_tensor(gates[g][:, :, :].rearrange("p b (c e) -> p b c e", c=3)
                                [:, :, :, 0:experts],
                                lg.unsqueeze(2).broadcast_to([128, G, 3, experts]),
                                gate_sum[:, 3, :].unsqueeze(2).unsqueeze(3).broadcast_to([128, G, 3, experts]),
                                ALU.mult).then_inc(gates_ready, 1)
                split(1, ("gates_t", layer, g), gate_parts[g], gate_parts_ready)

            def layer3(g):
                first = block_rank(3, g)

                def hide(k):
                    n = first + k
                    dve.wait_ge(silu_ready, n + 1)
                    if n >= 3:
                        dve.wait_ge(hidden_used, n - 2)
                    if k == 0:
                        v.tensor_tensor(hidden[k % 3][:, :], silu[k % 2][:, :], slot[4][:, 1, :],
                                        ALU.mult).then_inc(hidden_ready, 1)
                    else:
                        if k >= 2:
                            dve.wait_ge(hidden_ready, n)
                        then(v.tensor_tensor(product[g], silu[k % 2][:, :], slot[4 + k % 2][:, 1, :], ALU.mult))
                        dve.wait_ge(full[2], nth["gate", 3, g, k])
                        v.tensor_tensor(hidden[k % 3][:, :], product[g], slot[2], ALU.mult
                                        ).then_inc(hidden_ready, 1)

                route(3, g)
                for k in range(A_BLOCKS):
                    hide(k)
                add_residual(3, g, 0, x_tok[g])
                norm(3, g, h_tok[g], x_tok[g]).then_inc(x_tok_ready, 1)

            def layer6(g):
                first, blocks, per = block_rank(6, g), MOE[6][1], F_I // 128

                def gate_x(e):
                    s = 1 + e % 2
                    dve.wait_ge(full[s], nth["gate", 6, g, e])
                    v.tensor_tensor(x_gated[g][e % 2], x_t[g][:, :], slot[s], ALU.mult
                                    ).then_inc(x_gated_ready, 1)

                route(6, g)
                gate_x(0)
                for k in range(blocks):
                    n = first + k
                    if k % per == 0 and k // per + 1 < F_E:
                        gate_x(k // per + 1)
                    dve.wait_ge(silu_ready, n + 1)
                    dve.wait_ge(full[4 + k % 2], nth["up", 6, g, k])
                    if n >= 3:
                        dve.wait_ge(hidden_used, n - 2)
                    v.tensor_tensor(hidden[k % 3][:, :], silu[k % 2][:, :], slot[4 + k % 2][:, 1, :], ALU.mult
                                    ).then_inc(hidden_ready, 1)
                add_residual(6, g, 0, x_tok[g])
                norm(6, g, h_tok[g], x_tok[g]).then_inc(x_tok_ready, 1)

            def layer4(g):
                dve.wait_ge(loaded["mamba"], 16)
                if g == 0:
                    dve.wait_ge(scalar_consts, 1)
                    v.tensor_scalar(neg_a[:, :], a_exp[:, :], -1.0, None, ALU.mult).then_inc(neg_a_ready, 1)
                dve.wait_ge(padded_ready, 2 * g + 1)
                out3 = conv_x[g].rearrange("p (b l) -> p b l", b=G)
                then(v.tensor_scalar(out3, padded[0][:, :, 0:S], W["k_x"][:, 0:1], None, ALU.mult))
                for tap in range(1, 4):
                    last = v.scalar_tensor_tensor(out3, padded[0][:, :, tap:tap + S], W["k_x"][:, tap:tap + 1],
                                                  out3, ALU.mult, ALU.add)
                    if tap < 3:
                        then(last)
                last.then_inc(conv_x_ready, 1)
                split(1, ("bc", g), bc_parts[g], bc_parts_ready)
                dve.wait_ge(dt_exp_ready, g + 1)
                v.tensor_scalar(dt_one[g], dt_exp[g], 1.0, None, ALU.add).then_inc(dt_one_ready, 1)
                dve.wait_ge(dt_one_ready, g + 1)
                then(v.tensor_scalar(dt_back[g], dt_one[g], -1.0, None, ALU.add))
                then(v.tensor_scalar(dt_zero[g], dt_back[g], 0.0, None, ALU.is_equal))
                then(v.tensor_tensor(dt_back[g], dt_back[g], dt_zero[g], ALU.add))
                then(v.reciprocal(dt_div[g], dt_back[g]))
                then(v.tensor_tensor(dt_div[g], dt_div[g], dt_exp[g], ALU.mult))
                dve.wait_ge(dt_ln_ready, g + 1)
                then(v.tensor_tensor(dt_zero[g], dt_ln[g], dt_zero[g], ALU.add))
                then(v.tensor_tensor(dt_div[g], dt_div[g], dt_zero[g], ALU.mult))
                v.tensor_tensor(delta[g], dt_div[g], dt_relu[g], ALU.add).then_inc(delta_ready, 1)
                dve.wait_ge(delta_ready, g + 1)
                then(v.tensor_tensor(delta_u[g], delta[g], u_t[g], ALU.mult))
                for c in range(CHUNKS):
                    chunk = g * CHUNKS + c
                    if c:
                        dve.wait_ge(scanned, chunk)
                    for i in range(NS // 2):
                        unit = 2 * c * (NS // 2) + i
                        s = 4 + unit % 2
                        dve.wait_ge(full[s], nth["bc", g, unit])
                        v.tensor_tensor(drive[g][:, 2 * i:2 * i + 2, :], slot[s],
                                        delta_u[g].unsqueeze(1).broadcast_to([128, 2, T]), ALU.mult
                                        ).then_inc(bc_used, 1)
                    dve.wait_ge(bc_used, g * NSTATE + 2 * c * (NS // 2) + NS // 2)
                    dve.wait_ge(decay_ready, chunk + 1)
                    v.tensor_tensor_scan(state[g][:, :, :].rearrange("p n l -> p (n l)"),
                                         decay[c % 2][:, :, :].rearrange("p n l -> p (n l)"),
                                         drive[g][:, :, :].rearrange("p n l -> p (n l)"), 0.0,
                                         ALU.mult, ALU.add).then_inc(scanned, 1)
                    dve.wait_ge(scanned, chunk + 1)
                    if chunk >= 2:
                        dve.wait_ge(y_sum_ready, chunk - 1)
                    for i in range(NS // 2):
                        unit = (2 * c + 1) * (NS // 2) + i
                        s = 4 + unit % 2
                        dve.wait_ge(full[s], nth["bc", g, unit])
                        v.tensor_tensor(read[g][c % 2][:, 2 * i:2 * i + 2, :], slot[s], state[g][:, 2 * i:2 * i + 2, :],
                                        ALU.mult).then_inc(bc_used, 1)
                dve.wait_ge(y_sum_ready, (g + 1) * CHUNKS)
                v.scalar_tensor_tensor(y_t[g], u_t[g], W["d_skip"], y_sum[g], ALU.mult, ALU.add
                                       ).then_inc(y_ready, 1)
                add_residual(4, g, 0, x_tok[g])
                norm(4, g, h_tok[g], x_tok[g]).then_inc(x_tok_ready, 1)

            constants()
            for layer, g in ORDER:
                (layer1, layer2, layer3, layer4, layer5, layer6)[layer - 1](g)

        @block.scalar
        def _(act):
            sc = nc.scalar

            def copy_x_t(layer, g):
                act.wait_ge(full[2], nth["x_t", layer, g])
                sc.copy(x_t[g][:, :], slot[2]).then_inc(x_t_ready, 1)

            def exponentials(layer, g):
                heads, _, _ = FORM[layer]
                a = att_rank(layer, g)
                for u in range(2 * G):
                    b, s = u // 2, 4 + u % 2
                    bias = {1: 0.0, 2: fk_bias[:, g * G + b:g * G + b + 1],
                            5: ik_bias_b1[:, g * G + b:g * G + b + 1]}[layer]
                    act.wait_ge(full[s], nth["scores_t", layer, g, u])
                    if a * 2 * G + u >= 2:
                        act.wait_ge(weighed, a * 2 * G + u - 1)
                    sc.activation(probs[u % 2][:, :, 0:heads * 128], slot[s][:, :, 0:heads * 128], ACT.Exp,
                                  bias=bias).then_inc(exp_ready, 1)

            def copy_att_t(layer, g):
                act.wait_ge(full[0], nth["att_t", layer, g])
                sc.copy(att_t[g][:, :], slot[0]).then_inc(att_t_ready, 1)

            def gate_exponentials(layer, g):
                experts, m = MOE[layer][0], moe_rank(layer, g)
                act.wait_ge(gate_shift_ready, m + 1)
                sc.activation(gate_exp[:, :, 0:experts], gate_exp[:, :, 0:experts], ACT.Exp
                              ).then_inc(gate_exp_ready, 1)

            def blocks_of(layer, g):
                first = block_rank(layer, g)
                for k in range(MOE[layer][1]):
                    n = first + k
                    act.wait_ge(full[4 + k % 2], nth["up", layer, g, k])
                    if n >= 2:
                        act.wait_ge(hidden_ready, n - 1)
                    sc.activation(silu[k % 2][:, :], slot[4 + k % 2][:, 0, :], ACT.Silu).then_inc(silu_ready, 1)

            def copy_moe_t(layer, g):
                act.wait_ge(hidden_used, block_rank(layer, g) + MOE[layer][1])
                sc.copy(moe_t[g], slot[3]).then_inc(moe_t_ready, 1)

            def layer1(g):
                copy_x_t(1, g)
                exponentials(1, g)
                copy_att_t(1, g)

            def layer2(g):
                copy_x_t(2, g)
                exponentials(2, g)
                copy_att_t(2, g)

            def moe(layer, g):
                copy_x_t(layer, g)
                gate_exponentials(layer, g)
                blocks_of(layer, g)
                copy_moe_t(layer, g)

            def layer4(g):
                copy_x_t(4, g)
                for s, convolved in enumerate((conv_x_ready, conv_z_ready)):
                    if g:
                        act.wait_ge(convolved, g)
                    act.wait_ge(full[s], nth["in", g, s])
                    sc.copy(padded[s][:, :, 1:S + 1], slot[s].rearrange("p (b l) -> p b l", b=G)
                            ).then_inc(padded_ready, 1)
                act.wait_ge(conv_x_ready, g + 1)
                sc.activation(u_t[g], conv_x[g], ACT.Gelu, bias=W["b_x"]).then_inc(u_ready, 1)
                act.wait_ge(full[2], nth["dt_low", g])
                sc.copy(dt_low[:, :], slot[2][0:RANK, :]).then_inc(dt_low_ready, 1)
                act.wait_ge(full[0], nth["dt", g])
                sc.activation(dt_abs[g], slot[0], ACT.Abs, bias=W["b_dt"]).then_inc(scalar_step, 1)
                sc.activation(dt_relu[g], slot[0], ACT.Relu, bias=W["b_dt"])
                act.wait_ge(scalar_step, g + 1)
                sc.activation(dt_exp[g], dt_abs[g], ACT.Exp, scale=-1.0).then_inc(dt_exp_ready, 1)
                act.wait_ge(dt_one_ready, g + 1)
                sc.activation(dt_ln[g], dt_one[g], ACT.Ln).then_inc(dt_ln_ready, 1)
                act.wait_ge(delta_ready, g + 1)
                if g == 0:
                    act.wait_ge(neg_a_ready, 1)
                for c in range(CHUNKS):
                    chunk = g * CHUNKS + c
                    if chunk >= 2:
                        act.wait_ge(scanned, chunk - 1)
                    for i in range(NS):
                        last = sc.activation(decay[c % 2][:, i, :], delta[g], ACT.Exp,
                                             scale=neg_a[:, c * NS + i:c * NS + i + 1])
                    last.then_inc(decay_exp_ready, 1)
                act.wait_ge(conv_z_ready, g + 1)
                sc.activation(z_t[g], conv_z[g], ACT.Gelu, bias=W["b_z"]).then_inc(z_ready, 1)

            def layer5(g):
                copy_x_t(5, g)
                exponentials(5, g)

            act.wait_ge(vector_consts, VECTOR_CONSTS)
            if STAGE >= 4:
                act.wait_ge(loaded["mamba"], 16)
                sc.activation(a_exp[:, :], W["a_log"], ACT.Exp).then_inc(scalar_consts, 1)
            for layer, g in ORDER:
                {1: layer1, 2: layer2, 4: layer4, 5: layer5}.get(layer, lambda g: moe(layer, g))(g)

        @block.gpsimd
        def _(pool):
            p = nc.gpsimd
            steps = [0]

            def then(instruction):
                steps[0] += 1
                instruction.then_inc(pool_step, 1)
                pool.wait_ge(pool_step, steps[0])

            def deviations(layer, g, second=False):
                pool.wait_ge(var_ready, norm_rank(layer, g, second) + 1)
                then(p.tensor_scalar(var_eps[:, :], mean_var[g][:, :, 1], LN_EPS, None, ALU.add))
                p.tensor_tensor(rstd[g][:, :], var_eps[:, :], half[:, :], ALU.pow).then_inc(rstd_ready, 1)

            def residual(layer, g, src, bias):
                p.tensor_tensor(x_res[g][:, :, :], src[g][:, :, :], R[bias].unsqueeze(1).broadcast_to([128, G, D]),
                                ALU.add).then_inc(res_ready, 1)

            def layer4(g):
                pool.wait_ge(padded_ready, 2 * g + 2)
                pool.wait_ge(loaded["mamba"], 16)
                out3 = conv_z[g].rearrange("p (b l) -> p b l", b=G)
                tap3 = conv_z_tap[g].rearrange("p (b l) -> p b l", b=G)
                then(p.tensor_scalar(out3, padded[1][:, :, 0:S], W["k_z"][:, 0:1], None, ALU.mult))
                for tap in range(1, 4):
                    then(p.tensor_scalar(tap3, padded[1][:, :, tap:tap + S], W["k_z"][:, tap:tap + 1], None,
                                         ALU.mult))
                    last = p.tensor_tensor(out3, out3, tap3, ALU.add)
                    if tap < 3:
                        then(last)
                last.then_inc(conv_z_ready, 1)
                starts = lambda c: decay[c % 2][:, :, :].rearrange("p n (b l) -> p n b l", b=G)[:, :, :, 0:1]

                def cut(c):
                    pool.wait_ge(decay_exp_ready, g * CHUNKS + c + 1)
                    p.memset(starts(c), 0.0).then_inc(decay_ready, 1)

                cut(0)
                for c in range(CHUNKS):
                    if c + 1 < CHUNKS:
                        cut(c + 1)
                    pool.wait_ge(bc_used, g * NSTATE + (c + 1) * NS)
                    pair = y_sum[g] if c == 0 else y_pair[g]
                    last = p.tensor_tensor(pair, read[g][c % 2][:, 0, :], read[g][c % 2][:, 1, :], ALU.add)
                    if c:
                        then(last)
                        last = p.tensor_tensor(y_sum[g], y_sum[g], y_pair[g], ALU.add)
                    last.then_inc(y_sum_ready, 1)
                    pool.wait_ge(y_sum_ready, g * CHUNKS + c + 1)

            p.memset(ones[:, :], 1.0).then_inc(pool_consts, 1)
            p.memset(half[:, :], -0.5).then_inc(pool_consts, 1)
            for g in groups:
                p.memset(neg_max[g][:, :, :], 0.0).then_inc(pool_consts, 1)
                p.memset(v_heads_a[g][:, :, :], 1.0).then_inc(pool_consts, 1)
                p.memset(v_heads_x[g][:, :, :], 1.0).then_inc(pool_consts, 1)
                p.memset(gates[g][:, :, :], 0.0).then_inc(pool_consts, 1)
                p.memset(padded[g][:, :, :], 0.0).then_inc(pool_consts, 1)
            pool.wait_ge(pool_consts, POOL_CONSTS)
            for layer, g in ORDER:
                if layer == 1:
                    if g == 0:
                        pool.wait_ge(loaded["rows"], 16)
                    pool.wait_ge(x_pe_ready, g + 1)
                    residual(1, g, x_pe, "bo")
                    deviations(1, g)
                    deviations(1, g, second=True)
                    continue
                if layer == 2:
                    pool.wait_ge(x_tok_ready, rank(1, g) + 1)
                    residual(2, g, x_tok, "b_out")
                if layer == 4:
                    layer4(g)
                deviations(layer, g)

        @block.sync
        def _(sp):
            where = dict(packed)
            for g in groups:
                sp.dma_start(x_tok[g][:, :, :], x[g * G:(g + 1) * G].rearrange("b s d -> s b d")
                             ).then_inc(x_loaded[g], 16)
                if g == 0:
                    sp.dma_start(pack_sb["first"][:, :], where["first"]).then_inc(loaded["first"], 16)
                    sp.dma_start(rows_sb[:, :], rows.broadcast_to([128, rows_width])).then_inc(loaded["rows"], 16)
            sp.dma_start(pack_sb["masks"][:, :], where["masks"]).then_inc(loaded["masks"], 16)
            sp.dma_start(ik_tok_sb[:, :], ik_tok).then_inc(loaded["ik"], 16)
            sp.dma_start(ik_row_sb, ik_row.broadcast_to([128, B * S])).then_inc(loaded["ik"], 16)
            sp.dma_start(pack_sb["cross"][:, :], where["cross"]).then_inc(loaded["cross"], 16)
            for g in groups:
                sp.dma_start(ctx_sb[g][:, :, :], ctx_t[:, :, g * T:(g + 1) * T].rearrange("c p t -> p c t")
                             ).then_inc(ctx_loaded[g], 16)
                sp.dma_start(v_ctx_sb[g][:, :, :], v_ctx[g * G:(g + 1) * G].rearrange("b s d -> s b d")
                             ).then_inc(ctx_loaded[g], 16)
            for name in ("moe0", "mamba", "moe1"):
                sp.dma_start(pack_sb[name][:, :], where[name]).then_inc(loaded[name], 16)
            for g in groups:
                sp.wait_ge(x_tok_ready, rank(STAGE, g) + 1)
                sp.dma_start(out[g * G:(g + 1) * G].rearrange("b s d -> s b d"), x_tok[g][:, :, :]
                             ).then_inc(stored, 16)
            sp.wait_ge(stored, 16 * NG)


def lay_out(i):
    def rows_of(a):
        return np.ascontiguousarray(a, dtype=np.float32)

    def col(a):
        return a.reshape(-1, 1)

    def halves(a):
        return np.concatenate([a[:128], a[128:]], axis=1)

    p = np.arange(128)
    w_src, w_mo = i["L0_xattn_W_src"].T, i["L1_attn_W_out"]
    xproj = i["L1_attn_W_xproj"]
    w_dt = np.zeros((128, 128), np.float32)
    w_dt[:RANK] = i["L1_attn_W_dt"]
    per_block = lambda w: np.transpose(w.reshape(F_E, D, F_I // 128, 128), (3, 0, 2, 1)).reshape(128, -1)
    side = lambda w: np.transpose(w, (1, 0, 2)).reshape(D, -1)
    down0 = np.concatenate([i["L0_ffn_wd_s"].reshape(128, D), i["L0_ffn_wd_r"].reshape(-1, D)])
    a = {
        "ident": np.eye(128), "head4": (p[:, None] // 8 % 4 == np.arange(4)),
        "head2": (p[:, None] // 16 % 2 == np.arange(4)), "quad_row": (p[:, None] % 32 == np.arange(4)),
        "iota": np.tile(np.arange(16), (128, 1)), "sel32": (p[:, None] % 32 == np.arange(32)),
        "pe": i["L0_attn_pe"][0, :S], "wq": i["L0_attn_wq"], "wk": i["L0_attn_wk"], "bq": col(i["L0_attn_bq"]),
        "bk": col(i["L0_attn_bk"]), "wv": i["L0_attn_wv"], "wo": i["L0_attn_wo"],
        "w_src": halves(w_src), "w_tgt": i["L0_xattn_W_tgt"].T, "w_out": halves(i["L0_xattn_W_out"].T),
        "b_srck": col(i["L0_xattn_b_src"][:128]), "b_tgt": col(i["L0_xattn_b_tgt"]),
        "b1": np.tile(i["L1_xattn_b"], (128, 1)),
        "router0": i["L0_ffn_router_w"],
        "wg0": np.concatenate([side(i["L0_ffn_wg_s"]), side(i["L0_ffn_wg_r"])], axis=1),
        "wu0": np.concatenate([side(i["L0_ffn_wu_s"]), side(i["L0_ffn_wu_r"])], axis=1),
        "wd0": np.transpose(down0.reshape(A_BLOCKS, 128, D), (1, 0, 2)).reshape(128, -1),
        "w_in": i["L1_attn_W_in"], "w_dtlow": xproj[:, :RANK], "w_bc": np.tile(xproj[:, RANK:], (1, 3)),
        "w_dt": w_dt, "w_mo": halves(w_mo), "b_dt": col(i["L1_attn_b_dt"]), "b_x": col(i["L1_attn_b_x"]),
        "b_z": col(i["L1_attn_b_z"]), "d_skip": col(i["L1_attn_D"]), "k_x": i["L1_attn_K_x"][:, 0],
        "k_z": i["L1_attn_K_z"][:, 0], "a_log": i["L1_attn_A_log"],
        "router1": i["L1_ffn_wg"].T, "w1": i["L1_ffn_w1"].reshape(-1, D).T, "w3": i["L1_ffn_w3"].reshape(-1, D).T,
        "w2": per_block(i["L1_ffn_w2"]), "fk_tok": i["mask_BxS2_fk1"].T,
        "bv": i["L0_attn_bv"], "bo": i["L0_attn_bo"], "gamma": i["L0_attn_gamma"], "beta": i["L0_attn_beta"],
        "b_srcv": i["L0_xattn_b_src"][128:], "b_out": i["L0_xattn_b_out"], "fk": i["mask_BxS2_fk1"].reshape(-1),
    }
    arrays = {f"pack_{name}": rows_of(np.concatenate([a[n] for n, _ in pack], axis=1))
              for name, pack in PACKS.items()}
    arrays["rows"] = rows_of(np.concatenate([a[n].reshape(1, -1) for n, _ in ROWS], axis=1))
    ik = i["mask_BxS2_ik0"]
    arrays["ik_tok"], arrays["ik_row"] = np.ascontiguousarray(ik.T), np.ascontiguousarray(ik.reshape(1, -1))
    arrays["x"] = rows_of(i["x"])
    ctx = i["ctx_2048"]
    arrays["ctx_t"] = rows_of(np.transpose(ctx, (2, 0, 1)).reshape(2, 128, B * S))
    arrays["v_ctx"] = rows_of(ctx[:, :, 128:])
    return arrays


def kernel(**inputs):
    import concourse.bacc as bacc
    from concourse.bass_utils import run_bass_kernel_spmd

    arrays = lay_out({name: np.asarray(a) for name, a in inputs.items()})
    nc = bacc.Bacc("TRN2", target_bir_lowering=False, num_devices=1)
    d = {name: nc.dram_tensor(f"in_{name}", a.shape, mybir.dt.from_np(a.dtype), kind="ExternalInput").ap()
         for name, a in arrays.items()}
    out = nc.dram_tensor("out", (B, S, D), mybir.dt.float32, kind="ExternalOutput").ap()
    packed = [(name, d[f"pack_{name}"]) for name in PACKS]
    decoder(nc, packed, d["rows"], d["ik_tok"], d["ik_row"], d["x"], d["ctx_t"], d["v_ctx"], out)
    result = run_bass_kernel_spmd(nc, [{f"in_{name}": a for name, a in arrays.items()}], core_ids=[0])
    return result.results[0]["out"]
```

```python
from contextlib import ExitStack

import numpy as np

import concourse.bass as bass
from concourse import mybir

STAGE = 6

B, S, D = 8, 128, 128
NG = 2
G = B // NG
T = G * S
NQ = 4
A_HEADS, X_HEADS = 16, 8
A_E, F_E = 16, 8
F_I = 256
A_BLOCKS = 5
NSTATE, RANK = 16, 8
LN_EPS = 1e-5
MASKED = 2.0 ** 100

CONST_ROW = 96

PACKS = {
    "first": [("ident", 128), ("max_row", 4), ("quad", NQ), ("fk_row", 1), ("ik_row", 1), ("b_rows", 3), ("iota", 16), ("sel32", 32),
              ("pe", 128), ("wq", 128), ("wk", 128), ("bq", 1), ("bk", 1), ("wv", 128), ("wo", 128)],
    "cross": [("w_src", 512), ("w_tgt", 128), ("w_out", 256), ("b_srck", 1), ("b_tgt", 1), ("b1", 1)],
    "moe0": [("router0", A_E), ("wg0", 128 * A_BLOCKS), ("wu0", 128 * A_BLOCKS), ("wd0", 128 * A_BLOCKS)],
    "mamba": [("w_in", 256), ("w_dtlow", RANK), ("w_bc", 96), ("w_dt", 128), ("w_mo", 256), ("b_dt", 1),
              ("b_x", 1), ("b_z", 1), ("d_skip", 1), ("k_x", 4), ("k_z", 4), ("a_log", NSTATE)],
    "moe1": [("router1", F_E), ("w1", F_E * F_I), ("w3", F_E * F_I), ("w2", F_E * F_I)],
    "masks": [("fk_tok", B)],
}
ROWS = [("bv", D), ("bo", D), ("gamma", D), ("beta", D), ("b_srcv", D), ("b_out", D), ("fk", B * S)]


def columns(pack):
    at, out = 0, {}
    for name, width in pack:
        out[name] = (at, width)
        at += width
    return out, at


def decoder(nc, packed, rows, ik_row, x, ctx_t, v_ctx, k_made, q_made, out):
    fp32, bf16, u32, i32 = mybir.dt.float32, mybir.dt.bfloat16, mybir.dt.uint32, mybir.dt.int32
    ALU = mybir.AluOpType
    ACT = mybir.ActivationFunctionType
    AX = mybir.AxisListType.X
    groups = range(NG)

    with ExitStack() as stack:
        def sb(name, shape, dt=fp32):
            return stack.enter_context(nc.sbuf_tensor(name, shape, dt))

        def sem(name):
            return stack.enter_context(nc.semaphore(name))

        pack_sb, W = {}, {}
        for pname, pack in PACKS.items():
            where, width = columns(pack)
            pack_sb[pname] = sb("pack_" + pname, [128, width])
            for name, (at, w) in where.items():
                W[name] = pack_sb[pname][:, at:at + w]
        where, rows_width = columns(ROWS)
        rows_sb = sb("rows_sb", [128, rows_width])
        R = {name: rows_sb[:, at:at + w] for name, (at, w) in where.items()}
        ident = W["ident"]
        ones_b = sb("ones_b", [128, T], bf16)
        quad_ones_b = sb("quad_ones_b", [128, NQ, 128], bf16)
        sel32_b = sb("sel32_b", [128, 32, 128], bf16)
        spread_b = sb("spread_b", [128, A_E, 32], bf16)
        half = sb("half", [128, G])
        neg_a = sb("neg_a", [128, NSTATE])
        fk_rows = sb("fk_rows", [128, B * S], bf16)
        ik_rows = sb("ik_rows", [128, B * S], bf16)
        b_parts = sb("b_parts", [128, 3], bf16)
        b_rest = sb("b_rest", [128, 1])
        b_col = sb("b_col", [128, 1])
        a_exp = sb("a_exp", [128, NSTATE])

        def per_group(name, shape, dt=fp32):
            return [sb(f"{name}{g}", shape, dt) for g in groups]

        x_tok = per_group("x_tok", [128, G, D])
        x_pe = per_group("x_pe", [128, G, D])
        x_res = per_group("x_res", [128, G, D])
        h_tok = per_group("h_tok", [128, G, D])
        x_t = per_group("x_t", [128, T])
        ctx_sb = per_group("ctx_sb", [128, 2, T])
        v_ctx_sb = per_group("v_ctx_sb", [128, G, D])
        q_t = per_group("q_t", [128, T])
        k_t = per_group("k_t", [128, T])
        q_stack = per_group("q_stack", [128, 8, T], bf16)
        k_stack = per_group("k_stack", [128, 8, T], bf16)
        v_heads_a = per_group("v_heads_a", [128, G, A_HEADS * (D // A_HEADS + 1)])
        v_heads_x = per_group("v_heads_x", [128, G, X_HEADS * (D // X_HEADS + 1)])
        neg_max = per_group("neg_max", [128, G, 128])
        neg_high = sb("neg_high", [128, NQ, 4], bf16)
        max_t = per_group("max_t", [128, 2, 4, 128], bf16)
        probs = [sb(f"probs{i}", [128, 2, 512]) for i in range(2)]
        weighed_t = sb("weighed_t", [128, T])
        rec = sb("rec", [128, A_HEADS])
        att = per_group("att", [128, G, D])
        att_t = per_group("att_t", [128, T])
        stats = sb("stats", [128, G, 6])
        mean_var = per_group("mean_var", [128, G, 2])
        var_eps = sb("var_eps", [128, G])
        rstd = per_group("rstd", [128, G])

        logits = sb("logits", [128, G, A_E])
        top8 = sb("top8", [128, G, 8])
        top_i = sb("top_i", [128, G, 8], u32)
        top_f = sb("top_f", [128, G, 2])
        picked = sb("picked", [128, 2, G, A_E])
        gate_exp = sb("gate_exp", [128, G, A_E])
        gate_sum = sb("gate_sum", [128, 4, G])
        gates = per_group("gates", [128, G, 96])
        residue = sb("residue", [96, T])
        middle = sb("middle", [96, T], bf16)
        gate_parts = per_group("gate_parts", [96, T], bf16)
        silu = [sb(f"silu{i}", [128, T]) for i in range(2)]
        hidden = [sb(f"hidden{i}", [128, T]) for i in range(3)]

        NS = 2
        CHUNKS = NSTATE // NS

        def flat(ap):
            return ap.rearrange("p a b -> p (a b)")

        halves = {name: [(flat(t[g][:, :, :]) if name != "att_t" else t[g][:, :]).bitcast(bf16)
                         .rearrange("p (n t) -> p n t", n=2) for g in groups]
                  for name, t in (("h_tok", h_tok), ("att_t", att_t), ("att", att))}
        k_parts = [[halves["h_tok"][g][:, 0, :], halves["h_tok"][g][:, 1, :], halves["att_t"][g][:, 0, :]]
                   for g in groups]
        q_parts = [[halves["att_t"][g][:, 1, :], halves["att"][g][:, 0, :], halves["att"][g][:, 1, :]]
                   for g in groups]
        product = [flat(x_res[g][:, :, :]) for g in groups]
        x_gated = [(flat(att[g][:, :, :]), att_t[g][:, :]) for g in groups]
        moe_t = [flat(x_pe[g][:, :, :]) for g in groups]
        u_t, y_t = [k_t[g][:, :] for g in groups], [q_t[g][:, :] for g in groups]
        delta, z_t = [att_t[g][:, :] for g in groups], [flat(att[g][:, :, :]) for g in groups]
        delta_u = [flat(x_pe[g][:, :, :]) for g in groups]
        y_sum = [flat(x_res[g][:, :, :]) for g in groups]
        y_pair = [flat(h_tok[g][:, :, :]) for g in groups]
        k_space, q_space = ([flat(t[g][:, :, :]).bitcast(fp32).rearrange("p (a b) -> p a b", b=T) for g in groups]
                            for t in (k_stack, q_stack))
        (dt_abs, dt_exp, dt_relu, dt_ln), (dt_one, dt_back, dt_zero, dt_div) = (
            [[t[g][:, i, :] for g in groups] for i in range(4)] for t in (k_space, q_space))
        drive, state = [k_space[g][:, 0:2, :] for g in groups], [k_space[g][:, 2:4, :] for g in groups]
        read = [[q_space[g][:, 2 * i:2 * i + 2, :] for i in range(2)] for g in groups]
        conv_x = dt_div
        conv_z_tap = [flat(max_t[g][:, :, 0:4, :].rearrange("p a b c -> p a (b c)")).bitcast(fp32) for g in groups]
        conv_z = [flat(v_heads_a[g][:, :, :])[:, 0:T] for g in groups]
        padded = [sb(f"padded_{n}", [128, G, S + 3]) for n in "xz"]
        dt_low = sb("dt_low", [RANK, T])
        bc_parts = per_group("bc_parts", [96, T], bf16)
        decay = [sb(f"decay{i}", [128, NS, T]) for i in range(2)]
        ik_row_sb = flat(decay[0][:, :, :]).bitcast(i32)

        psum = stack.enter_context(nc.psum_tensor("psum", [128, 8, 512], fp32))
        slot = [psum[:, i, :] for i in range(4)] + [psum[:, 4:6, :], psum[:, 6:8, :]]
        full = [sem(f"psum_full{i}") for i in range(6)]
        filled = [0] * 6
        released = [None] * 6
        nth = {}

        loaded = {p: sem("loaded_" + p) for p in [*PACKS, "rows", "ik"]}
        x_loaded = [sem(f"x_loaded{g}") for g in groups]
        ctx_loaded = [sem(f"ctx_loaded{g}") for g in groups]
        pool_consts, vector_consts, scalar_consts = sem("pool_consts"), sem("vector_consts"), sem("scalar_consts")
        x_pe_ready, res_ready = sem("x_pe_ready"), sem("res_ready")
        x_t_ready, x_tok_ready, sum_ready, var_ready, rstd_ready = (
            [sem(f"{n}{g}") for g in groups] for n in ("x_t_ready", "x_tok_ready", "sum_ready", "var_ready", "rstd_ready"))
        k_parts_ready, q_parts_ready = sem("k_parts_ready"), sem("q_parts_ready")
        k_parts_saved, q_parts_saved, stacks_ready = (
            [sem(f"{n}{g}") for g in groups] for n in ("k_parts_saved", "q_parts_saved", "stacks_ready"))
        v_ready, ik_rows_ready = sem("v_ready"), sem("ik_rows_ready")
        max_ready, lows_ready, max_t_ready = sem("max_ready"), sem("lows_ready"), sem("max_t_ready")
        exp_ready, weighed, weighed_t_ready = sem("exp_ready"), sem("weighed"), sem("weighed_t_ready")
        att_ready, att_t_ready = sem("att_ready"), sem("att_t_ready")
        logits_ready, gate_shift_ready, gate_exp_ready = sem("logits_ready"), sem("gate_shift_ready"), sem("gate_exp_ready")
        gates_ready, gate_parts_ready = sem("gates_ready"), sem("gate_parts_ready")
        x_gated_ready, silu_ready, hidden_ready = sem("x_gated_ready"), sem("silu_ready"), sem("hidden_ready")
        hidden_used, moe_t_ready = sem("hidden_used"), sem("moe_t_ready")
        padded_ready, conv_x_ready, conv_z_ready = sem("padded_ready"), sem("conv_x_ready"), sem("conv_z_ready")
        u_ready, z_ready, dt_low_ready = sem("u_ready"), sem("z_ready"), sem("dt_low_ready")
        bc_parts_ready, dt_exp_ready, dt_one_ready = sem("bc_parts_ready"), sem("dt_exp_ready"), sem("dt_one_ready")
        dt_ln_ready, delta_ready = sem("dt_ln_ready"), sem("delta_ready")
        neg_a_ready = sem("neg_a_ready")
        decay_exp_ready, decay_ready, scanned = sem("decay_exp_ready"), sem("decay_ready"), sem("scanned")
        bc_used, y_sum_ready, y_ready = sem("bc_used"), sem("y_sum_ready"), sem("y_ready")
        vector_step, scalar_step, pool_step = sem("vector_step"), sem("scalar_step"), sem("pool_step")
        stored = sem("stored")

        VECTOR_CONSTS, POOL_CONSTS = 5, 2 + 5 * NG

        block = stack.enter_context(nc.Block())

        ORDER = [(layer, g) for layer in range(1, STAGE + 1) for g in groups]
        FORM = {1: (A_HEADS // 4, D // A_HEADS), 2: (X_HEADS // 4, D // X_HEADS), 5: (X_HEADS // 4, D // X_HEADS)}
        MOE = {3: (A_E, A_BLOCKS), 6: (F_E, F_E * F_I // 128)}

        def before(layer, g, per):
            return sum(per(*o) for o in ORDER[:ORDER.index((layer, g))])

        def att_rank(layer, g):
            return before(layer, g, lambda l, _: l in FORM)

        def proj_rank(layer, g):
            return before(layer, g, lambda l, _: l in (1, 2))

        def moe_rank(layer, g):
            return before(layer, g, lambda l, _: l in MOE)

        def max_rank(layer, g):
            return before(layer, g, lambda l, _: FORM[l][0] * G if l in FORM else 0)

        def unit_rank(layer, g):
            return before(layer, g, lambda l, _: FORM[l][0] // 2 * G if l in FORM else 0)

        def stacking(layer):
            return 12 if layer == 1 else 8

        def att_nth(layer):
            return sum(l in FORM for l in range(1, layer + 1))

        def stack_loads(layer):
            return sum(stacking(l) for l in range(1, layer + 1) if l in FORM)

        def weighed_slot(layer, g):
            return 2 if (layer, g) == (5, 1) else 3

        def head_at(layer, quad, j):
            return 8 * (quad // 2) + 2 * j + quad % 2 if layer == 1 else 4 * quad + j

        def head_of(stack_, layer, h, b):
            if layer == 1:
                return stack_[64 * (h % 2):64 * (h % 2) + 6 * 8, h // 2, b * S:(b + 1) * S]
            return stack_[0:CONST_ROW + 4, h, b * S:(b + 1) * S]

        def block_rank(layer, g):
            return before(layer, g, lambda l, _: MOE[l][1] if l in MOE else 0)

        def norm_rank(layer, second=False):
            return layer - 1 + (layer > 1) + second

        def v_heads(layer, g):
            return v_heads_a[g] if layer == 1 else v_heads_x[g]

        def steps_of(layer, g):
            if layer in FORM:
                return [("attend", layer, g, b) for b in range(G)]
            if layer in MOE:
                return [("block", layer, g, k) for k in range(MOE[layer][1])]
            return [("chunk", layer, g, c) for c in range(CHUNKS)]

        def one(step, layer, g):
            return [(step, layer, g, 0)]

        def merge(a, b):
            at = [((i + 0.5) / len(a), 0, i, x) for i, x in enumerate(a)] + [
                ((i + 0.5) / len(b), 1, i, x) for i, x in enumerate(b)]
            return [x for _, _, _, x in sorted(at, key=lambda t: t[:3])]

        def tucked(steps, *extras):
            out_ = []
            for i, step in enumerate(steps):
                out_.append(step)
                for place, extra in extras:
                    if place in (i + 1, step):
                        out_ += extra
            return out_

        PLAN = one("prepare", 1, 0) + one("prepare", 1, 1) + steps_of(1, 0)
        PLAN += tucked(steps_of(1, 1), (1, one("finish", 1, 0)), (2, one("prepare", 2, 0)))
        PLAN += tucked(steps_of(2, 0), (1, one("finish", 1, 1)), (2, one("prepare", 2, 1)))
        PLAN += tucked(steps_of(2, 1), (1, one("finish", 2, 0)), (2, one("route", 3, 0)), (4, one("gate_rows", 3, 0)))
        PLAN += tucked(steps_of(3, 0), (1, one("finish", 2, 1)), (2, one("route", 3, 1)), (4, one("gate_rows", 3, 1)))
        PLAN += one("finish", 3, 0) + one("mamba_in", 4, 0) + one("mamba_dt", 4, 0)
        PLAN += tucked(merge(steps_of(3, 1), steps_of(4, 0)[:6]), (11, one("finish", 3, 1) + one("mamba_in", 4, 1)))
        PLAN += tucked(steps_of(4, 0)[6:], (1, one("mamba_dt", 4, 1))) + one("finish", 4, 0)
        PLAN += steps_of(4, 1)[:1] + one("prepare", 5, 0) + steps_of(4, 1)[1:3] + merge(steps_of(5, 0), steps_of(4, 1)[3:])
        PLAN += one("finish", 5, 0) + one("route", 6, 0) + one("finish", 4, 1) + one("gate_rows", 6, 0)
        PLAN += tucked(merge(steps_of(6, 0)[:2], one("prepare", 5, 1)) + merge(steps_of(6, 0)[2:], steps_of(5, 1)),
                       (("attend", 5, 1, G - 1), one("finish", 5, 1)))
        PLAN += one("route", 6, 1) + one("gate_rows", 6, 1)
        PLAN += tucked(steps_of(6, 1), (1, one("finish", 6, 0))) + one("finish", 6, 1)
        PLAN = [step for step in PLAN if step[1] <= STAGE]

        @block.tensor
        def _(pe):
            mm = nc.tensor.matmul

            def claim(s, label, sem_, value):
                if released[s]:
                    pe.wait_ge(*released[s])
                released[s] = (sem_, value)
                if label:
                    filled[s] += 1
                    nth[label] = filled[s]
                return slot[s]

            def to_t(src, dst):
                for b in range(G):
                    last = nc.tensor.transpose(dst[0:src.shape[2], b * S:(b + 1) * S], src[:, b, :], ident)
                return last

            def by_token(dst, *pairs):
                for b in range(G):
                    for n, (left_t, right) in enumerate(pairs):
                        last = mm(dst[:, b * S:(b + 1) * S], left_t[:, b * S:(b + 1) * S], right,
                                  start=n == 0, stop=n == len(pairs) - 1)
                return last

            def x_to_t(layer, g):
                pe.wait_ge(x_tok_ready[g], layer - 1)
                dst = claim(2, ("x_t", layer, g), x_t_ready[g], layer)
                to_t(x_tok[g], dst).then_inc(full[2], 1)

            def scores(layer, g, b):
                for quad in range(FORM[layer][0]):
                    s = quad % 2
                    dst = claim(s, ("scores", layer, g, b, quad), max_ready,
                                max_rank(layer, g) + FORM[layer][0] * b + quad + 1)
                    for j in range(4):
                        h = head_at(layer, quad, j)
                        last = mm(dst[:, j * 128:(j + 1) * 128], head_of(q_stack[g], layer, h, b),
                                  head_of(k_stack[g], layer, h, b), start=True, stop=True)
                    last.then_inc(full[s], 1)

            def maxima_to_t(layer, g, b):
                n = att_rank(layer, g) * G + b + 1
                pe.wait_ge(lows_ready, n)
                dst = claim(2, ("max_t", layer, g, b), max_t_ready, n)
                nc.tensor.transpose(dst[:, 0:S], neg_max[g][:, b, :], ident).then_inc(full[2], 1)

            def weigh(layer, g, u):
                quads, hd = FORM[layer]
                units = quads // 2
                b = u // units
                if u % units == 0:
                    claim(weighed_slot(layer, g), None, weighed_t_ready, att_rank(layer, g) * G + b + 1)
                pe.wait_ge(exp_ready, unit_rank(layer, g) + u + 1)
                for i in range(8):
                    h = head_at(layer, 2 * (u % units) + i // 4, i % 4)
                    cols = slice(h * (hd + 1), (h + 1) * (hd + 1))
                    last = mm(slot[weighed_slot(layer, g)][32 * (h % 4):32 * (h % 4) + hd + 1,
                                                           h // 4 * 128:(h // 4 + 1) * 128],
                              v_heads(layer, g)[:, b, cols], probs[u % 2][:, i // 4, i % 4 * 128:(i % 4 + 1) * 128],
                              start=True, stop=True)
                last.then_inc(weighed, 1)

            def weighed_to_tok(layer, g, b):
                n = att_rank(layer, g) * G + b + 1
                pe.wait_ge(weighed_t_ready, n)
                dst = claim(2, ("weighed", layer, g, b), att_ready, n)
                for c in range(FORM[layer][0]):
                    last = nc.tensor.transpose(dst[:, c * 128:(c + 1) * 128], weighed_t[:, c * 128:(c + 1) * 128], ident)
                last.then_inc(full[2], 1)

            def attend(layer, g, b):
                units = FORM[layer][0] // 2
                if b == 0:
                    pe.wait_ge(stacks_ready[g], 16 * stack_loads(layer))
                    scores(layer, g, 0)
                    scores(layer, g, 1)
                    maxima_to_t(layer, g, 0)
                if b + 1 < G:
                    maxima_to_t(layer, g, b + 1)
                for u in range(units * b, units * (b + 1)):
                    s = 4 + u % 2
                    pe.wait_ge(max_t_ready, att_rank(layer, g) * G + b + 1)
                    dst = claim(s, ("scores_t", layer, g, u), exp_ready, unit_rank(layer, g) + u + 1)
                    for i in range(2):
                        quad = 2 * (u % units) + i
                        mm(dst[:, i, :], quad_ones_b[:, quad, :],
                           max_t[g][:, b % 2, :, :].rearrange("p a b -> p (a b)"), start=True, stop=False)
                        for j in range(4):
                            h = head_at(layer, quad, j)
                            last = mm(dst[:, i, j * 128:(j + 1) * 128], head_of(k_stack[g], layer, h, b),
                                      head_of(q_stack[g], layer, h, b), start=False, stop=j == 3)
                    last.then_inc(full[s], 1)
                    if u == 0:
                        pe.wait_ge(v_ready, att_rank(layer, g) + 1)
                    else:
                        weigh(layer, g, u - 1)
                if b + 2 < G:
                    scores(layer, g, b + 2)
                if b:
                    weighed_to_tok(layer, g, b - 1)
                if b == G - 1:
                    weigh(layer, g, units * G - 1)

            def att_to_t(layer, g):
                weighed_to_tok(layer, g, G - 1)
                p = proj_rank(layer, g)
                pe.wait_ge(att_ready, (att_rank(layer, g) + 1) * G)
                to_t(att[g], claim(0, ("att_t", layer, g), att_t_ready, p + 1)).then_inc(full[0], 1)
                pe.wait_ge(att_t_ready, p + 1)

            def prepare1(g):
                pe.wait_ge(x_pe_ready, g + 1)
                to_t(x_pe[g], claim(2, ("x_t", 1, g), x_t_ready[g], 1)).then_inc(full[2], 1)
                pe.wait_ge(x_t_ready[g], 1)
                a = att_rank(1, g)
                if g == 0:
                    to_t(x_pe[g], slot[3])
                mm(claim(1, ("wk", 1, g), k_parts_ready, a + 1), W["wk"], x_t[g][:, :],
                   start=True, stop=True).then_inc(full[1], 1)
                mm(claim(0, ("wq", 1, g), q_parts_ready, a + 1), W["wq"], x_t[g][:, :],
                   start=True, stop=True).then_inc(full[0], 1)
                by_token(claim(2, ("wv", 1, g), v_ready, a + 1), (x_t[g], W["wv"])).then_inc(full[2], 1)

            def finish1(g):
                att_to_t(1, g)
                by_token(claim(1, ("sum", 1, g), sum_ready[g], 1), (att_t[g], W["wo"])).then_inc(full[1], 1)

            def prepare2(g):
                a = att_rank(2, g)
                if g == 0:
                    pe.wait_ge(loaded["cross"], 16)
                pe.wait_ge(ctx_loaded[g], 32)
                dst = claim(0, ("wk", 2, g), k_parts_ready, a + 1)
                for c in range(2):
                    last = mm(dst, W["w_src"][:, c * 256:c * 256 + 128], ctx_sb[g][:, c, :],
                              start=c == 0, stop=c == 1)
                last.then_inc(full[0], 1)
                by_token(claim(1, ("wv", 2, g), v_ready, a + 1),
                         *((ctx_sb[g][:, c, :], W["w_src"][:, c * 256 + 128:c * 256 + 256]) for c in range(2))
                         ).then_inc(full[1], 1)
                x_to_t(2, g)
                pe.wait_ge(x_t_ready[g], 2)
                mm(claim(0, ("wq", 2, g), q_parts_ready, a + 1), W["w_tgt"], x_t[g][:, :],
                   start=True, stop=True).then_inc(full[0], 1)

            def finish2(g):
                att_to_t(2, g)
                by_token(claim(1, ("sum", 2, g), sum_ready[g], 2),
                         (x_t[g], W["w_out"][:, 0:128]), (att_t[g], W["w_out"][:, 128:256])).then_inc(full[1], 1)

            def gate_rows(layer, g):
                m = moe_rank(layer, g)
                pe.wait_ge(gates_ready, m + 1)
                to_t(gates[g], claim(1, ("gates_t", layer, g), gate_parts_ready, m + 1)
                     ).then_inc(full[1], 1)

            def route(layer, g):
                experts = MOE[layer][0]
                name = "router0" if layer == 3 else "router1"
                if g == 0:
                    pe.wait_ge(loaded["moe0" if layer == 3 else "moe1"], 16)
                x_to_t(layer, g)
                pe.wait_ge(x_t_ready[g], layer)
                dst = claim(0, ("logits", layer, g), logits_ready, moe_rank(layer, g) + 1)
                for b in range(G):
                    last = mm(dst[:, b * experts:(b + 1) * experts], x_t[g][:, b * S:(b + 1) * S], W[name],
                              start=True, stop=True)
                last.then_inc(full[0], 1)

            def down(layer, g, k, w):
                blocks = MOE[layer][1]
                if k == 0:
                    claim(3, None, moe_t_ready, moe_rank(layer, g) + 1)
                pe.wait_ge(hidden_ready, block_rank(layer, g) + k + 1)
                mm(slot[3], w[:, k * 128:(k + 1) * 128], hidden[k % 3][:, :],
                   start=k == 0, stop=k == blocks - 1).then_inc(hidden_used, 1)

            def moe_to_tok(layer, g):
                pe.wait_ge(moe_t_ready, moe_rank(layer, g) + 1)
                dst = claim(0, ("sum", layer, g), sum_ready[g], layer)
                for b in range(G):
                    last = nc.tensor.transpose(dst[:, b * S:(b + 1) * S], moe_t[g][:, b * S:(b + 1) * S], ident)
                last.then_inc(full[0], 1)

            def block3(g, k):
                first, s = block_rank(3, g), 4 + k % 2
                dst = claim(s, ("up", 3, g, k), hidden_ready, first + k + 1)
                for i, name in enumerate(("wg0", "wu0")):
                    last = mm(dst[:, i, :], W[name][:, k * 128:(k + 1) * 128], x_t[g][:, :], start=True, stop=True)
                last.then_inc(full[s], 1)
                if k == 0:
                    pe.wait_ge(gate_parts_ready, moe_rank(3, g) + 1)
                else:
                    mm(claim(2, ("gate", 3, g, k), hidden_ready, first + k + 1),
                       spread_b[0:96, 4 * (k - 1):4 * k, :].rearrange("p e m -> p (e m)"), gate_parts[g][:, :],
                       start=True, stop=True).then_inc(full[2], 1)
                    down(3, g, k - 1, W["wd0"])
                if k == A_BLOCKS - 1:
                    down(3, g, k, W["wd0"])

            def block6(g, k):
                first, blocks, per = block_rank(6, g), MOE[6][1], F_I // 128
                e, s = k // per, 4 + k % 2

                def gate(e):
                    s = e % 2
                    mm(claim(s, ("gate", 6, g, e), x_gated_ready, g * F_E + e + 1), sel32_b[0:96, e, :],
                       gate_parts[g][:, :], start=True, stop=True).then_inc(full[s], 1)

                dst = claim(s, ("up", 6, g, k), hidden_ready, first + k + 1)
                mm(dst[:, 0, :], W["w1"][:, k * 128:(k + 1) * 128], x_t[g][:, :], start=True, stop=True)
                if k == 0:
                    pe.wait_ge(gate_parts_ready, moe_rank(6, g) + 1)
                    gate(0)
                if k % per == 0:
                    if e + 1 < F_E:
                        gate(e + 1)
                    pe.wait_ge(x_gated_ready, g * F_E + e + 1)
                mm(dst[:, 1, :], W["w3"][:, k * 128:(k + 1) * 128], x_gated[g][e % 2],
                   start=True, stop=True).then_inc(full[s], 1)
                if k:
                    down(6, g, k - 1, W["w2"])
                if k == blocks - 1:
                    down(6, g, k, W["w2"])

            def mamba_in(g):
                if g == 0:
                    pe.wait_ge(loaded["mamba"], 16)
                x_to_t(4, g)
                pe.wait_ge(x_t_ready[g], 4)
                for s in range(2):
                    mm(claim(s, ("in", g, s), padded_ready, 2 * g + s + 1), W["w_in"][:, s * 128:(s + 1) * 128],
                       x_t[g][:, :], start=True, stop=True).then_inc(full[s], 1)

            def mamba_dt(g):
                pe.wait_ge(u_ready, g + 1)
                mm(claim(2, ("dt_low", g), dt_low_ready, g + 1)[0:RANK, :], W["w_dtlow"], u_t[g],
                   start=True, stop=True).then_inc(full[2], 1)
                mm(claim(1, ("bc", g), bc_parts_ready, g + 1)[0:96, :], W["w_bc"], u_t[g],
                   start=True, stop=True).then_inc(full[1], 1)
                pe.wait_ge(dt_low_ready, g + 1)
                mm(claim(0, ("dt", g), dt_exp_ready, g + 1), W["w_dt"][0:RANK, :], dt_low[:, :],
                   start=True, stop=True).then_inc(full[0], 1)

            def chunk(g, c):
                if c == 0:
                    pe.wait_ge(bc_parts_ready, g + 1)
                for kind in range(2):
                    unit, s = 2 * c + kind, 4 + kind
                    dst = claim(s, ("bc", g, unit), bc_used, g * NSTATE + unit + 1)
                    for i in range(NS):
                        last = mm(dst[:, i, :], sel32_b[0:96, kind * NSTATE + c * NS + i, :], bc_parts[g][:, :],
                                  start=True, stop=True)
                    last.then_inc(full[s], 1)

            def finish4(g):
                pe.wait_ge(y_ready, g + 1)
                pe.wait_ge(z_ready, g + 1)
                by_token(claim(0, ("sum", 4, g), sum_ready[g], 4),
                         (y_t[g], W["w_mo"][:, 0:128]), (z_t[g], W["w_mo"][:, 128:256])).then_inc(full[0], 1)

            pe.wait_ge(loaded["first"], 16)
            pe.wait_ge(pool_consts, POOL_CONSTS)
            pe.wait_ge(vector_consts, VECTOR_CONSTS)
            for step, layer, g, n in PLAN:
                if step == "prepare":
                    {1: prepare1, 2: prepare2, 5: lambda g: x_to_t(5, g)}[layer](g)
                elif step == "attend":
                    attend(layer, g, n)
                elif step == "route":
                    route(layer, g)
                elif step == "gate_rows":
                    gate_rows(layer, g)
                elif step == "block":
                    (block3 if layer == 3 else block6)(g, n)
                elif step == "mamba_in":
                    mamba_in(g)
                elif step == "mamba_dt":
                    mamba_dt(g)
                elif step == "chunk":
                    chunk(g, n)
                elif layer in MOE:
                    moe_to_tok(layer, g)
                elif layer == 5:
                    weighed_to_tok(5, g, G - 1)
                else:
                    {1: finish1, 2: finish2, 4: finish4}[layer](g)

        @block.vector
        def _(dve):
            v = nc.vector
            steps = [0]

            def then(instruction):
                steps[0] += 1
                instruction.then_inc(vector_step, 1)
                dve.wait_ge(vector_step, steps[0])

            def constants():
                dve.wait_ge(loaded["first"], 16)
                v.tensor_copy(quad_ones_b[:, :, :], W["quad"].unsqueeze(2).broadcast_to([128, NQ, 128])
                              ).then_inc(vector_consts, 1)
                v.tensor_copy(sel32_b[:, :, :], W["sel32"].unsqueeze(2).broadcast_to([128, 32, 128])
                              ).then_inc(vector_consts, 1)
                v.tensor_copy(spread_b[:, :, :], W["sel32"][:, 0:A_E].unsqueeze(2).broadcast_to([128, A_E, 32])
                              ).then_inc(vector_consts, 1)
                dve.wait_ge(loaded["rows"], 16)
                dve.wait_ge(loaded["ik"], 16)
                v.tensor_scalar(fk_rows[:, :], R["fk"], 0.0, W["fk_row"], ALU.is_equal, ALU.mult
                                ).then_inc(vector_consts, 1)
                v.tensor_scalar(ik_rows[:, :], ik_row_sb, -1.0, W["ik_row"], ALU.add, ALU.mult
                                ).then_inc(vector_consts, 1)

            def cross_constants():
                dve.wait_ge(vector_consts, VECTOR_CONSTS)
                dve.wait_ge(loaded["cross"], 16)
                then(v.tensor_copy(b_parts[:, 0:1], W["b1"]))
                then(v.tensor_tensor(b_rest[:, :], W["b1"], b_parts[:, 0:1], ALU.subtract))
                then(v.tensor_copy(b_parts[:, 1:2], b_rest[:, :]))
                then(v.tensor_tensor(b_parts[:, 2:3], b_rest[:, :], b_parts[:, 1:2], ALU.subtract))
                then(v.tensor_tensor(b_parts[:, :], b_parts[:, :], W["b_rows"], ALU.mult))
                then(v.tensor_reduce(b_col[:, :], b_parts[:, :], AX, ALU.add))
                v.tensor_scalar(ik_rows[:, :], ik_rows[:, :], b_col[:, :], None, ALU.add).then_inc(ik_rows_ready, 1)

            def split_parts(src, scale, rest, dst):
                high, middle_, low = dst
                if scale == 1.0:
                    then(v.tensor_copy(high, src))
                    then(v.tensor_tensor(rest, src, high, ALU.subtract))
                else:
                    then(v.tensor_scalar(high, src, scale, None, ALU.mult))
                    then(v.scalar_tensor_tensor(rest, src, scale, high, ALU.mult, ALU.subtract))
                then(v.tensor_copy(middle_, rest))
                return v.tensor_tensor(low, rest, middle_, ALU.subtract)

            def prepare1(g):
                dve.wait_ge(x_loaded[g], 16)
                v.tensor_tensor(x_pe[g][:, :, :], x_tok[g][:, :, :],
                                W["pe"].unsqueeze(1).broadcast_to([128, G, D]), ALU.add).then_inc(x_pe_ready, 1)
                dve.wait_ge(full[1], nth["wk", 1, g])
                then(v.tensor_scalar(k_t[g][:, :], slot[1], W["bk"], None, ALU.add))
                split_parts(k_t[g][:, :], 1.0, k_t[g][:, :], k_parts[g]).then_inc(k_parts_ready, 1)
                dve.wait_ge(full[0], nth["wq", 1, g])
                then(v.tensor_scalar(q_t[g][:, :], slot[0], W["bq"], float(D // A_HEADS) ** -0.5, ALU.add, ALU.mult))
                split_parts(q_t[g][:, :], 1.0, q_t[g][:, :], q_parts[g]).then_inc(q_parts_ready, 1)
                dve.wait_ge(full[2], nth["wv", 1, g])
                hd = D // A_HEADS
                v.tensor_tensor(v_heads_a[g][:, :, :].rearrange("p b (h e) -> p b h e", e=hd + 1)[:, :, :, 0:hd],
                                slot[2].rearrange("p (b h e) -> p b h e", b=G, e=hd),
                                R["bv"].rearrange("p (h e) -> p h e", e=hd).unsqueeze(1)
                                .broadcast_to([128, G, A_HEADS, hd]), ALU.add).then_inc(v_ready, 1)

            def values_x(g):
                hd = D // X_HEADS
                return (v_heads_x[g][:, :, :].rearrange("p b (h e) -> p b h e", e=hd + 1)[:, :, :, 0:hd], hd)

            def prepare2(g):
                if g == 0:
                    cross_constants()
                dve.wait_ge(x_tok_ready[g], 1)
                at = slice(g * T, (g + 1) * T)
                dve.wait_ge(full[0], nth["wk", 2, g])
                then(v.scalar_tensor_tensor(k_t[g][:, :], slot[0], W["b_srck"], R["fk"][:, at], ALU.add, ALU.mult))
                split_parts(k_t[g][:, :], 1.0, k_t[g][:, :], k_parts[g]).then_inc(k_parts_ready, 1)
                dve.wait_ge(full[1], nth["wv", 2, g])
                then(v.tensor_tensor(x_pe[g][:, :, :], slot[1].rearrange("p (b e) -> p b e", b=G),
                                     R["b_srcv"].unsqueeze(1).broadcast_to([128, G, D]), ALU.add))
                if g == 0:
                    dve.wait_ge(loaded["masks"], 16)
                dst, hd = values_x(g)
                v.tensor_tensor(dst, x_pe[g][:, :, :].rearrange("p b (h e) -> p b h e", e=hd),
                                W["fk_tok"][:, g * G:(g + 1) * G].unsqueeze(2).unsqueeze(3)
                                .broadcast_to([128, G, X_HEADS, hd]), ALU.mult).then_inc(v_ready, 1)
                dve.wait_ge(full[0], nth["wq", 2, g])
                then(v.scalar_tensor_tensor(q_t[g][:, :], slot[0], W["b_tgt"], R["fk"][:, at],
                                            ALU.add, ALU.mult))
                split_parts(q_t[g][:, :], float(D // X_HEADS) ** -0.5, q_t[g][:, :], q_parts[g]
                            ).then_inc(q_parts_ready, 1)

            def prepare5(g):
                dve.wait_ge(ctx_loaded[g], 32)
                dve.wait_ge(x_tok_ready[g], 4)
                split_parts(ctx_sb[g][:, 0, :], 1.0, k_t[g][:, :], k_parts[g]).then_inc(k_parts_ready, 1)
                dst, hd = values_x(g)
                v.tensor_copy(dst, v_ctx_sb[g][:, :, :].rearrange("p b (h e) -> p b h e", e=hd)).then_inc(v_ready, 1)
                dve.wait_ge(x_t_ready[g], 5)
                split_parts(x_t[g][:, :], float(D // X_HEADS) ** -0.5, q_t[g][:, :], q_parts[g]
                            ).then_inc(q_parts_ready, 1)

            def maxima(layer, g, b):
                quads = FORM[layer][0]
                by_quad = neg_max[g][:, b, :].rearrange("p (q r) -> p q r", q=NQ)[:, 0:quads, :]
                for quad in range(quads):
                    s = quad % 2
                    dve.wait_ge(full[s], nth["scores", layer, g, b, quad])
                    v.tensor_reduce(by_quad[:, quad, 0:4], slot[s].rearrange("p (j k) -> p j k", j=4), AX,
                                    ALU.max, negate=True).then_inc(max_ready, 1)
                dve.wait_ge(max_ready, max_rank(layer, g) + quads * (b + 1))
                then(v.tensor_copy(neg_high[:, 0:quads, :], by_quad[:, :, 0:4]))
                v.tensor_tensor(by_quad[:, :, 4:8], by_quad[:, :, 0:4], neg_high[:, 0:quads, :],
                                ALU.subtract).then_inc(lows_ready, 1)
                dve.wait_ge(lows_ready, att_rank(layer, g) * G + b + 1)

            def maxima_to_rows(layer, g, b):
                dve.wait_ge(full[2], nth["max_t", layer, g, b])
                if b >= 2:
                    u = FORM[layer][0] // 2 * (b - 1) - 1
                    dve.wait_ge(full[4 + u % 2], nth["scores_t", layer, g, u])
                v.tensor_tensor(max_t[g][:, b % 2, :, :], slot[2][:, 0:S].unsqueeze(1).broadcast_to([128, 4, S]),
                                W["max_row"].unsqueeze(2).broadcast_to([128, 4, S]), ALU.mult
                                ).then_inc(max_t_ready, 1)

            def normalize(layer, g, b):
                quads, hd = FORM[layer]
                heads = 4 * quads
                dve.wait_ge(full[2], nth["weighed", layer, g, b])
                sums = slot[2][:, 0:heads * 32].rearrange("p (h e) -> p h e", e=32)
                then(v.reciprocal(rec[:, 0:heads].unsqueeze(2), sums[:, :, hd:hd + 1]))
                v.tensor_tensor(att[g][:, b, :].rearrange("p (h e) -> p h e", e=hd), sums[:, :, 0:hd],
                                rec[:, 0:heads].unsqueeze(2).broadcast_to([128, heads, hd]),
                                ALU.mult).then_inc(att_ready, 1)

            def attend(layer, g, b):
                if b == 0:
                    maxima(layer, g, 0)
                    maxima(layer, g, 1)
                    maxima_to_rows(layer, g, 0)
                if b + 1 < G:
                    maxima_to_rows(layer, g, b + 1)
                if b + 2 < G:
                    maxima(layer, g, b + 2)
                if b:
                    normalize(layer, g, b - 1)

            def norm(layer, g, src, dst, second=False):
                for b in range(G):
                    last = v.bn_stats(stats[:, b, :], src[:, b, :])
                then(last)
                for b in range(G):
                    last = v.bn_aggr(mean_var[g][:, b, :], stats[:, b, :])
                last.then_inc(var_ready[g], 1)
                dve.wait_ge(rstd_ready[g], norm_rank(layer, second) + 1)
                for b in range(G):
                    last = v.tensor_scalar(dst[:, b, :], src[:, b, :], mean_var[g][:, b, 0:1],
                                           rstd[g][:, b:b + 1], ALU.subtract, ALU.mult)
                return last

            def add_residual(layer, g, s, residual):
                dve.wait_ge(full[s], nth["sum", layer, g])
                v.tensor_tensor(h_tok[g][:, :, :], slot[s].rearrange("p (b e) -> p b e", b=G), residual[:, :, :],
                                ALU.add).then_inc(sum_ready[g], 1)
                dve.wait_ge(sum_ready[g], layer)

            def finish1(g):
                normalize(1, g, G - 1)
                dve.wait_ge(res_ready, proj_rank(1, g) + 1)
                add_residual(1, g, 1, x_res[g])
                then(norm(1, g, h_tok[g], h_tok[g]))
                wide = [128, G, D]
                then(v.tensor_tensor(h_tok[g][:, :, :], h_tok[g][:, :, :],
                                     R["gamma"].unsqueeze(1).broadcast_to(wide), ALU.mult))
                then(v.tensor_tensor(h_tok[g][:, :, :], h_tok[g][:, :, :],
                                     R["beta"].unsqueeze(1).broadcast_to(wide), ALU.add))
                then(v.tensor_tensor(h_tok[g][:, :, :], h_tok[g][:, :, :], x_tok[g][:, :, :], ALU.add))
                norm(1, g, h_tok[g], x_tok[g], second=True).then_inc(x_tok_ready[g], 1)

            def finish2(g):
                normalize(2, g, G - 1)
                dve.wait_ge(res_ready, proj_rank(2, g) + 1)
                add_residual(2, g, 1, x_res[g])
                norm(2, g, h_tok[g], x_tok[g]).then_inc(x_tok_ready[g], 1)

            def finish5(g):
                normalize(5, g, G - 1)
                dve.wait_ge(att_ready, (att_rank(5, g) + 1) * G)
                v.tensor_tensor(h_tok[g][:, :, :], att[g][:, :, :], x_tok[g][:, :, :], ALU.add).then_inc(sum_ready[g], 1)
                dve.wait_ge(sum_ready[g], 5)
                norm(5, g, h_tok[g], x_tok[g]).then_inc(x_tok_ready[g], 1)

            def split(s, label, dst, done):
                dve.wait_ge(full[s], nth[label])
                x96 = slot[s][0:96, :]
                then(v.tensor_copy(dst[0:96, :], x96))
                then(v.tensor_tensor(residue[0:96, :], x96, dst[0:96, :], ALU.subtract))
                v.tensor_copy(dst[32:64, :], residue[32:64, :])
                then(v.tensor_copy(middle[64:96, :], residue[64:96, :]))
                v.tensor_tensor(dst[64:96, :], residue[64:96, :], middle[64:96, :], ALU.subtract).then_inc(done, 1)

            def route(layer, g):
                experts = MOE[layer][0]
                m = moe_rank(layer, g)
                lg = logits[:, :, 0:experts]
                full_shape = [128, G, experts]
                dve.wait_ge(full[0], nth["logits", layer, g])
                v.tensor_copy(lg, slot[0][:, 0:G * experts].rearrange("p (b e) -> p b e", b=G)
                              ).then_inc(logits_ready, 1)
                dve.wait_ge(logits_ready, m + 1)
                for b in range(G):
                    last = v.max(top8[:, b, :], logits[:, b, 0:experts])
                then(last)
                v.tensor_tensor(gate_exp[:, :, 0:experts], lg, top8[:, :, 0:1].broadcast_to(full_shape),
                                ALU.subtract).then_inc(gate_shift_ready, 1)
                for b in range(G):
                    last = v.max_index(top_i[:, b, :], top8[:, b, :], logits[:, b, 0:experts])
                then(last)
                then(v.tensor_copy(top_f[:, :, :], top_i[:, :, 0:2]))
                for i in range(2):
                    last = v.tensor_tensor(picked[:, i, :, 0:experts],
                                           W["iota"][:, 0:experts].unsqueeze(1).broadcast_to(full_shape),
                                           top_f[:, :, i:i + 1].broadcast_to(full_shape), ALU.is_equal)
                then(last)
                then(v.tensor_tensor(picked[:, 0, :, 0:experts], picked[:, 0, :, 0:experts],
                                     picked[:, 1, :, 0:experts], ALU.add))
                dve.wait_ge(gate_exp_ready, m + 1)
                ge = gate_exp[:, :, 0:experts]
                then(v.tensor_reduce(gate_sum[:, 0, :], ge, AX, ALU.add))
                then(v.reciprocal(gate_sum[:, 1, :], gate_sum[:, 0, :]))
                then(v.tensor_tensor(lg, ge, gate_sum[:, 1, :].unsqueeze(2).broadcast_to(full_shape), ALU.mult))
                then(v.tensor_tensor(lg, lg, picked[:, 0, :, 0:experts], ALU.mult))
                then(v.tensor_reduce(gate_sum[:, 2, :], lg, AX, ALU.add))
                if layer == 3:
                    then(v.tensor_scalar(gate_sum[:, 2, :], gate_sum[:, 2, :], 1e-9, None, ALU.add))
                then(v.reciprocal(gate_sum[:, 3, :], gate_sum[:, 2, :]))
                v.tensor_tensor(gates[g][:, :, :].rearrange("p b (c e) -> p b c e", c=3)
                                [:, :, :, 0:experts],
                                lg.unsqueeze(2).broadcast_to([128, G, 3, experts]),
                                gate_sum[:, 3, :].unsqueeze(2).unsqueeze(3).broadcast_to([128, G, 3, experts]),
                                ALU.mult).then_inc(gates_ready, 1)

            def block3(g, k):
                first = block_rank(3, g)
                n = first + k
                dve.wait_ge(silu_ready, n + 1)
                if n >= 3:
                    dve.wait_ge(hidden_used, n - 2)
                if k == 0:
                    v.tensor_tensor(hidden[k % 3][:, :], silu[k % 2][:, :], slot[4][:, 1, :],
                                    ALU.mult).then_inc(hidden_ready, 1)
                else:
                    if k >= 2:
                        dve.wait_ge(hidden_ready, n)
                    then(v.tensor_tensor(product[g], silu[k % 2][:, :], slot[4 + k % 2][:, 1, :], ALU.mult))
                    dve.wait_ge(full[2], nth["gate", 3, g, k])
                    v.tensor_tensor(hidden[k % 3][:, :], product[g], slot[2], ALU.mult
                                    ).then_inc(hidden_ready, 1)

            def block6(g, k):
                first, per = block_rank(6, g), F_I // 128

                def gate_x(e):
                    s = e % 2
                    dve.wait_ge(full[s], nth["gate", 6, g, e])
                    v.tensor_tensor(x_gated[g][e % 2], x_t[g][:, :], slot[s], ALU.mult
                                    ).then_inc(x_gated_ready, 1)

                if k == 0:
                    gate_x(0)
                n = first + k
                if k % per == 0 and k // per + 1 < F_E:
                    gate_x(k // per + 1)
                dve.wait_ge(silu_ready, n + 1)
                dve.wait_ge(full[4 + k % 2], nth["up", 6, g, k])
                if n >= 3:
                    dve.wait_ge(hidden_used, n - 2)
                v.tensor_tensor(hidden[k % 3][:, :], silu[k % 2][:, :], slot[4 + k % 2][:, 1, :], ALU.mult
                                ).then_inc(hidden_ready, 1)

            def mamba_in(g):
                dve.wait_ge(loaded["mamba"], 16)
                if g == 0:
                    dve.wait_ge(scalar_consts, 1)
                    v.tensor_scalar(neg_a[:, :], a_exp[:, :], -1.0, None, ALU.mult).then_inc(neg_a_ready, 1)
                dve.wait_ge(padded_ready, 2 * g + 1)
                out3 = conv_x[g].rearrange("p (b l) -> p b l", b=G)
                then(v.tensor_scalar(out3, padded[0][:, :, 0:S], W["k_x"][:, 0:1], None, ALU.mult))
                for tap in range(1, 4):
                    last = v.scalar_tensor_tensor(out3, padded[0][:, :, tap:tap + S], W["k_x"][:, tap:tap + 1],
                                                  out3, ALU.mult, ALU.add)
                    if tap < 3:
                        then(last)
                last.then_inc(conv_x_ready, 1)

            def mamba_dt(g):
                split(1, ("bc", g), bc_parts[g], bc_parts_ready)
                dve.wait_ge(dt_exp_ready, g + 1)
                v.tensor_scalar(dt_one[g], dt_exp[g], 1.0, None, ALU.add).then_inc(dt_one_ready, 1)
                dve.wait_ge(dt_one_ready, g + 1)
                then(v.tensor_scalar(dt_back[g], dt_one[g], -1.0, None, ALU.add))
                then(v.tensor_scalar(dt_zero[g], dt_back[g], 0.0, None, ALU.is_equal))
                then(v.tensor_tensor(dt_back[g], dt_back[g], dt_zero[g], ALU.add))
                then(v.reciprocal(dt_div[g], dt_back[g]))
                then(v.tensor_tensor(dt_div[g], dt_div[g], dt_exp[g], ALU.mult))
                dve.wait_ge(dt_ln_ready, g + 1)
                then(v.tensor_tensor(dt_zero[g], dt_ln[g], dt_zero[g], ALU.add))
                then(v.tensor_tensor(dt_div[g], dt_div[g], dt_zero[g], ALU.mult))
                v.tensor_tensor(delta[g], dt_div[g], dt_relu[g], ALU.add).then_inc(delta_ready, 1)
                dve.wait_ge(delta_ready, g + 1)
                then(v.tensor_tensor(delta_u[g], delta[g], u_t[g], ALU.mult))

            def chunk(g, c):
                n = g * CHUNKS + c
                if c:
                    dve.wait_ge(scanned, n)
                dve.wait_ge(full[4], nth["bc", g, 2 * c])
                v.tensor_tensor(drive[g], slot[4], delta_u[g].unsqueeze(1).broadcast_to([128, NS, T]), ALU.mult
                                ).then_inc(bc_used, 1)
                dve.wait_ge(bc_used, 2 * n + 1)
                dve.wait_ge(decay_ready, n + 1)
                v.tensor_tensor_scan(state[g].rearrange("p n l -> p (n l)"),
                                     decay[c % 2][:, :, :].rearrange("p n l -> p (n l)"),
                                     drive[g].rearrange("p n l -> p (n l)"), 0.0,
                                     ALU.mult, ALU.add).then_inc(scanned, 1)
                dve.wait_ge(scanned, n + 1)
                if n >= 2:
                    dve.wait_ge(y_sum_ready, n - 1)
                dve.wait_ge(full[5], nth["bc", g, 2 * c + 1])
                v.tensor_tensor(read[g][c % 2], slot[5], state[g], ALU.mult).then_inc(bc_used, 1)

            def finish4(g):
                dve.wait_ge(y_sum_ready, (g + 1) * CHUNKS)
                v.scalar_tensor_tensor(y_t[g], u_t[g], W["d_skip"], y_sum[g], ALU.mult, ALU.add
                                       ).then_inc(y_ready, 1)
                add_residual(4, g, 0, x_tok[g])
                norm(4, g, h_tok[g], x_tok[g]).then_inc(x_tok_ready[g], 1)

            def finish_moe(layer, g):
                add_residual(layer, g, 0, x_tok[g])
                norm(layer, g, h_tok[g], x_tok[g]).then_inc(x_tok_ready[g], 1)

            constants()
            for step, layer, g, n in PLAN:
                if step == "prepare":
                    {1: prepare1, 2: prepare2, 5: prepare5}[layer](g)
                elif step == "attend":
                    attend(layer, g, n)
                elif step == "route":
                    route(layer, g)
                elif step == "gate_rows":
                    split(1, ("gates_t", layer, g), gate_parts[g], gate_parts_ready)
                elif step == "block":
                    (block3 if layer == 3 else block6)(g, n)
                elif step == "mamba_in":
                    mamba_in(g)
                elif step == "mamba_dt":
                    mamba_dt(g)
                elif step == "chunk":
                    chunk(g, n)
                elif layer in MOE:
                    finish_moe(layer, g)
                else:
                    {1: finish1, 2: finish2, 4: finish4, 5: finish5}[layer](g)

        @block.scalar
        def _(act):
            sc = nc.scalar

            def copy_x_t(layer, g):
                act.wait_ge(full[2], nth["x_t", layer, g])
                sc.copy(x_t[g][:, :], slot[2]).then_inc(x_t_ready[g], 1)

            def copy_weighed_t(layer, g, b):
                columns_ = FORM[layer][0] * 128
                act.wait_ge(weighed, unit_rank(layer, g) + FORM[layer][0] // 2 * (b + 1))
                if b:
                    act.wait_ge(full[2], nth["weighed", layer, g, b - 1])
                sc.copy(weighed_t[:, 0:columns_], slot[weighed_slot(layer, g)][:, 0:columns_]
                        ).then_inc(weighed_t_ready, 1)

            def exponentials(layer, g, b):
                first, units = unit_rank(layer, g), FORM[layer][0] // 2
                for u in range(units * b, units * (b + 1)):
                    s = 4 + u % 2
                    act.wait_ge(full[s], nth["scores_t", layer, g, u])
                    if first + u >= 2:
                        act.wait_ge(weighed, first + u - 1)
                    sc.activation(probs[u % 2][:, :, :], slot[s], ACT.Exp).then_inc(exp_ready, 1)
                    if b and u == units * b:
                        copy_weighed_t(layer, g, b - 1)

            def copy_att_t(layer, g):
                act.wait_ge(full[0], nth["att_t", layer, g])
                sc.copy(att_t[g][:, :], slot[0]).then_inc(att_t_ready, 1)

            def gate_exponentials(layer, g):
                experts, m = MOE[layer][0], moe_rank(layer, g)
                act.wait_ge(gate_shift_ready, m + 1)
                sc.activation(gate_exp[:, :, 0:experts], gate_exp[:, :, 0:experts], ACT.Exp
                              ).then_inc(gate_exp_ready, 1)

            def block_silu(layer, g, k):
                n = block_rank(layer, g) + k
                act.wait_ge(full[4 + k % 2], nth["up", layer, g, k])
                if n >= 2:
                    act.wait_ge(hidden_ready, n - 1)
                sc.activation(silu[k % 2][:, :], slot[4 + k % 2][:, 0, :], ACT.Silu).then_inc(silu_ready, 1)

            def copy_moe_t(layer, g):
                act.wait_ge(hidden_used, block_rank(layer, g) + MOE[layer][1])
                sc.copy(moe_t[g], slot[3]).then_inc(moe_t_ready, 1)

            def mamba_in(g):
                if g == 0:
                    act.wait_ge(loaded["mamba"], 16)
                    sc.activation(a_exp[:, :], W["a_log"], ACT.Exp).then_inc(scalar_consts, 1)
                copy_x_t(4, g)
                for s, convolved in enumerate((conv_x_ready, conv_z_ready)):
                    if g:
                        act.wait_ge(convolved, g)
                    act.wait_ge(full[s], nth["in", g, s])
                    sc.copy(padded[s][:, :, 1:S + 1], slot[s].rearrange("p (b l) -> p b l", b=G)
                            ).then_inc(padded_ready, 1)
                act.wait_ge(conv_x_ready, g + 1)
                sc.activation(u_t[g], conv_x[g], ACT.Gelu, bias=W["b_x"]).then_inc(u_ready, 1)

            def mamba_z(g):
                act.wait_ge(conv_z_ready, g + 1)
                sc.activation(z_t[g], conv_z[g], ACT.Gelu, bias=W["b_z"]).then_inc(z_ready, 1)

            def mamba_dt(g):
                act.wait_ge(full[2], nth["dt_low", g])
                sc.copy(dt_low[:, :], slot[2][0:RANK, :]).then_inc(dt_low_ready, 1)
                act.wait_ge(full[0], nth["dt", g])
                sc.activation(dt_abs[g], slot[0], ACT.Abs, bias=W["b_dt"]).then_inc(scalar_step, 1)
                sc.activation(dt_relu[g], slot[0], ACT.Relu, bias=W["b_dt"])
                act.wait_ge(scalar_step, g + 1)
                sc.activation(dt_exp[g], dt_abs[g], ACT.Exp, scale=-1.0).then_inc(dt_exp_ready, 1)
                act.wait_ge(dt_one_ready, g + 1)
                sc.activation(dt_ln[g], dt_one[g], ACT.Ln).then_inc(dt_ln_ready, 1)
                act.wait_ge(delta_ready, g + 1)
                if g == 0:
                    act.wait_ge(neg_a_ready, 1)

            def chunk(g, c):
                n = g * CHUNKS + c
                if n >= 2:
                    act.wait_ge(scanned, n - 1)
                for i in range(NS):
                    last = sc.activation(decay[c % 2][:, i, :], delta[g], ACT.Exp,
                                         scale=neg_a[:, c * NS + i:c * NS + i + 1])
                last.then_inc(decay_exp_ready, 1)

            act.wait_ge(vector_consts, VECTOR_CONSTS)
            for step, layer, g, n in PLAN:
                if step == "prepare":
                    copy_x_t(layer, g)
                elif step == "attend":
                    exponentials(layer, g, n)
                elif step == "route":
                    copy_x_t(layer, g)
                    gate_exponentials(layer, g)
                elif step == "block":
                    block_silu(layer, g, n)
                elif step == "mamba_in":
                    mamba_in(g)
                elif step == "mamba_dt":
                    mamba_dt(g)
                elif step == "chunk":
                    chunk(g, n)
                    if n == 1:
                        mamba_z(g)
                elif step == "finish" and layer in MOE:
                    copy_moe_t(layer, g)
                elif step == "finish" and layer in FORM:
                    copy_weighed_t(layer, g, G - 1)
                    if layer < 3:
                        copy_att_t(layer, g)

        @block.gpsimd
        def _(pool):
            p = nc.gpsimd
            steps = [0]

            def then(instruction):
                steps[0] += 1
                instruction.then_inc(pool_step, 1)
                pool.wait_ge(pool_step, steps[0])

            def deviations(layer, g, second=False):
                pool.wait_ge(var_ready[g], norm_rank(layer, second) + 1)
                then(p.tensor_scalar(var_eps[:, :], mean_var[g][:, :, 1], LN_EPS, None, ALU.add))
                p.tensor_tensor(rstd[g][:, :], var_eps[:, :], half[:, :], ALU.pow).then_inc(rstd_ready[g], 1)

            def residual(layer, g, src, bias):
                p.tensor_tensor(x_res[g][:, :, :], src[g][:, :, :], R[bias].unsqueeze(1).broadcast_to([128, G, D]),
                                ALU.add).then_inc(res_ready, 1)

            def mamba_in(g):
                pool.wait_ge(padded_ready, 2 * g + 2)
                pool.wait_ge(loaded["mamba"], 16)
                out3 = conv_z[g].rearrange("p (b l) -> p b l", b=G)
                tap3 = conv_z_tap[g].rearrange("p (b l) -> p b l", b=G)
                then(p.tensor_scalar(out3, padded[1][:, :, 0:S], W["k_z"][:, 0:1], None, ALU.mult))
                for tap in range(1, 4):
                    then(p.tensor_scalar(tap3, padded[1][:, :, tap:tap + S], W["k_z"][:, tap:tap + 1], None,
                                         ALU.mult))
                    last = p.tensor_tensor(out3, out3, tap3, ALU.add)
                    if tap < 3:
                        then(last)
                last.then_inc(conv_z_ready, 1)

            def cut(g, c):
                pool.wait_ge(decay_exp_ready, g * CHUNKS + c + 1)
                p.memset(decay[c % 2][:, :, :].rearrange("p n (b l) -> p n b l", b=G)[:, :, :, 0:1], 0.0
                         ).then_inc(decay_ready, 1)

            def chunk(g, c):
                cut(g, c)
                pool.wait_ge(bc_used, 2 * (g * CHUNKS + c + 1))
                pair = y_sum[g] if c == 0 else y_pair[g]
                last = p.tensor_tensor(pair, read[g][c % 2][:, 0, :], read[g][c % 2][:, 1, :], ALU.add)
                if c:
                    then(last)
                    last = p.tensor_tensor(y_sum[g], y_sum[g], y_pair[g], ALU.add)
                last.then_inc(y_sum_ready, 1)
                pool.wait_ge(y_sum_ready, g * CHUNKS + c + 1)

            p.memset(ones_b[:, :], 1.0).then_inc(pool_consts, 1)
            p.memset(half[:, :], -0.5).then_inc(pool_consts, 1)
            for g in groups:
                p.memset(neg_max[g][:, :, :], 0.0).then_inc(pool_consts, 1)
                p.memset(v_heads_a[g][:, :, :], 1.0).then_inc(pool_consts, 1)
                p.memset(v_heads_x[g][:, :, :], 1.0).then_inc(pool_consts, 1)
                p.memset(gates[g][:, :, :], 0.0).then_inc(pool_consts, 1)
                p.memset(padded[g][:, :, :], 0.0).then_inc(pool_consts, 1)
            pool.wait_ge(pool_consts, POOL_CONSTS)
            for step, layer, g, n in PLAN:
                if step == "prepare" and layer == 1:
                    if g == 0:
                        pool.wait_ge(loaded["rows"], 16)
                    pool.wait_ge(x_pe_ready, g + 1)
                    residual(1, g, x_pe, "bo")
                elif step == "prepare" and layer == 2:
                    pool.wait_ge(x_tok_ready[g], 1)
                    residual(2, g, x_tok, "b_out")
                elif step == "mamba_in":
                    mamba_in(g)
                elif step == "chunk":
                    chunk(g, n)
                elif step == "finish":
                    deviations(layer, g)
                    if layer == 1:
                        deviations(1, g, second=True)

        @block.sync
        def _(sp):
            where = dict(packed)

            def load(name):
                sp.dma_start(pack_sb[name][:, :], where[name]).then_inc(loaded[name], 16)

            def form_stacks(layer, g):
                a = att_rank(layer, g)
                hd = FORM[layer][1]
                sides = 16 // hd
                for parts, ready, saved, made in ((k_parts[g], k_parts_ready, k_parts_saved, k_made[a]),
                                                  (q_parts[g], q_parts_ready, q_parts_saved, q_made[a])):
                    sp.wait_ge(ready, a + 1)
                    for i in range(3):
                        sp.dma_start(made[i].rearrange("d h t -> h d t"), parts[i]).then_inc(saved[g], 16)
                at = slice(g * T, (g + 1) * T)
                if layer > 1:
                    if layer == 5:
                        sp.wait_ge(ik_rows_ready, 1)
                    rows_ = fk_rows if layer == 2 else ik_rows
                    const = slice(CONST_ROW, CONST_ROW + 4)
                    sp.dma_start(k_stack[g][const, :, :], rows_[const, at].unsqueeze(1).broadcast_to([4, 8, T])
                                 ).then_inc(stacks_ready[g], 16)
                    sp.dma_start(q_stack[g][const, :, :], ones_b[const, :].unsqueeze(1).broadcast_to([4, 8, T])
                                 ).then_inc(stacks_ready[g], 16)
                for is_q, saved, made, stack_ in ((False, k_parts_saved, k_made[a], k_stack[g]),
                                                  (True, q_parts_saved, q_made[a], q_stack[g])):
                    sp.wait_ge(saved[g], 16 * 3 * att_nth(layer))
                    for side in range(sides):
                        row = 64 * side
                        for n in range(3):
                            many = 3 - n
                            src = made[0:many] if is_q else made[n:n + 1].broadcast_to([many, 16, 8, T])
                            src = src[:, side * hd:(side + 1) * hd, :, :].rearrange("n d h t -> n d (h t)")
                            sp.dma_start(stack_[row:row + many * hd, :, :], src).then_inc(stacks_ready[g], 16)
                            row += many * hd

            sp.dma_start(x_tok[0][:, :, :], x[0:G].rearrange("b s d -> s b d")).then_inc(x_loaded[0], 16)
            load("first")
            sp.dma_start(rows_sb[:, :], rows.broadcast_to([128, rows_width])).then_inc(loaded["rows"], 16)
            sp.dma_start(ik_row_sb, ik_row.broadcast_to([128, B * S])).then_inc(loaded["ik"], 16)
            sp.dma_start(x_tok[1][:, :, :], x[G:2 * G].rearrange("b s d -> s b d")).then_inc(x_loaded[1], 16)
            sp.wait_ge(vector_consts, VECTOR_CONSTS)
            sp.wait_ge(pool_consts, POOL_CONSTS)
            form_stacks(1, 0)
            load("masks")
            load("cross")
            for g in groups:
                sp.dma_start(ctx_sb[g][:, :, :], ctx_t[:, :, g * T:(g + 1) * T].rearrange("c p t -> p c t")
                             ).then_inc(ctx_loaded[g], 16)
                sp.dma_start(v_ctx_sb[g][:, :, :], v_ctx[g * G:(g + 1) * G].rearrange("b s d -> s b d")
                             ).then_inc(ctx_loaded[g], 16)
            form_stacks(1, 1)
            load("moe0")
            for step, layer, g, _ in PLAN:
                if step == "prepare" and layer > 1:
                    form_stacks(layer, g)
                    if (layer, g) == (2, 0):
                        load("mamba")
                    if (layer, g) == (2, 1):
                        load("moe1")
            for g in groups:
                sp.wait_ge(x_tok_ready[g], STAGE)
                sp.dma_start(out[g * G:(g + 1) * G].rearrange("b s d -> s b d"), x_tok[g][:, :, :]
                             ).then_inc(stored, 16)
            sp.wait_ge(stored, 16 * NG)
            for g in groups:
                sp.wait_ge(k_parts_saved[g], 16 * 3 * att_nth(STAGE))
                sp.wait_ge(q_parts_saved[g], 16 * 3 * att_nth(STAGE))


def lay_out(i):
    def rows_of(a):
        return np.ascontiguousarray(a, dtype=np.float32)

    def col(a):
        return a.reshape(-1, 1)

    def halves(a):
        return np.concatenate([a[:128], a[128:]], axis=1)

    p = np.arange(128)
    w_src, w_mo = i["L0_xattn_W_src"].T, i["L1_attn_W_out"]
    xproj = i["L1_attn_W_xproj"]
    w_dt = np.zeros((128, 128), np.float32)
    w_dt[:RANK] = i["L1_attn_W_dt"]
    per_block = lambda w: np.transpose(w.reshape(F_E, D, F_I // 128, 128), (3, 0, 2, 1)).reshape(128, -1)
    side = lambda w: np.transpose(w, (1, 0, 2)).reshape(D, -1)
    down0 = np.concatenate([i["L0_ffn_wd_s"].reshape(128, D), i["L0_ffn_wd_r"].reshape(-1, D)])
    a = {
        "ident": np.eye(128), "max_row": (p[:, None] % 4 == np.arange(4)) & (p[:, None] % 32 < 8),
        "quad": (p[:, None] // 32 == np.arange(NQ)), "fk_row": (p[:, None] == CONST_ROW) * -MASKED,
        "ik_row": (p[:, None] == CONST_ROW) * MASKED, "b_rows": (p[:, None] == CONST_ROW + 1 + np.arange(3)),
        "iota": np.tile(np.arange(16), (128, 1)), "sel32": (p[:, None] % 32 == np.arange(32)),
        "pe": i["L0_attn_pe"][0, :S], "wq": i["L0_attn_wq"], "wk": i["L0_attn_wk"], "bq": col(i["L0_attn_bq"]),
        "bk": col(i["L0_attn_bk"]), "wv": i["L0_attn_wv"], "wo": i["L0_attn_wo"],
        "w_src": halves(w_src), "w_tgt": i["L0_xattn_W_tgt"].T, "w_out": halves(i["L0_xattn_W_out"].T),
        "b_srck": col(i["L0_xattn_b_src"][:128]), "b_tgt": col(i["L0_xattn_b_tgt"]),
        "b1": np.tile(i["L1_xattn_b"], (128, 1)),
        "router0": i["L0_ffn_router_w"],
        "wg0": np.concatenate([side(i["L0_ffn_wg_s"]), side(i["L0_ffn_wg_r"])], axis=1),
        "wu0": np.concatenate([side(i["L0_ffn_wu_s"]), side(i["L0_ffn_wu_r"])], axis=1),
        "wd0": np.transpose(down0.reshape(A_BLOCKS, 128, D), (1, 0, 2)).reshape(128, -1),
        "w_in": i["L1_attn_W_in"], "w_dtlow": xproj[:, :RANK], "w_bc": np.tile(xproj[:, RANK:], (1, 3)),
        "w_dt": w_dt, "w_mo": halves(w_mo), "b_dt": col(i["L1_attn_b_dt"]), "b_x": col(i["L1_attn_b_x"]),
        "b_z": col(i["L1_attn_b_z"]), "d_skip": col(i["L1_attn_D"]), "k_x": i["L1_attn_K_x"][:, 0],
        "k_z": i["L1_attn_K_z"][:, 0], "a_log": i["L1_attn_A_log"],
        "router1": i["L1_ffn_wg"].T, "w1": i["L1_ffn_w1"].reshape(-1, D).T, "w3": i["L1_ffn_w3"].reshape(-1, D).T,
        "w2": per_block(i["L1_ffn_w2"]), "fk_tok": i["mask_BxS2_fk1"].T,
        "bv": i["L0_attn_bv"], "bo": i["L0_attn_bo"], "gamma": i["L0_attn_gamma"], "beta": i["L0_attn_beta"],
        "b_srcv": i["L0_xattn_b_src"][128:], "b_out": i["L0_xattn_b_out"], "fk": i["mask_BxS2_fk1"].reshape(-1),
    }
    arrays = {f"pack_{name}": rows_of(np.concatenate([a[n] for n, _ in pack], axis=1))
              for name, pack in PACKS.items()}
    arrays["rows"] = rows_of(np.concatenate([a[n].reshape(1, -1) for n, _ in ROWS], axis=1))
    ik = i["mask_BxS2_ik0"]
    arrays["ik_row"] = np.ascontiguousarray(ik.reshape(1, -1))
    arrays["x"] = rows_of(i["x"])
    ctx = i["ctx_2048"]
    arrays["ctx_t"] = rows_of(np.transpose(ctx, (2, 0, 1)).reshape(2, 128, B * S))
    arrays["v_ctx"] = rows_of(ctx[:, :, 128:])
    return arrays


def kernel(**inputs):
    import concourse.bacc as bacc
    from concourse.bass_utils import run_bass_kernel_spmd

    arrays = lay_out({name: np.asarray(a) for name, a in inputs.items()})
    nc = bacc.Bacc("TRN2", target_bir_lowering=False, num_devices=1)
    d = {name: nc.dram_tensor(f"in_{name}", a.shape, mybir.dt.from_np(a.dtype), kind="ExternalInput").ap()
         for name, a in arrays.items()}
    out = nc.dram_tensor("out", (B, S, D), mybir.dt.float32, kind="ExternalOutput").ap()
    packed = [(name, d[f"pack_{name}"]) for name in PACKS]
    k_made, q_made = ([nc.dram_tensor(f"{n}_made{i}", (3, 16, 8, T), mybir.dt.bfloat16, kind="Internal").ap()
                       for i in range(3 * NG)] for n in "kq")
    decoder(nc, packed, d["rows"], d["ik_row"], d["x"], d["ctx_t"], d["v_ctx"], k_made, q_made, out)
    result = run_bass_kernel_spmd(nc, [{f"in_{name}": a for name, a in arrays.items()}], core_ids=[0])
    return result.results[0]["out"]
```

```python
from contextlib import ExitStack

import numpy as np

import concourse.bass as bass
from concourse import mybir

STAGE = 6

B, S, D = 8, 128, 128
NG = 2
G = B // NG
T = G * S
NQ = 4
A_HEADS, X_HEADS = 16, 8
A_E, F_E = 16, 8
F_I = 256
A_BLOCKS = 5
NSTATE, RANK = 16, 8
LN_EPS = 1e-5
MASKED = 2.0 ** 100

CONST_ROW = 96

PACKS = {
    "first": [("ident", 128), ("max_row", 4), ("quad", NQ), ("fk_row", 1), ("ik_row", 1), ("b_rows", 3),
              ("iota", 16), ("sel32", 32), ("pe", 128), ("wq", 128), ("wk", 128), ("bq", 1), ("bk", 1), ("wv", 128), ("wo", 128)],
    "cross": [("w_src", 512), ("w_tgt", 128), ("w_out", 256), ("b_srck", 1), ("b_tgt", 1), ("b1", 1)],
    "moe0": [("router0", A_E), ("wg0", 128 * A_BLOCKS), ("wu0", 128 * A_BLOCKS), ("wd0", 128 * A_BLOCKS)],
    "mamba": [("w_in", 256), ("w_dtlow", RANK), ("w_bc", 96), ("w_dt", 128), ("w_mo", 256), ("b_dt", 1),
              ("b_x", 1), ("b_z", 1), ("d_skip", 1), ("k_x", 4), ("k_z", 4), ("a_log", NSTATE)],
    "moe1": [("router1", F_E), ("w1", F_E * F_I), ("w3", F_E * F_I), ("w2", F_E * F_I)],
    "masks": [("fk_tok", B)],
}
ROWS = [("bv", D), ("bo", D), ("gamma", D), ("beta", D), ("b_srcv", D), ("b_out", D), ("fk", B * S)]


def columns(pack):
    at, out = 0, {}
    for name, width in pack:
        out[name] = (at, width)
        at += width
    return out, at


def decoder(nc, packed, rows, ik_row, x, ctx_t, v_ctx, k_made, q_made, out):
    fp32, bf16, u32, i32 = mybir.dt.float32, mybir.dt.bfloat16, mybir.dt.uint32, mybir.dt.int32
    ALU = mybir.AluOpType
    ACT = mybir.ActivationFunctionType
    AX = mybir.AxisListType.X
    groups = range(NG)

    with ExitStack() as stack:
        def sb(name, shape, dt=fp32):
            return stack.enter_context(nc.sbuf_tensor(name, shape, dt))

        def sem(name):
            return stack.enter_context(nc.semaphore(name))

        pack_sb, W = {}, {}
        for pname, pack in PACKS.items():
            where, width = columns(pack)
            pack_sb[pname] = sb("pack_" + pname, [128, width])
            for name, (at, w) in where.items():
                W[name] = pack_sb[pname][:, at:at + w]
        where, rows_width = columns(ROWS)
        rows_sb = sb("rows_sb", [128, rows_width])
        R = {name: rows_sb[:, at:at + w] for name, (at, w) in where.items()}
        ident = W["ident"]
        ones_b = sb("ones_b", [128, T], bf16)
        quad_ones_b = sb("quad_ones_b", [128, NQ, 128], bf16)
        sel32_b = sb("sel32_b", [128, 32, 128], bf16)
        spread_b = sb("spread_b", [128, A_E, 32], bf16)
        half = sb("half", [128, G])
        neg_a = sb("neg_a", [128, NSTATE])
        fk_rows = sb("fk_rows", [128, B * S], bf16)
        ik_rows = sb("ik_rows", [128, B * S], bf16)
        b_parts = sb("b_parts", [128, 3], bf16)
        b_rest = sb("b_rest", [128, 1])
        b_col = sb("b_col", [128, 1])
        a_exp = sb("a_exp", [128, NSTATE])

        def per_group(name, shape, dt=fp32):
            return [sb(f"{name}{g}", shape, dt) for g in groups]

        x_tok = per_group("x_tok", [128, G, D])
        x_pe = per_group("x_pe", [128, G, D])
        x_res = per_group("x_res", [128, G, D])
        h_tok = per_group("h_tok", [128, G, D])
        x_t = per_group("x_t", [128, T])
        ctx_sb = per_group("ctx_sb", [128, 2, T])
        v_ctx_sb = per_group("v_ctx_sb", [128, G, D])
        q_t = per_group("q_t", [128, T])
        k_t = per_group("k_t", [128, T])
        q_stack = per_group("q_stack", [128, 8, T], bf16)
        k_stack = per_group("k_stack", [128, 8, T], bf16)
        v_heads_a = per_group("v_heads_a", [128, G, A_HEADS * (D // A_HEADS + 1)])
        v_heads_x = per_group("v_heads_x", [128, G, X_HEADS * (D // X_HEADS + 1)])
        neg_max = per_group("neg_max", [128, G, 128])
        neg_high = sb("neg_high", [128, NQ, 4], bf16)
        max_t = per_group("max_t", [128, 2, 4, 128], bf16)
        probs = [sb(f"probs{i}", [128, 2, 512]) for i in range(2)]
        weighed_t = sb("weighed_t", [128, T])
        rec = sb("rec", [128, A_HEADS])
        att = per_group("att", [128, G, D])
        att_t = per_group("att_t", [128, T])
        stats = sb("stats", [128, G, 6])
        mean_var = per_group("mean_var", [128, G, 2])
        var_eps = per_group("var_eps", [128, G])
        rstd = per_group("rstd", [128, G])

        logits = sb("logits", [128, G, A_E])
        top8 = sb("top8", [128, G, 8])
        top_i = sb("top_i", [128, G, 8], u32)
        top_f = sb("top_f", [128, G, 2])
        picked = sb("picked", [128, 2, G, A_E])
        gate_exp = sb("gate_exp", [128, G, A_E])
        gate_sum = sb("gate_sum", [128, 4, G])
        gates = per_group("gates", [128, G, 96])
        residue = sb("residue", [96, T])
        middle = sb("middle", [96, T], bf16)
        gate_parts = per_group("gate_parts", [96, T], bf16)
        silu = [sb(f"silu{i}", [128, T]) for i in range(2)]
        hidden = [sb(f"hidden{i}", [128, T]) for i in range(3)]

        NS = 2
        CHUNKS = NSTATE // NS

        def flat(ap):
            return ap.rearrange("p a b -> p (a b)")

        halves = {name: [(flat(t[g][:, :, :]) if name != "att_t" else t[g][:, :]).bitcast(bf16)
                         .rearrange("p (n t) -> p n t", n=2) for g in groups]
                  for name, t in (("h_tok", h_tok), ("att_t", att_t), ("att", att))}
        k_parts = [[halves["h_tok"][g][:, 0, :], halves["h_tok"][g][:, 1, :], halves["att_t"][g][:, 0, :]]
                   for g in groups]
        early = [[t[:, :].bitcast(bf16).rearrange("p (n t) -> p n t", n=2) for t in pair] for pair in (hidden[0:2], silu)]
        k_parts_2 = [[early[g][0][:, 0, :], early[g][0][:, 1, :], early[g][1][:, 0, :]] for g in groups]
        q_parts = [[halves["att_t"][g][:, 1, :], halves["att"][g][:, 0, :], halves["att"][g][:, 1, :]]
                   for g in groups]
        product = [flat(x_res[g][:, :, :]) for g in groups]
        x_gated = [(flat(att[g][:, :, :]), att_t[g][:, :]) for g in groups]
        moe_t = [flat(x_pe[g][:, :, :]) for g in groups]
        u_t, y_t = [k_t[g][:, :] for g in groups], [q_t[g][:, :] for g in groups]
        delta, z_t = [att_t[g][:, :] for g in groups], [flat(att[g][:, :, :]) for g in groups]
        delta_u = [flat(x_pe[g][:, :, :]) for g in groups]
        y_sum = [flat(x_res[g][:, :, :]) for g in groups]
        y_pair = [flat(h_tok[g][:, :, :]) for g in groups]
        k_space, q_space = ([flat(t[g][:, :, :]).bitcast(fp32).rearrange("p (a b) -> p a b", b=T) for g in groups]
                            for t in (k_stack, q_stack))
        (dt_abs, dt_exp, dt_relu, dt_ln), (dt_one, dt_back, dt_zero, dt_div) = (
            [[t[g][:, i, :] for g in groups] for i in range(4)] for t in (k_space, q_space))
        drive, state = [k_space[g][:, 0:2, :] for g in groups], [k_space[g][:, 2:4, :] for g in groups]
        read = [[q_space[g][:, 2 * i:2 * i + 2, :] for i in range(2)] for g in groups]
        conv_x = dt_div
        conv_z = [flat(v_heads_a[g][:, :, :])[:, 0:T] for g in groups]
        padded = [sb(f"padded_{n}", [128, G, S + 3]) for n in "xz"]
        dt_low = sb("dt_low", [RANK, T])
        bc_parts = per_group("bc_parts", [96, T], bf16)
        decay = [sb(f"decay{i}", [128, NS, T]) for i in range(2)]
        ik_row_sb = flat(decay[0][:, :, :]).bitcast(i32)

        psum = stack.enter_context(nc.psum_tensor("psum", [128, 8, 512], fp32))
        slot = [psum[:, i, :] for i in range(4)] + [psum[:, 4:6, :], psum[:, 6:8, :]]
        full = [sem(f"psum_full{i}") for i in range(6)]
        filled = [0] * 6
        released = [None] * 6
        nth = {}

        loaded = {p: sem("loaded_" + p) for p in [*PACKS, "rows", "ik"]}
        x_loaded = [sem(f"x_loaded{g}") for g in groups]
        ctx_loaded = [sem(f"ctx_loaded{g}") for g in groups]
        pool_consts, vector_consts, scalar_consts = sem("pool_consts"), sem("vector_consts"), sem("scalar_consts")
        x_pe_ready, res_ready = sem("x_pe_ready"), sem("res_ready")
        x_t_ready, x_tok_ready, sum_ready, var_ready, rstd_ready = (
            [sem(f"{n}{g}") for g in groups] for n in ("x_t_ready", "x_tok_ready", "sum_ready", "var_ready", "rstd_ready"))
        k_parts_ready, q_parts_ready = sem("k_parts_ready"), sem("q_parts_ready")
        k_parts_saved, q_parts_saved, stacks_ready = (
            [sem(f"{n}{g}") for g in groups] for n in ("k_parts_saved", "q_parts_saved", "stacks_ready"))
        v_ready, ik_rows_ready = sem("v_ready"), sem("ik_rows_ready")
        max_ready, lows_ready, max_t_ready = sem("max_ready"), sem("lows_ready"), sem("max_t_ready")
        exp_ready, weighed, weighed_t_ready = sem("exp_ready"), sem("weighed"), sem("weighed_t_ready")
        att_ready, att_t_ready = sem("att_ready"), sem("att_t_ready")
        logits_ready, gate_shift_ready, gate_exp_ready = sem("logits_ready"), sem("gate_shift_ready"), sem("gate_exp_ready")
        gates_ready, gate_parts_ready = sem("gates_ready"), sem("gate_parts_ready")
        x_gated_ready, silu_ready, hidden_ready = sem("x_gated_ready"), sem("silu_ready"), sem("hidden_ready")
        hidden_used, moe_t_ready = sem("hidden_used"), sem("moe_t_ready")
        padded_ready, conv_x_ready, conv_z_ready = sem("padded_ready"), sem("conv_x_ready"), sem("conv_z_ready")
        u_ready, z_ready, dt_low_ready = sem("u_ready"), sem("z_ready"), sem("dt_low_ready")
        bc_parts_ready, dt_exp_ready, dt_one_ready = sem("bc_parts_ready"), sem("dt_exp_ready"), sem("dt_one_ready")
        dt_ln_ready, delta_ready = sem("dt_ln_ready"), sem("delta_ready")
        neg_a_ready = sem("neg_a_ready")
        decay_ready, scanned = sem("decay_ready"), sem("scanned")
        bc_used, y_sum_ready, y_ready = sem("bc_used"), sem("y_sum_ready"), sem("y_ready")
        vector_step, scalar_step, pool_step = sem("vector_step"), sem("scalar_step"), sem("pool_step")
        stored = sem("stored")

        VECTOR_CONSTS, POOL_CONSTS = 5, 2 + 5 * NG

        block = stack.enter_context(nc.Block())

        ORDER = [(layer, g) for layer in range(1, STAGE + 1) for g in groups]
        FORM = {1: (A_HEADS // 4, D // A_HEADS), 2: (X_HEADS // 4, D // X_HEADS), 5: (X_HEADS // 4, D // X_HEADS)}
        MOE = {3: (A_E, A_BLOCKS), 6: (F_E, F_E * F_I // 128)}

        def before(layer, g, per):
            return sum(per(*o) for o in ORDER[:ORDER.index((layer, g))])

        def att_rank(layer, g):
            return before(layer, g, lambda l, _: l in FORM)

        def proj_rank(layer, g):
            return before(layer, g, lambda l, _: l in (1, 2))

        def moe_rank(layer, g):
            return before(layer, g, lambda l, _: l in MOE)

        def max_rank(layer, g):
            return before(layer, g, lambda l, _: FORM[l][0] * G if l in FORM else 0)

        def unit_rank(layer, g):
            return before(layer, g, lambda l, _: FORM[l][0] // 2 * G if l in FORM else 0)

        def stacking(layer):
            return 12 if layer == 1 else 8

        def att_nth(layer):
            return sum(l in FORM for l in range(1, layer + 1))

        def stack_loads(layer):
            return sum(stacking(l) for l in range(1, layer + 1) if l in FORM)

        def weighed_slot(layer, g):
            return 2 if (layer, g) == (5, 1) else 3

        def head_at(layer, quad, j):
            return 8 * (quad // 2) + 2 * j + quad % 2 if layer == 1 else 4 * quad + j

        def head_of(stack_, layer, h, b):
            if layer == 1:
                return stack_[64 * (h % 2):64 * (h % 2) + 6 * 8, h // 2, b * S:(b + 1) * S]
            return stack_[0:CONST_ROW + 4, h, b * S:(b + 1) * S]

        def block_rank(layer, g):
            return before(layer, g, lambda l, _: MOE[l][1] if l in MOE else 0)

        def norm_rank(layer, second=False):
            return layer - 1 + (layer > 1) + second

        def v_heads(layer, g):
            return v_heads_a[g] if layer == 1 else v_heads_x[g]

        def steps_of(layer, g):
            if layer in FORM:
                return [("attend", layer, g, b) for b in range(G)]
            if layer in MOE:
                return [("block", layer, g, k) for k in range(MOE[layer][1])]
            return [("chunk", layer, g, c) for c in range(CHUNKS)]

        def item(names, layer, g):
            main = steps_of(layer, g)
            return [main[int(name)] if name.isdigit() else (name, layer, g, 0) for name in names.split()]

        PLAN = item("prepare", 1, 0) + item("prepare", 1, 1) + item("scores 0 1", 1, 0) + item("keys", 2, 0)
        PLAN += item("2 3", 1, 0) + item("scores", 1, 1) + item("finish", 1, 0) + item("0", 1, 1)
        PLAN += item("project norm", 1, 0) + item("1", 1, 1) + item("second_norm", 1, 0) + item("prepare", 2, 0)
        PLAN += item("2", 1, 1) + item("keys", 2, 1) + item("3", 1, 1) + item("scores", 2, 0)
        PLAN += item("finish project", 1, 1) + item("0", 2, 0) + item("norm", 1, 1) + item("1", 2, 0)
        PLAN += item("second_norm", 1, 1) + item("prepare", 2, 1) + item("2 3", 2, 0) + item("scores", 2, 1)
        PLAN += item("finish", 2, 0) + item("0", 2, 1) + item("project", 2, 0) + item("1", 2, 1)
        PLAN += item("norm", 2, 0) + item("route", 3, 0) + item("2 3", 2, 1) + item("gate_rows 0", 3, 0)
        PLAN += item("finish", 2, 1) + item("1", 3, 0) + item("project", 2, 1) + item("2", 3, 0)
        PLAN += item("norm", 2, 1) + item("3", 3, 0) + item("route", 3, 1) + item("4 finish", 3, 0)
        PLAN += item("gate_rows 0", 3, 1) + item("project norm", 3, 0) + item("mamba_in mamba_dt", 4, 0)
        PLAN += item("1 2", 3, 1) + item("mamba_ln 0", 4, 0) + item("3", 3, 1) + item("1", 4, 0) + item("4", 3, 1)
        PLAN += item("2 3", 4, 0) + item("project finish", 3, 1) + item("4", 4, 0) + item("norm", 3, 1)
        PLAN += item("5 6", 4, 0) + item("mamba_in", 4, 1) + item("7", 4, 0) + item("mamba_dt mamba_ln", 4, 1)
        PLAN += item("finish", 4, 0) + item("0", 4, 1) + item("project", 4, 0) + item("1", 4, 1)
        PLAN += item("norm", 4, 0) + item("prepare", 5, 0) + item("2 3", 4, 1) + item("scores 0", 5, 0)
        PLAN += item("4", 4, 1) + item("1", 5, 0) + item("5", 4, 1) + item("2 3", 5, 0) + item("6", 4, 1)
        PLAN += item("finish project", 5, 0) + item("7", 4, 1) + item("norm", 5, 0) + item("finish", 4, 1)
        PLAN += item("route", 6, 0) + item("project norm", 4, 1) + item("gate_rows 0 1", 6, 0)
        PLAN += item("prepare", 5, 1) + item("2 3 4 5", 6, 0) + item("scores", 5, 1) + item("6", 6, 0)
        PLAN += item("0", 5, 1) + item("7 8", 6, 0) + item("1", 5, 1) + item("9 10", 6, 0) + item("2", 5, 1)
        PLAN += item("11 12", 6, 0) + item("3", 5, 1) + item("13", 6, 0) + item("finish", 5, 1) + item("14", 6, 0)
        PLAN += item("project", 5, 1) + item("15", 6, 0) + item("norm", 5, 1) + item("route", 6, 1)
        PLAN += item("finish", 6, 0) + item("gate_rows 0", 6, 1) + item("project", 6, 0) + item("1", 6, 1)
        PLAN += item("norm", 6, 0) + item("2 3 4 5 6 7 8 9 10 11 12 13 14 15 finish project norm", 6, 1)
        PLAN = [step for step in PLAN if step[1] <= STAGE]

        @block.tensor
        def _(pe):
            mm = nc.tensor.matmul

            def claim(s, label, sem_, value):
                if released[s]:
                    pe.wait_ge(*released[s])
                released[s] = (sem_, value)
                if label:
                    filled[s] += 1
                    nth[label] = filled[s]
                return slot[s]

            def to_t(src, dst):
                for b in range(G):
                    last = nc.tensor.transpose(dst[0:src.shape[2], b * S:(b + 1) * S], src[:, b, :], ident)
                return last

            def by_token(dst, *pairs):
                for b in range(G):
                    for n, (left_t, right) in enumerate(pairs):
                        last = mm(dst[:, b * S:(b + 1) * S], left_t[:, b * S:(b + 1) * S], right,
                                  start=n == 0, stop=n == len(pairs) - 1)
                return last

            def x_to_t(layer, g):
                pe.wait_ge(x_tok_ready[g], layer - 1)
                dst = claim(2, ("x_t", layer, g), x_t_ready[g], layer)
                to_t(x_tok[g], dst).then_inc(full[2], 1)

            def scores(layer, g, b):
                for quad in range(FORM[layer][0]):
                    s = quad % 2
                    dst = claim(s, ("scores", layer, g, b, quad), max_ready,
                                max_rank(layer, g) + FORM[layer][0] * b + quad + 1)
                    for j in range(4):
                        h = head_at(layer, quad, j)
                        last = mm(dst[:, j * 128:(j + 1) * 128], head_of(q_stack[g], layer, h, b),
                                  head_of(k_stack[g], layer, h, b), start=True, stop=True)
                    last.then_inc(full[s], 1)

            def maxima_to_t(layer, g, b):
                n = att_rank(layer, g) * G + b + 1
                pe.wait_ge(lows_ready, n)
                dst = claim(2, ("max_t", layer, g, b), max_t_ready, n)
                nc.tensor.transpose(dst[:, 0:S], neg_max[g][:, b, :], ident).then_inc(full[2], 1)

            def weigh(layer, g, u):
                quads, hd = FORM[layer]
                units = quads // 2
                b = u // units
                if u % units == 0:
                    claim(weighed_slot(layer, g), None, weighed_t_ready, att_rank(layer, g) * G + b + 1)
                pe.wait_ge(exp_ready, unit_rank(layer, g) + u + 1)
                for i in range(8):
                    h = head_at(layer, 2 * (u % units) + i // 4, i % 4)
                    cols = slice(h * (hd + 1), (h + 1) * (hd + 1))
                    last = mm(slot[weighed_slot(layer, g)][32 * (h % 4):32 * (h % 4) + hd + 1,
                                                           h // 4 * 128:(h // 4 + 1) * 128],
                              v_heads(layer, g)[:, b, cols], probs[u % 2][:, i // 4, i % 4 * 128:(i % 4 + 1) * 128],
                              start=True, stop=True)
                last.then_inc(weighed, 1)

            def weighed_to_tok(layer, g, b):
                n = att_rank(layer, g) * G + b + 1
                pe.wait_ge(weighed_t_ready, n)
                dst = claim(2, ("weighed", layer, g, b), att_ready, n)
                for c in range(FORM[layer][0]):
                    last = nc.tensor.transpose(dst[:, c * 128:(c + 1) * 128], weighed_t[:, c * 128:(c + 1) * 128], ident)
                last.then_inc(full[2], 1)

            def attend(layer, g, b):
                units = FORM[layer][0] // 2
                if b == 0:
                    maxima_to_t(layer, g, 0)
                if b + 1 < G:
                    maxima_to_t(layer, g, b + 1)
                for u in range(units * b, units * (b + 1)):
                    s = 4 + u % 2
                    pe.wait_ge(max_t_ready, att_rank(layer, g) * G + b + 1)
                    dst = claim(s, ("scores_t", layer, g, u), exp_ready, unit_rank(layer, g) + u + 1)
                    for i in range(2):
                        quad = 2 * (u % units) + i
                        mm(dst[:, i, :], quad_ones_b[:, quad, :],
                           max_t[g][:, b % 2, :, :].rearrange("p a b -> p (a b)"), start=True, stop=False)
                        for j in range(4):
                            h = head_at(layer, quad, j)
                            last = mm(dst[:, i, j * 128:(j + 1) * 128], head_of(k_stack[g], layer, h, b),
                                      head_of(q_stack[g], layer, h, b), start=False, stop=j == 3)
                    last.then_inc(full[s], 1)
                    if u == 0:
                        pe.wait_ge(v_ready, att_rank(layer, g) + 1)
                    else:
                        weigh(layer, g, u - 1)
                if b + 2 < G:
                    scores(layer, g, b + 2)
                if b:
                    weighed_to_tok(layer, g, b - 1)
                if b == G - 1:
                    weigh(layer, g, units * G - 1)

            def att_to_t(layer, g):
                p = proj_rank(layer, g)
                pe.wait_ge(att_ready, (att_rank(layer, g) + 1) * G)
                to_t(att[g], claim(0, ("att_t", layer, g), att_t_ready, p + 1)).then_inc(full[0], 1)
                pe.wait_ge(att_t_ready, p + 1)

            def prepare1(g):
                pe.wait_ge(x_pe_ready, g + 1)
                to_t(x_pe[g], claim(2, ("x_t", 1, g), x_t_ready[g], 1)).then_inc(full[2], 1)
                pe.wait_ge(x_t_ready[g], 1)
                a = att_rank(1, g)
                if g == 0:
                    to_t(x_pe[g], slot[3])
                mm(claim(1, ("wk", 1, g), k_parts_ready, a + 1), W["wk"], x_t[g][:, :],
                   start=True, stop=True).then_inc(full[1], 1)
                mm(claim(0, ("wq", 1, g), q_parts_ready, a + 1), W["wq"], x_t[g][:, :],
                   start=True, stop=True).then_inc(full[0], 1)
                by_token(claim(2, ("wv", 1, g), v_ready, a + 1), (x_t[g], W["wv"])).then_inc(full[2], 1)

            def project1(g):
                att_to_t(1, g)
                by_token(claim(1, ("sum", 1, g), sum_ready[g], 1), (att_t[g], W["wo"])).then_inc(full[1], 1)

            def keys2(g):
                a = att_rank(2, g)
                if g == 0:
                    pe.wait_ge(loaded["cross"], 16)
                pe.wait_ge(ctx_loaded[g], 32)
                dst = claim(0, ("wk", 2, g), k_parts_ready, a + 1)
                for c in range(2):
                    last = mm(dst, W["w_src"][:, c * 256:c * 256 + 128], ctx_sb[g][:, c, :],
                              start=c == 0, stop=c == 1)
                last.then_inc(full[0], 1)
                by_token(claim(1, ("wv", 2, g), v_ready, a + 1),
                         *((ctx_sb[g][:, c, :], W["w_src"][:, c * 256 + 128:c * 256 + 256]) for c in range(2))
                         ).then_inc(full[1], 1)

            def prepare2(g):
                a = att_rank(2, g)
                x_to_t(2, g)
                pe.wait_ge(x_t_ready[g], 2)
                mm(claim(0, ("wq", 2, g), q_parts_ready, a + 1), W["w_tgt"], x_t[g][:, :],
                   start=True, stop=True).then_inc(full[0], 1)

            def project2(g):
                att_to_t(2, g)
                by_token(claim(1, ("sum", 2, g), sum_ready[g], 2),
                         (x_t[g], W["w_out"][:, 0:128]), (att_t[g], W["w_out"][:, 128:256])).then_inc(full[1], 1)

            def gate_rows(layer, g):
                m = moe_rank(layer, g)
                pe.wait_ge(gates_ready, m + 1)
                to_t(gates[g], claim(1, ("gates_t", layer, g), gate_parts_ready, m + 1)
                     ).then_inc(full[1], 1)

            def route(layer, g):
                experts = MOE[layer][0]
                name = "router0" if layer == 3 else "router1"
                if g == 0:
                    pe.wait_ge(loaded["moe0" if layer == 3 else "moe1"], 16)
                x_to_t(layer, g)
                pe.wait_ge(x_t_ready[g], layer)
                dst = claim(0, ("logits", layer, g), logits_ready, moe_rank(layer, g) + 1)
                for b in range(G):
                    last = mm(dst[:, b * experts:(b + 1) * experts], x_t[g][:, b * S:(b + 1) * S], W[name],
                              start=True, stop=True)
                last.then_inc(full[0], 1)

            def down(layer, g, k, w):
                blocks = MOE[layer][1]
                if k == 0:
                    claim(3, None, moe_t_ready, moe_rank(layer, g) + 1)
                pe.wait_ge(hidden_ready, block_rank(layer, g) + k + 1)
                mm(slot[3], w[:, k * 128:(k + 1) * 128], hidden[k % 3][:, :],
                   start=k == 0, stop=k == blocks - 1).then_inc(hidden_used, 1)

            def moe_to_tok(layer, g):
                pe.wait_ge(moe_t_ready, moe_rank(layer, g) + 1)
                dst = claim(0, ("sum", layer, g), sum_ready[g], layer)
                for b in range(G):
                    last = nc.tensor.transpose(dst[:, b * S:(b + 1) * S], moe_t[g][:, b * S:(b + 1) * S], ident)
                last.then_inc(full[0], 1)

            def block3(g, k):
                first, s = block_rank(3, g), 4 + k % 2
                dst = claim(s, ("up", 3, g, k), hidden_ready, first + k + 1)
                for i, name in enumerate(("wg0", "wu0")):
                    last = mm(dst[:, i, :], W[name][:, k * 128:(k + 1) * 128], x_t[g][:, :], start=True, stop=True)
                last.then_inc(full[s], 1)
                if k == 0:
                    pe.wait_ge(gate_parts_ready, moe_rank(3, g) + 1)
                else:
                    mm(claim(2, ("gate", 3, g, k), hidden_ready, first + k + 1),
                       spread_b[0:96, 4 * (k - 1):4 * k, :].rearrange("p e m -> p (e m)"), gate_parts[g][:, :],
                       start=True, stop=True).then_inc(full[2], 1)
                    down(3, g, k - 1, W["wd0"])
                if k == A_BLOCKS - 1:
                    down(3, g, k, W["wd0"])

            def block6(g, k):
                first, blocks, per = block_rank(6, g), MOE[6][1], F_I // 128
                e, s = k // per, 4 + k % 2

                def gate(e):
                    s = e % 2
                    mm(claim(s, ("gate", 6, g, e), x_gated_ready, g * F_E + e + 1), sel32_b[0:96, e, :],
                       gate_parts[g][:, :], start=True, stop=True).then_inc(full[s], 1)

                dst = claim(s, ("up", 6, g, k), hidden_ready, first + k + 1)
                mm(dst[:, 0, :], W["w1"][:, k * 128:(k + 1) * 128], x_t[g][:, :], start=True, stop=True)
                if k == 0:
                    pe.wait_ge(gate_parts_ready, moe_rank(6, g) + 1)
                    gate(0)
                if k % per == 0:
                    if e + 1 < F_E:
                        gate(e + 1)
                    pe.wait_ge(x_gated_ready, g * F_E + e + 1)
                mm(dst[:, 1, :], W["w3"][:, k * 128:(k + 1) * 128], x_gated[g][e % 2],
                   start=True, stop=True).then_inc(full[s], 1)
                if k:
                    down(6, g, k - 1, W["w2"])
                if k == blocks - 1:
                    down(6, g, k, W["w2"])

            def mamba_in(g):
                if g == 0:
                    pe.wait_ge(loaded["mamba"], 16)
                x_to_t(4, g)
                pe.wait_ge(x_t_ready[g], 4)
                for s in range(2):
                    mm(claim(s, ("in", g, s), padded_ready, 2 * g + s + 1), W["w_in"][:, s * 128:(s + 1) * 128],
                       x_t[g][:, :], start=True, stop=True).then_inc(full[s], 1)

            def mamba_dt(g):
                pe.wait_ge(u_ready, g + 1)
                mm(claim(2, ("dt_low", g), dt_low_ready, g + 1)[0:RANK, :], W["w_dtlow"], u_t[g],
                   start=True, stop=True).then_inc(full[2], 1)
                mm(claim(1, ("bc", g), bc_parts_ready, g + 1)[0:96, :], W["w_bc"], u_t[g],
                   start=True, stop=True).then_inc(full[1], 1)
                pe.wait_ge(dt_low_ready, g + 1)
                mm(claim(0, ("dt", g), dt_exp_ready, g + 1), W["w_dt"][0:RANK, :], dt_low[:, :],
                   start=True, stop=True).then_inc(full[0], 1)

            def chunk(g, c):
                if c == 0:
                    pe.wait_ge(bc_parts_ready, g + 1)
                for kind in range(2):
                    unit, s = 2 * c + kind, 4 + kind
                    dst = claim(s, ("bc", g, unit), bc_used, g * NSTATE + unit + 1)
                    for i in range(NS):
                        last = mm(dst[:, i, :], sel32_b[0:96, kind * NSTATE + c * NS + i, :], bc_parts[g][:, :],
                                  start=True, stop=True)
                    last.then_inc(full[s], 1)

            def project4(g):
                pe.wait_ge(y_ready, g + 1)
                pe.wait_ge(z_ready, g + 1)
                by_token(claim(0, ("sum", 4, g), sum_ready[g], 4),
                         (y_t[g], W["w_mo"][:, 0:128]), (z_t[g], W["w_mo"][:, 128:256])).then_inc(full[0], 1)

            pe.wait_ge(loaded["first"], 16)
            for step, layer, g, n in PLAN:
                if step == "prepare":
                    {1: prepare1, 2: prepare2, 5: lambda g: x_to_t(5, g)}[layer](g)
                elif step == "keys":
                    keys2(g)
                elif step == "scores":
                    if (layer, g) == (1, 0):
                        pe.wait_ge(pool_consts, POOL_CONSTS)
                        pe.wait_ge(vector_consts, VECTOR_CONSTS)
                    pe.wait_ge(stacks_ready[g], 16 * stack_loads(layer))
                    scores(layer, g, 0)
                    scores(layer, g, 1)
                elif step == "attend":
                    attend(layer, g, n)
                elif step == "route":
                    route(layer, g)
                elif step == "gate_rows":
                    gate_rows(layer, g)
                elif step == "block":
                    (block3 if layer == 3 else block6)(g, n)
                elif step == "mamba_in":
                    mamba_in(g)
                elif step == "mamba_dt":
                    mamba_dt(g)
                elif step == "chunk":
                    chunk(g, n)
                elif step == "finish" and layer in FORM:
                    weighed_to_tok(layer, g, G - 1)
                elif step == "project" and layer in MOE:
                    moe_to_tok(layer, g)
                elif step == "project" and layer != 5:
                    {1: project1, 2: project2, 4: project4}[layer](g)

        @block.vector
        def _(dve):
            v = nc.vector
            steps = [0]

            def then(instruction):
                steps[0] += 1
                instruction.then_inc(vector_step, 1)
                dve.wait_ge(vector_step, steps[0])

            def constants():
                v.tensor_copy(quad_ones_b[:, :, :], W["quad"].unsqueeze(2).broadcast_to([128, NQ, 128])
                              ).then_inc(vector_consts, 1)
                v.tensor_copy(sel32_b[:, :, :], W["sel32"].unsqueeze(2).broadcast_to([128, 32, 128])
                              ).then_inc(vector_consts, 1)
                v.tensor_copy(spread_b[:, :, :], W["sel32"][:, 0:A_E].unsqueeze(2).broadcast_to([128, A_E, 32])
                              ).then_inc(vector_consts, 1)
                dve.wait_ge(loaded["ik"], 16)
                v.tensor_scalar(fk_rows[:, :], R["fk"], 0.0, W["fk_row"], ALU.is_equal, ALU.mult
                                ).then_inc(vector_consts, 1)
                v.tensor_scalar(ik_rows[:, :], ik_row_sb, -1.0, W["ik_row"], ALU.add, ALU.mult
                                ).then_inc(vector_consts, 1)

            def cross_constants():
                dve.wait_ge(vector_consts, VECTOR_CONSTS)
                dve.wait_ge(loaded["cross"], 16)
                then(v.tensor_copy(b_parts[:, 0:1], W["b1"]))
                then(v.tensor_tensor(b_rest[:, :], W["b1"], b_parts[:, 0:1], ALU.subtract))
                then(v.tensor_copy(b_parts[:, 1:2], b_rest[:, :]))
                then(v.tensor_tensor(b_parts[:, 2:3], b_rest[:, :], b_parts[:, 1:2], ALU.subtract))
                then(v.tensor_tensor(b_parts[:, :], b_parts[:, :], W["b_rows"], ALU.mult))
                then(v.tensor_reduce(b_col[:, :], b_parts[:, :], AX, ALU.add))
                v.tensor_scalar(ik_rows[:, :], ik_rows[:, :], b_col[:, :], None, ALU.add).then_inc(ik_rows_ready, 1)

            def split_parts(src, scale, rest, dst):
                high, middle_, low = dst
                if scale == 1.0:
                    then(v.tensor_copy(high, src))
                    then(v.tensor_tensor(rest, src, high, ALU.subtract))
                else:
                    then(v.tensor_scalar(high, src, scale, None, ALU.mult))
                    then(v.scalar_tensor_tensor(rest, src, scale, high, ALU.mult, ALU.subtract))
                then(v.tensor_copy(middle_, rest))
                return v.tensor_tensor(low, rest, middle_, ALU.subtract)

            def prepare1(g):
                if g == 0:
                    dve.wait_ge(loaded["first"], 16)
                dve.wait_ge(x_loaded[g], 16)
                v.tensor_tensor(x_pe[g][:, :, :], x_tok[g][:, :, :],
                                W["pe"].unsqueeze(1).broadcast_to([128, G, D]), ALU.add).then_inc(x_pe_ready, 1)
                dve.wait_ge(full[1], nth["wk", 1, g])
                then(v.tensor_scalar(k_t[g][:, :], slot[1], W["bk"], None, ALU.add))
                split_parts(k_t[g][:, :], 1.0, k_t[g][:, :], k_parts[g]).then_inc(k_parts_ready, 1)
                dve.wait_ge(full[0], nth["wq", 1, g])
                then(v.tensor_scalar(q_t[g][:, :], slot[0], W["bq"], float(D // A_HEADS) ** -0.5, ALU.add, ALU.mult))
                split_parts(q_t[g][:, :], 1.0, q_t[g][:, :], q_parts[g]).then_inc(q_parts_ready, 1)
                dve.wait_ge(full[2], nth["wv", 1, g])
                if g == 0:
                    dve.wait_ge(loaded["rows"], 16)
                    dve.wait_ge(pool_consts, POOL_CONSTS)
                hd = D // A_HEADS
                v.tensor_tensor(v_heads_a[g][:, :, :].rearrange("p b (h e) -> p b h e", e=hd + 1)[:, :, :, 0:hd],
                                slot[2].rearrange("p (b h e) -> p b h e", b=G, e=hd),
                                R["bv"].rearrange("p (h e) -> p h e", e=hd).unsqueeze(1)
                                .broadcast_to([128, G, A_HEADS, hd]), ALU.add).then_inc(v_ready, 1)
                if g == 0:
                    constants()

            def values_x(g):
                hd = D // X_HEADS
                return (v_heads_x[g][:, :, :].rearrange("p b (h e) -> p b h e", e=hd + 1)[:, :, :, 0:hd], hd)

            def keys2(g):
                if g == 0:
                    cross_constants()
                dve.wait_ge(res_ready, g + 1)
                at = slice(g * T, (g + 1) * T)
                dve.wait_ge(full[0], nth["wk", 2, g])
                then(v.scalar_tensor_tensor(k_t[g][:, :], slot[0], W["b_srck"], R["fk"][:, at], ALU.add, ALU.mult))
                split_parts(k_t[g][:, :], 1.0, k_t[g][:, :], k_parts_2[g]).then_inc(k_parts_ready, 1)
                dve.wait_ge(full[1], nth["wv", 2, g])
                then(v.tensor_tensor(x_pe[g][:, :, :], slot[1].rearrange("p (b e) -> p b e", b=G),
                                     R["b_srcv"].unsqueeze(1).broadcast_to([128, G, D]), ALU.add))
                if g == 0:
                    dve.wait_ge(loaded["masks"], 16)
                dst, hd = values_x(g)
                v.tensor_tensor(dst, x_pe[g][:, :, :].rearrange("p b (h e) -> p b h e", e=hd),
                                W["fk_tok"][:, g * G:(g + 1) * G].unsqueeze(2).unsqueeze(3)
                                .broadcast_to([128, G, X_HEADS, hd]), ALU.mult).then_inc(v_ready, 1)

            def prepare2(g):
                at = slice(g * T, (g + 1) * T)
                dve.wait_ge(full[0], nth["wq", 2, g])
                then(v.scalar_tensor_tensor(q_t[g][:, :], slot[0], W["b_tgt"], R["fk"][:, at],
                                            ALU.add, ALU.mult))
                split_parts(q_t[g][:, :], float(D // X_HEADS) ** -0.5, q_t[g][:, :], q_parts[g]
                            ).then_inc(q_parts_ready, 1)

            def prepare5(g):
                dve.wait_ge(ctx_loaded[g], 32)
                dve.wait_ge(x_tok_ready[g], 4)
                split_parts(ctx_sb[g][:, 0, :], 1.0, k_t[g][:, :], k_parts[g]).then_inc(k_parts_ready, 1)
                dst, hd = values_x(g)
                v.tensor_copy(dst, v_ctx_sb[g][:, :, :].rearrange("p b (h e) -> p b h e", e=hd)).then_inc(v_ready, 1)
                dve.wait_ge(x_t_ready[g], 5)
                split_parts(x_t[g][:, :], float(D // X_HEADS) ** -0.5, q_t[g][:, :], q_parts[g]
                            ).then_inc(q_parts_ready, 1)

            def maxima(layer, g, b):
                quads = FORM[layer][0]
                by_quad = neg_max[g][:, b, :].rearrange("p (q r) -> p q r", q=NQ)[:, 0:quads, :]
                for quad in range(quads):
                    s = quad % 2
                    dve.wait_ge(full[s], nth["scores", layer, g, b, quad])
                    v.tensor_reduce(by_quad[:, quad, 0:4], slot[s].rearrange("p (j k) -> p j k", j=4), AX,
                                    ALU.max, negate=True).then_inc(max_ready, 1)
                dve.wait_ge(max_ready, max_rank(layer, g) + quads * (b + 1))
                then(v.tensor_copy(neg_high[:, 0:quads, :], by_quad[:, :, 0:4]))
                v.tensor_tensor(by_quad[:, :, 4:8], by_quad[:, :, 0:4], neg_high[:, 0:quads, :],
                                ALU.subtract).then_inc(lows_ready, 1)
                dve.wait_ge(lows_ready, att_rank(layer, g) * G + b + 1)

            def maxima_to_rows(layer, g, b):
                dve.wait_ge(full[2], nth["max_t", layer, g, b])
                if b >= 2:
                    u = FORM[layer][0] // 2 * (b - 1) - 1
                    dve.wait_ge(full[4 + u % 2], nth["scores_t", layer, g, u])
                v.tensor_tensor(max_t[g][:, b % 2, :, :], slot[2][:, 0:S].unsqueeze(1).broadcast_to([128, 4, S]),
                                W["max_row"].unsqueeze(2).broadcast_to([128, 4, S]), ALU.mult
                                ).then_inc(max_t_ready, 1)

            def normalize(layer, g, b):
                quads, hd = FORM[layer]
                heads = 4 * quads
                dve.wait_ge(full[2], nth["weighed", layer, g, b])
                sums = slot[2][:, 0:heads * 32].rearrange("p (h e) -> p h e", e=32)
                then(v.reciprocal(rec[:, 0:heads].unsqueeze(2), sums[:, :, hd:hd + 1]))
                v.tensor_tensor(att[g][:, b, :].rearrange("p (h e) -> p h e", e=hd), sums[:, :, 0:hd],
                                rec[:, 0:heads].unsqueeze(2).broadcast_to([128, heads, hd]),
                                ALU.mult).then_inc(att_ready, 1)

            def attend(layer, g, b):
                if b == 0:
                    maxima_to_rows(layer, g, 0)
                if b + 1 < G:
                    maxima_to_rows(layer, g, b + 1)
                if b + 2 < G:
                    maxima(layer, g, b + 2)
                if b:
                    normalize(layer, g, b - 1)

            def statistics(src, g):
                for b in range(G):
                    last = v.bn_stats(stats[:, b, :], src[g][:, b, :])
                then(last)
                for b in range(G):
                    last = v.bn_aggr(mean_var[g][:, b, :], stats[:, b, :])
                then(last)
                v.tensor_scalar(var_eps[g][:, :], mean_var[g][:, :, 1], LN_EPS, None, ALU.add
                                ).then_inc(var_ready[g], 1)

            def normed(layer, g, dst, second=False):
                dve.wait_ge(rstd_ready[g], norm_rank(layer, second) + 1)
                for b in range(G):
                    last = v.tensor_scalar(dst[g][:, b, :], h_tok[g][:, b, :], mean_var[g][:, b, 0:1],
                                           rstd[g][:, b:b + 1], ALU.subtract, ALU.mult)
                return last

            def first_norm(g):
                then(normed(1, g, h_tok))
                then(v.tensor_tensor(h_tok[g][:, :, :], h_tok[g][:, :, :],
                                     R["gamma"].unsqueeze(1).broadcast_to([128, G, D]), ALU.mult))
                then(v.tensor_tensor(h_tok[g][:, :, :], h_tok[g][:, :, :], x_tok[g][:, :, :], ALU.add))
                statistics(h_tok, g)

            def add_residual(layer, g, s, residual):
                dve.wait_ge(full[s], nth["sum", layer, g])
                v.tensor_tensor(h_tok[g][:, :, :], slot[s].rearrange("p (b e) -> p b e", b=G), residual[:, :, :],
                                ALU.add).then_inc(sum_ready[g], 1)
                dve.wait_ge(sum_ready[g], layer)
                statistics(h_tok, g)

            def project(layer, g):
                if layer == 5:
                    dve.wait_ge(att_ready, (att_rank(5, g) + 1) * G)
                    v.tensor_tensor(h_tok[g][:, :, :], att[g][:, :, :], x_tok[g][:, :, :], ALU.add
                                    ).then_inc(sum_ready[g], 1)
                    dve.wait_ge(sum_ready[g], 5)
                    statistics(h_tok, g)
                elif layer in (1, 2):
                    dve.wait_ge(res_ready, proj_rank(layer, g) + 1)
                    add_residual(layer, g, 1, x_res[g])
                else:
                    add_residual(layer, g, 0, x_tok[g])

            def split(s, label, dst, done):
                dve.wait_ge(full[s], nth[label])
                x96 = slot[s][0:96, :]
                then(v.tensor_copy(dst[0:96, :], x96))
                then(v.tensor_tensor(residue[0:96, :], x96, dst[0:96, :], ALU.subtract))
                v.tensor_copy(dst[32:64, :], residue[32:64, :])
                then(v.tensor_copy(middle[64:96, :], residue[64:96, :]))
                v.tensor_tensor(dst[64:96, :], residue[64:96, :], middle[64:96, :], ALU.subtract).then_inc(done, 1)

            def route(layer, g):
                experts = MOE[layer][0]
                m = moe_rank(layer, g)
                lg = logits[:, :, 0:experts]
                full_shape = [128, G, experts]
                dve.wait_ge(full[0], nth["logits", layer, g])
                v.tensor_copy(lg, slot[0][:, 0:G * experts].rearrange("p (b e) -> p b e", b=G)
                              ).then_inc(logits_ready, 1)
                dve.wait_ge(logits_ready, m + 1)
                for b in range(G):
                    last = v.max(top8[:, b, :], logits[:, b, 0:experts])
                then(last)
                v.tensor_tensor(gate_exp[:, :, 0:experts], lg, top8[:, :, 0:1].broadcast_to(full_shape),
                                ALU.subtract).then_inc(gate_shift_ready, 1)
                for b in range(G):
                    last = v.max_index(top_i[:, b, :], top8[:, b, :], logits[:, b, 0:experts])
                then(last)
                then(v.tensor_copy(top_f[:, :, :], top_i[:, :, 0:2]))
                for i in range(2):
                    last = v.tensor_tensor(picked[:, i, :, 0:experts],
                                           W["iota"][:, 0:experts].unsqueeze(1).broadcast_to(full_shape),
                                           top_f[:, :, i:i + 1].broadcast_to(full_shape), ALU.is_equal)
                then(last)
                then(v.tensor_tensor(picked[:, 0, :, 0:experts], picked[:, 0, :, 0:experts],
                                     picked[:, 1, :, 0:experts], ALU.add))
                dve.wait_ge(gate_exp_ready, m + 1)
                ge = gate_exp[:, :, 0:experts]
                then(v.tensor_reduce(gate_sum[:, 0, :], ge, AX, ALU.add))
                then(v.reciprocal(gate_sum[:, 1, :], gate_sum[:, 0, :]))
                then(v.tensor_tensor(lg, ge, gate_sum[:, 1, :].unsqueeze(2).broadcast_to(full_shape), ALU.mult))
                then(v.tensor_tensor(lg, lg, picked[:, 0, :, 0:experts], ALU.mult))
                then(v.tensor_reduce(gate_sum[:, 2, :], lg, AX, ALU.add))
                if layer == 3:
                    then(v.tensor_scalar(gate_sum[:, 2, :], gate_sum[:, 2, :], 1e-9, None, ALU.add))
                then(v.reciprocal(gate_sum[:, 3, :], gate_sum[:, 2, :]))
                v.tensor_tensor(gates[g][:, :, :].rearrange("p b (c e) -> p b c e", c=3)
                                [:, :, :, 0:experts],
                                lg.unsqueeze(2).broadcast_to([128, G, 3, experts]),
                                gate_sum[:, 3, :].unsqueeze(2).unsqueeze(3).broadcast_to([128, G, 3, experts]),
                                ALU.mult).then_inc(gates_ready, 1)

            def block3(g, k):
                first = block_rank(3, g)
                n = first + k
                dve.wait_ge(silu_ready, n + 1)
                if n >= 3:
                    dve.wait_ge(hidden_used, n - 2)
                if k == 0:
                    v.tensor_tensor(hidden[k % 3][:, :], silu[k % 2][:, :], slot[4][:, 1, :],
                                    ALU.mult).then_inc(hidden_ready, 1)
                else:
                    if k >= 2:
                        dve.wait_ge(hidden_ready, n)
                    then(v.tensor_tensor(product[g], silu[k % 2][:, :], slot[4 + k % 2][:, 1, :], ALU.mult))
                    dve.wait_ge(full[2], nth["gate", 3, g, k])
                    v.tensor_tensor(hidden[k % 3][:, :], product[g], slot[2], ALU.mult
                                    ).then_inc(hidden_ready, 1)

            def block6(g, k):
                first, per = block_rank(6, g), F_I // 128

                def gate_x(e):
                    s = e % 2
                    dve.wait_ge(full[s], nth["gate", 6, g, e])
                    v.tensor_tensor(x_gated[g][e % 2], x_t[g][:, :], slot[s], ALU.mult
                                    ).then_inc(x_gated_ready, 1)

                if k == 0:
                    gate_x(0)
                n = first + k
                if k % per == 0 and k // per + 1 < F_E:
                    gate_x(k // per + 1)
                dve.wait_ge(silu_ready, n + 1)
                dve.wait_ge(full[4 + k % 2], nth["up", 6, g, k])
                if n >= 3:
                    dve.wait_ge(hidden_used, n - 2)
                v.tensor_tensor(hidden[k % 3][:, :], silu[k % 2][:, :], slot[4 + k % 2][:, 1, :], ALU.mult
                                ).then_inc(hidden_ready, 1)

            def mamba_in(g):
                dve.wait_ge(loaded["mamba"], 16)
                if g == 0:
                    dve.wait_ge(scalar_consts, 1)
                    v.tensor_scalar(neg_a[:, :], a_exp[:, :], -1.0, None, ALU.mult).then_inc(neg_a_ready, 1)
                for s, name, out_, done in ((0, "k_x", conv_x[g], conv_x_ready), (1, "k_z", conv_z[g], conv_z_ready)):
                    dve.wait_ge(padded_ready, 2 * g + s + 1)
                    out3 = out_.rearrange("p (b l) -> p b l", b=G)
                    then(v.tensor_scalar(out3, padded[s][:, :, 0:S], W[name][:, 0:1], None, ALU.mult))
                    for tap in range(1, 4):
                        last = v.scalar_tensor_tensor(out3, padded[s][:, :, tap:tap + S], W[name][:, tap:tap + 1],
                                                      out3, ALU.mult, ALU.add)
                        if tap < 3:
                            then(last)
                    last.then_inc(done, 1)

            def mamba_dt(g):
                split(1, ("bc", g), bc_parts[g], bc_parts_ready)
                dve.wait_ge(dt_exp_ready, g + 1)
                v.tensor_scalar(dt_one[g], dt_exp[g], 1.0, None, ALU.add).then_inc(dt_one_ready, 1)
                dve.wait_ge(dt_one_ready, g + 1)
                then(v.tensor_scalar(dt_back[g], dt_one[g], -1.0, None, ALU.add))
                then(v.tensor_scalar(dt_zero[g], dt_back[g], 0.0, None, ALU.is_equal))
                then(v.tensor_tensor(dt_back[g], dt_back[g], dt_zero[g], ALU.add))
                then(v.reciprocal(dt_div[g], dt_back[g]))
                then(v.tensor_tensor(dt_div[g], dt_div[g], dt_exp[g], ALU.mult))

            def mamba_ln(g):
                dve.wait_ge(dt_ln_ready, g + 1)
                then(v.tensor_tensor(dt_zero[g], dt_ln[g], dt_zero[g], ALU.add))
                then(v.tensor_tensor(dt_div[g], dt_div[g], dt_zero[g], ALU.mult))
                v.tensor_tensor(delta[g], dt_div[g], dt_relu[g], ALU.add).then_inc(delta_ready, 1)
                dve.wait_ge(delta_ready, g + 1)
                then(v.tensor_tensor(delta_u[g], delta[g], u_t[g], ALU.mult))

            def chunk(g, c):
                n = g * CHUNKS + c
                if c:
                    dve.wait_ge(scanned, n)
                dve.wait_ge(full[4], nth["bc", g, 2 * c])
                v.tensor_tensor(drive[g], slot[4], delta_u[g].unsqueeze(1).broadcast_to([128, NS, T]), ALU.mult
                                ).then_inc(bc_used, 1)
                dve.wait_ge(bc_used, 2 * n + 1)
                dve.wait_ge(decay_ready, n + 1)
                then(v.memset(decay[c % 2][:, :, :].rearrange("p n (b l) -> p n b l", b=G)[:, :, :, 0:1], 0.0))
                v.tensor_tensor_scan(state[g].rearrange("p n l -> p (n l)"),
                                     decay[c % 2][:, :, :].rearrange("p n l -> p (n l)"),
                                     drive[g].rearrange("p n l -> p (n l)"), 0.0,
                                     ALU.mult, ALU.add).then_inc(scanned, 1)
                dve.wait_ge(scanned, n + 1)
                if n >= 2:
                    dve.wait_ge(y_sum_ready, n - 1)
                dve.wait_ge(full[5], nth["bc", g, 2 * c + 1])
                v.tensor_tensor(read[g][c % 2], slot[5], state[g], ALU.mult).then_inc(bc_used, 1)

            def finish4(g):
                dve.wait_ge(y_sum_ready, (g + 1) * CHUNKS)
                v.scalar_tensor_tensor(y_t[g], u_t[g], W["d_skip"], y_sum[g], ALU.mult, ALU.add
                                       ).then_inc(y_ready, 1)

            for step, layer, g, n in PLAN:
                if step == "prepare":
                    {1: prepare1, 2: prepare2, 5: prepare5}[layer](g)
                elif step == "keys":
                    keys2(g)
                elif step == "scores":
                    maxima(layer, g, 0)
                    maxima(layer, g, 1)
                elif step == "attend":
                    attend(layer, g, n)
                elif step == "route":
                    route(layer, g)
                elif step == "gate_rows":
                    split(1, ("gates_t", layer, g), gate_parts[g], gate_parts_ready)
                elif step == "block":
                    (block3 if layer == 3 else block6)(g, n)
                elif step == "mamba_in":
                    mamba_in(g)
                elif step == "mamba_dt":
                    mamba_dt(g)
                elif step == "mamba_ln":
                    mamba_ln(g)
                elif step == "chunk":
                    chunk(g, n)
                elif step == "finish":
                    if layer == 4:
                        finish4(g)
                    elif layer in FORM:
                        normalize(layer, g, G - 1)
                elif step == "project":
                    project(layer, g)
                elif step == "norm" and layer == 1:
                    first_norm(g)
                else:
                    normed(layer, g, x_tok, second=layer == 1).then_inc(x_tok_ready[g], 1)

        @block.scalar
        def _(act):
            sc = nc.scalar

            def copy_x_t(layer, g):
                act.wait_ge(full[2], nth["x_t", layer, g])
                sc.copy(x_t[g][:, :], slot[2]).then_inc(x_t_ready[g], 1)

            def copy_weighed_t(layer, g, b):
                columns_ = FORM[layer][0] * 128
                act.wait_ge(weighed, unit_rank(layer, g) + FORM[layer][0] // 2 * (b + 1))
                if b:
                    act.wait_ge(full[2], nth["weighed", layer, g, b - 1])
                sc.copy(weighed_t[:, 0:columns_], slot[weighed_slot(layer, g)][:, 0:columns_]
                        ).then_inc(weighed_t_ready, 1)

            def exponentials(layer, g, b):
                first, units = unit_rank(layer, g), FORM[layer][0] // 2
                for u in range(units * b, units * (b + 1)):
                    s = 4 + u % 2
                    act.wait_ge(full[s], nth["scores_t", layer, g, u])
                    if first + u >= 2:
                        act.wait_ge(weighed, first + u - 1)
                    sc.activation(probs[u % 2][:, :, :], slot[s], ACT.Exp).then_inc(exp_ready, 1)
                    if b and u == units * b:
                        copy_weighed_t(layer, g, b - 1)

            def copy_att_t(layer, g):
                act.wait_ge(full[0], nth["att_t", layer, g])
                sc.copy(att_t[g][:, :], slot[0]).then_inc(att_t_ready, 1)

            def gate_exponentials(layer, g):
                experts, m = MOE[layer][0], moe_rank(layer, g)
                act.wait_ge(gate_shift_ready, m + 1)
                sc.activation(gate_exp[:, :, 0:experts], gate_exp[:, :, 0:experts], ACT.Exp
                              ).then_inc(gate_exp_ready, 1)

            def block_silu(layer, g, k):
                n = block_rank(layer, g) + k
                act.wait_ge(full[4 + k % 2], nth["up", layer, g, k])
                if n >= 2:
                    act.wait_ge(hidden_ready, n - 1)
                sc.activation(silu[k % 2][:, :], slot[4 + k % 2][:, 0, :], ACT.Silu).then_inc(silu_ready, 1)

            def copy_moe_t(layer, g):
                act.wait_ge(hidden_used, block_rank(layer, g) + MOE[layer][1])
                sc.copy(moe_t[g], slot[3]).then_inc(moe_t_ready, 1)

            def mamba_in(g):
                if g == 0:
                    act.wait_ge(vector_consts, VECTOR_CONSTS)
                    act.wait_ge(loaded["mamba"], 16)
                    sc.activation(a_exp[:, :], W["a_log"], ACT.Exp).then_inc(scalar_consts, 1)
                copy_x_t(4, g)
                for s, convolved in enumerate((conv_x_ready, conv_z_ready)):
                    if g:
                        act.wait_ge(convolved, g)
                    act.wait_ge(full[s], nth["in", g, s])
                    sc.copy(padded[s][:, :, 1:S + 1], slot[s].rearrange("p (b l) -> p b l", b=G)
                            ).then_inc(padded_ready, 1)
                act.wait_ge(conv_x_ready, g + 1)
                sc.activation(u_t[g], conv_x[g], ACT.Gelu, bias=W["b_x"]).then_inc(u_ready, 1)
                act.wait_ge(conv_z_ready, g + 1)
                sc.activation(z_t[g], conv_z[g], ACT.Gelu, bias=W["b_z"]).then_inc(z_ready, 1)

            def mamba_dt(g):
                act.wait_ge(full[2], nth["dt_low", g])
                sc.copy(dt_low[:, :], slot[2][0:RANK, :]).then_inc(dt_low_ready, 1)
                act.wait_ge(full[0], nth["dt", g])
                sc.activation(dt_abs[g], slot[0], ACT.Abs, bias=W["b_dt"]).then_inc(scalar_step, 1)
                sc.activation(dt_relu[g], slot[0], ACT.Relu, bias=W["b_dt"])
                act.wait_ge(scalar_step, g + 1)
                sc.activation(dt_exp[g], dt_abs[g], ACT.Exp, scale=-1.0).then_inc(dt_exp_ready, 1)
                act.wait_ge(dt_one_ready, g + 1)
                sc.activation(dt_ln[g], dt_one[g], ACT.Ln).then_inc(dt_ln_ready, 1)

            def mamba_ln(g):
                act.wait_ge(delta_ready, g + 1)
                if g == 0:
                    act.wait_ge(neg_a_ready, 1)

            def chunk(g, c):
                n = g * CHUNKS + c
                if n >= 2:
                    act.wait_ge(scanned, n - 1)
                for i in range(NS):
                    last = sc.activation(decay[c % 2][:, i, :], delta[g], ACT.Exp,
                                         scale=neg_a[:, c * NS + i:c * NS + i + 1])
                last.then_inc(decay_ready, 1)

            for step, layer, g, n in PLAN:
                if step == "prepare":
                    copy_x_t(layer, g)
                elif step == "attend":
                    exponentials(layer, g, n)
                elif step == "route":
                    copy_x_t(layer, g)
                    gate_exponentials(layer, g)
                elif step == "block":
                    block_silu(layer, g, n)
                elif step == "mamba_in":
                    mamba_in(g)
                elif step == "mamba_dt":
                    mamba_dt(g)
                elif step == "mamba_ln":
                    mamba_ln(g)
                elif step == "chunk":
                    chunk(g, n)
                elif step == "finish" and layer in MOE:
                    copy_moe_t(layer, g)
                elif step == "finish" and layer in FORM:
                    copy_weighed_t(layer, g, G - 1)
                elif step == "project" and layer < 3:
                    copy_att_t(layer, g)

        @block.gpsimd
        def _(pool):
            p = nc.gpsimd
            steps = [0]

            def then(instruction):
                steps[0] += 1
                instruction.then_inc(pool_step, 1)
                pool.wait_ge(pool_step, steps[0])

            def deviations(layer, g, second=False):
                pool.wait_ge(var_ready[g], norm_rank(layer, second) + 1)
                p.tensor_tensor(rstd[g][:, :], var_eps[g][:, :], half[:, :], ALU.pow).then_inc(rstd_ready[g], 1)

            def plus_row(dst, src, row):
                return p.tensor_tensor(dst[:, :, :], src[:, :, :], R[row].unsqueeze(1).broadcast_to([128, G, D]), ALU.add)

            def chunk(g, c):
                pool.wait_ge(bc_used, 2 * (g * CHUNKS + c + 1))
                pair = y_sum[g] if c == 0 else y_pair[g]
                last = p.tensor_tensor(pair, read[g][c % 2][:, 0, :], read[g][c % 2][:, 1, :], ALU.add)
                if c:
                    then(last)
                    last = p.tensor_tensor(y_sum[g], y_sum[g], y_pair[g], ALU.add)
                last.then_inc(y_sum_ready, 1)
                pool.wait_ge(y_sum_ready, g * CHUNKS + c + 1)

            p.memset(ones_b[:, :], 1.0).then_inc(pool_consts, 1)
            p.memset(half[:, :], -0.5).then_inc(pool_consts, 1)
            for g in groups:
                p.memset(neg_max[g][:, :, :], 0.0).then_inc(pool_consts, 1)
                p.memset(v_heads_a[g][:, :, :], 1.0).then_inc(pool_consts, 1)
                p.memset(v_heads_x[g][:, :, :], 1.0).then_inc(pool_consts, 1)
                p.memset(gates[g][:, :, :], 0.0).then_inc(pool_consts, 1)
                p.memset(padded[g][:, :, :], 0.0).then_inc(pool_consts, 1)
            pool.wait_ge(pool_consts, POOL_CONSTS)
            for step, layer, g, n in PLAN:
                if step == "prepare" and layer == 1:
                    if g == 0:
                        pool.wait_ge(loaded["rows"], 16)
                    pool.wait_ge(x_pe_ready, g + 1)
                    then(plus_row(x_tok[g], x_tok[g], "beta"))
                    plus_row(x_res[g], x_pe[g], "bo").then_inc(res_ready, 1)
                elif step == "prepare" and layer == 2:
                    pool.wait_ge(x_tok_ready[g], 1)
                    plus_row(x_res[g], x_tok[g], "b_out").then_inc(res_ready, 1)
                elif step == "chunk":
                    chunk(g, n)
                elif step == "project":
                    deviations(layer, g)
                elif step == "norm" and layer == 1:
                    deviations(1, g, second=True)

        @block.sync
        def _(sp):
            where = dict(packed)

            def load(name):
                sp.dma_start(pack_sb[name][:, :], where[name]).then_inc(loaded[name], 16)

            def form_stacks(layer, g):
                k_stack_of(layer, g)
                q_stack_of(layer, g)

            def save(parts, saved, made):
                for i in range(3):
                    sp.dma_start(made[i].rearrange("d h t -> h d t"), parts[i]).then_inc(saved, 16)

            def constant_rows(stack_, g, src):
                sp.dma_start(stack_[g][CONST_ROW:CONST_ROW + 4, :, :], src.unsqueeze(1).broadcast_to([4, 8, T])
                             ).then_inc(stacks_ready[g], 16)

            def read_back(layer, g, stack_, source_of):
                hd = FORM[layer][1]
                for side in range(16 // hd):
                    row = 64 * side
                    for n in range(3):
                        src = source_of(n)[:, side * hd:(side + 1) * hd, :, :].rearrange("n d h t -> n d (h t)")
                        sp.dma_start(stack_[g][row:row + (3 - n) * hd, :, :], src).then_inc(stacks_ready[g], 16)
                        row += (3 - n) * hd

            def k_stack_of(layer, g):
                a = att_rank(layer, g)
                sp.wait_ge(k_parts_ready, a + 1)
                save((k_parts_2 if layer == 2 else k_parts)[g], k_parts_saved[g], k_made[a])
                if layer == 2:
                    sp.wait_ge(vector_consts, VECTOR_CONSTS)
                    sp.wait_ge(weighed, unit_rank(1, g) + FORM[1][0] // 2 * G)
                if layer == 5:
                    sp.wait_ge(ik_rows_ready, 1)
                if layer > 1:
                    constant_rows(k_stack, g, (fk_rows if layer == 2 else ik_rows)[CONST_ROW:CONST_ROW + 4,
                                                                                   g * T:(g + 1) * T])
                sp.wait_ge(k_parts_saved[g], 16 * 3 * att_nth(layer))
                read_back(layer, g, k_stack, lambda n: k_made[a][n:n + 1].broadcast_to([3 - n, 16, 8, T]))

            def q_stack_of(layer, g):
                a = att_rank(layer, g)
                sp.wait_ge(q_parts_ready, a + 1)
                save(q_parts[g], q_parts_saved[g], q_made[a])
                if layer > 1:
                    if (layer, g) == (2, 0):
                        sp.wait_ge(pool_consts, POOL_CONSTS)
                    constant_rows(q_stack, g, ones_b[CONST_ROW:CONST_ROW + 4, :])
                sp.wait_ge(q_parts_saved[g], 16 * 3 * att_nth(layer))
                read_back(layer, g, q_stack, lambda n: q_made[a][0:3 - n])

            sp.dma_start(x_tok[0][:, :, :], x[0:G].rearrange("b s d -> s b d")).then_inc(x_loaded[0], 16)
            load("first")
            sp.dma_start(rows_sb[:, :], rows.broadcast_to([128, rows_width])).then_inc(loaded["rows"], 16)
            sp.dma_start(ik_row_sb, ik_row.broadcast_to([128, B * S])).then_inc(loaded["ik"], 16)
            sp.dma_start(x_tok[1][:, :, :], x[G:2 * G].rearrange("b s d -> s b d")).then_inc(x_loaded[1], 16)
            form_stacks(1, 0)
            load("masks")
            load("cross")
            for g in groups:
                sp.dma_start(ctx_sb[g][:, :, :], ctx_t[:, :, g * T:(g + 1) * T].rearrange("c p t -> p c t")
                             ).then_inc(ctx_loaded[g], 16)
                sp.dma_start(v_ctx_sb[g][:, :, :], v_ctx[g * G:(g + 1) * G].rearrange("b s d -> s b d")
                             ).then_inc(ctx_loaded[g], 16)
            form_stacks(1, 1)
            load("moe0")
            for step, layer, g, _ in PLAN:
                if step == "keys":
                    k_stack_of(layer, g)
                elif step == "prepare" and layer > 1:
                    if layer == 5:
                        k_stack_of(layer, g)
                    q_stack_of(layer, g)
                    if (layer, g) == (2, 0):
                        load("mamba")
                    if (layer, g) == (2, 1):
                        load("moe1")
            for g in groups:
                sp.wait_ge(x_tok_ready[g], STAGE)
                sp.dma_start(out[g * G:(g + 1) * G].rearrange("b s d -> s b d"), x_tok[g][:, :, :]
                             ).then_inc(stored, 16)
            sp.wait_ge(stored, 16 * NG)
            for g in groups:
                sp.wait_ge(k_parts_saved[g], 16 * 3 * att_nth(STAGE))
                sp.wait_ge(q_parts_saved[g], 16 * 3 * att_nth(STAGE))


def lay_out(i):
    def rows_of(a):
        return np.ascontiguousarray(a, dtype=np.float32)

    def col(a):
        return a.reshape(-1, 1)

    def halves(a):
        return np.concatenate([a[:128], a[128:]], axis=1)

    p = np.arange(128)
    w_src, w_mo = i["L0_xattn_W_src"].T, i["L1_attn_W_out"]
    xproj = i["L1_attn_W_xproj"]
    w_dt = np.zeros((128, 128), np.float32)
    w_dt[:RANK] = i["L1_attn_W_dt"]
    per_block = lambda w: np.transpose(w.reshape(F_E, D, F_I // 128, 128), (3, 0, 2, 1)).reshape(128, -1)
    side = lambda w: np.transpose(w, (1, 0, 2)).reshape(D, -1)
    down0 = np.concatenate([i["L0_ffn_wd_s"].reshape(128, D), i["L0_ffn_wd_r"].reshape(-1, D)])
    a = {
        "ident": np.eye(128), "max_row": (p[:, None] % 4 == np.arange(4)) & (p[:, None] % 32 < 8),
        "quad": (p[:, None] // 32 == np.arange(NQ)), "fk_row": (p[:, None] == CONST_ROW) * -MASKED,
        "ik_row": (p[:, None] == CONST_ROW) * MASKED, "b_rows": (p[:, None] == CONST_ROW + 1 + np.arange(3)),
        "iota": np.tile(np.arange(16), (128, 1)), "sel32": (p[:, None] % 32 == np.arange(32)),
        "pe": i["L0_attn_pe"][0, :S], "wq": i["L0_attn_wq"], "wk": i["L0_attn_wk"], "bq": col(i["L0_attn_bq"]),
        "bk": col(i["L0_attn_bk"]), "wv": i["L0_attn_wv"], "wo": i["L0_attn_wo"],
        "w_src": halves(w_src), "w_tgt": i["L0_xattn_W_tgt"].T, "w_out": halves(i["L0_xattn_W_out"].T),
        "b_srck": col(i["L0_xattn_b_src"][:128]), "b_tgt": col(i["L0_xattn_b_tgt"]),
        "b1": np.tile(i["L1_xattn_b"], (128, 1)),
        "router0": i["L0_ffn_router_w"],
        "wg0": np.concatenate([side(i["L0_ffn_wg_s"]), side(i["L0_ffn_wg_r"])], axis=1),
        "wu0": np.concatenate([side(i["L0_ffn_wu_s"]), side(i["L0_ffn_wu_r"])], axis=1),
        "wd0": np.transpose(down0.reshape(A_BLOCKS, 128, D), (1, 0, 2)).reshape(128, -1),
        "w_in": i["L1_attn_W_in"], "w_dtlow": xproj[:, :RANK], "w_bc": np.tile(xproj[:, RANK:], (1, 3)),
        "w_dt": w_dt, "w_mo": halves(w_mo), "b_dt": col(i["L1_attn_b_dt"]), "b_x": col(i["L1_attn_b_x"]),
        "b_z": col(i["L1_attn_b_z"]), "d_skip": col(i["L1_attn_D"]), "k_x": i["L1_attn_K_x"][:, 0],
        "k_z": i["L1_attn_K_z"][:, 0], "a_log": i["L1_attn_A_log"],
        "router1": i["L1_ffn_wg"].T, "w1": i["L1_ffn_w1"].reshape(-1, D).T, "w3": i["L1_ffn_w3"].reshape(-1, D).T,
        "w2": per_block(i["L1_ffn_w2"]), "fk_tok": i["mask_BxS2_fk1"].T,
        "bv": i["L0_attn_bv"], "bo": i["L0_attn_bo"], "gamma": i["L0_attn_gamma"], "beta": i["L0_attn_beta"],
        "b_srcv": i["L0_xattn_b_src"][128:], "b_out": i["L0_xattn_b_out"], "fk": i["mask_BxS2_fk1"].reshape(-1),
    }
    arrays = {f"pack_{name}": rows_of(np.concatenate([a[n] for n, _ in pack], axis=1))
              for name, pack in PACKS.items()}
    arrays["rows"] = rows_of(np.concatenate([a[n].reshape(1, -1) for n, _ in ROWS], axis=1))
    ik = i["mask_BxS2_ik0"]
    arrays["ik_row"] = np.ascontiguousarray(ik.reshape(1, -1))
    arrays["x"] = rows_of(i["x"])
    ctx = i["ctx_2048"]
    arrays["ctx_t"] = rows_of(np.transpose(ctx, (2, 0, 1)).reshape(2, 128, B * S))
    arrays["v_ctx"] = rows_of(ctx[:, :, 128:])
    return arrays


def kernel(**inputs):
    import concourse.bacc as bacc
    from concourse.bass_utils import run_bass_kernel_spmd

    arrays = lay_out({name: np.asarray(a) for name, a in inputs.items()})
    nc = bacc.Bacc("TRN2", target_bir_lowering=False, num_devices=1)
    d = {name: nc.dram_tensor(f"in_{name}", a.shape, mybir.dt.from_np(a.dtype), kind="ExternalInput").ap()
         for name, a in arrays.items()}
    out = nc.dram_tensor("out", (B, S, D), mybir.dt.float32, kind="ExternalOutput").ap()
    packed = [(name, d[f"pack_{name}"]) for name in PACKS]
    k_made, q_made = ([nc.dram_tensor(f"{n}_made{i}", (3, 16, 8, T), mybir.dt.bfloat16, kind="Internal").ap()
                       for i in range(3 * NG)] for n in "kq")
    decoder(nc, packed, d["rows"], d["ik_row"], d["x"], d["ctx_t"], d["v_ctx"], k_made, q_made, out)
    result = run_bass_kernel_spmd(nc, [{f"in_{name}": a for name, a in arrays.items()}], core_ids=[0])
    return result.results[0]["out"]
```
